# Optimizing a Trainium2 kernel written in Bass

```python
import numpy as np
import jax
import jax.numpy as jnp

def _softmax(x, axis=-1):
    return jax.nn.softmax(x, axis=axis)

def _gelu(x):
    return jax.nn.gelu(x, approximate=True)

def _silu(x):
    return jax.nn.silu(x)

def _sigmoid(x):
    return jax.nn.sigmoid(x)

def _layernorm(x, axis=-1, eps=1e-05):
    m = jnp.mean(x, axis=axis, keepdims=True)
    v = jnp.var(x, axis=axis, keepdims=True)
    return (x - m) / jnp.sqrt(v + eps)

def _scatter_add(tgt, idx, src, axis=0):
    return tgt.at[idx].add(src)

def _segment_sum(src, seg, n):
    return jax.ops.segment_sum(src, seg, n)
kernel_name = 'mk_seq_postln_d1_jaxref_r4_203509'

def setup_inputs(seed: int=0):
    np.random.seed(seed)
    _w = jnp.asarray

    def _L0_attn_setup():
        import jax, jax.numpy as jnp
        import numpy as np
        D_MODEL = 256
        N_HEADS = 16
        D_K = D_MODEL // N_HEADS
        MAX_LEN = 512
        B, T = (2, 512)
        key = jax.random.key(seed)
        ks = jax.random.split(key, 10)
        s = 1.0 / np.sqrt(D_MODEL)
        inp = {'x': jax.random.normal(ks[0], (B, T, D_MODEL), dtype=jnp.float32), 'WQ': jax.random.uniform(ks[1], (D_MODEL, D_MODEL), minval=-s, maxval=s, dtype=jnp.float32), 'bQ': jax.random.uniform(ks[2], (D_MODEL,), minval=-s, maxval=s, dtype=jnp.float32), 'WK': jax.random.uniform(ks[3], (D_MODEL, D_MODEL), minval=-s, maxval=s, dtype=jnp.float32), 'bK': jax.random.uniform(ks[4], (D_MODEL,), minval=-s, maxval=s, dtype=jnp.float32), 'WV': jax.random.uniform(ks[5], (D_MODEL, D_MODEL), minval=-s, maxval=s, dtype=jnp.float32), 'bV': jax.random.uniform(ks[6], (D_MODEL,), minval=-s, maxval=s, dtype=jnp.float32), 'WO': jax.random.uniform(ks[7], (D_MODEL, D_MODEL), minval=-s, maxval=s, dtype=jnp.float32), 'bO': jax.random.uniform(ks[8], (D_MODEL,), minval=-s, maxval=s, dtype=jnp.float32), 'rel_pos_table': jax.random.normal(ks[9], (2 * MAX_LEN - 1, N_HEADS), dtype=jnp.float32)}
        return inp
    _L0_attn_in = _L0_attn_setup()

    def _L0_ffn_setup():
        import jax, jax.numpy as jnp
        import numpy as np
        CAP_FACTOR = 1.5
        key = jax.random.key(seed)
        ks = jax.random.split(key, 6)
        E, S, D, M = (48, 4, 256, 256)
        K = D // S
        x = jax.random.normal(ks[0], (4, 1024, D), dtype=jnp.float32)
        Wr = jax.random.normal(ks[1], (E, D), dtype=jnp.float32) * 0.02
        W1 = jax.random.normal(ks[2], (E, S, D, M), dtype=jnp.float32) * (1.0 / np.sqrt(D))
        b1 = jnp.zeros((E, S, M), dtype=jnp.float32)
        W2 = jax.random.normal(ks[3], (E, S, M, K), dtype=jnp.float32) * (1.0 / np.sqrt(M))
        b2 = jnp.zeros((E, S, K), dtype=jnp.float32)
        return {'x': x, 'Wr': Wr, 'W1': W1, 'b1': b1, 'W2': W2, 'b2': b2}
    _L0_ffn_in = _L0_ffn_setup()
    _d = {'L0_attn_x': _L0_attn_in['x'], 'L0_attn_WQ': _L0_attn_in['WQ'], 'L0_attn_bQ': _L0_attn_in['bQ'], 'L0_attn_WK': _L0_attn_in['WK'], 'L0_attn_bK': _L0_attn_in['bK'], 'L0_attn_WV': _L0_attn_in['WV'], 'L0_attn_bV': _L0_attn_in['bV'], 'L0_attn_WO': _L0_attn_in['WO'], 'L0_attn_bO': _L0_attn_in['bO'], 'L0_attn_rel_pos_table': _L0_attn_in['rel_pos_table'], 'L0_ffn_Wr': _L0_ffn_in['Wr'], 'L0_ffn_W1': _L0_ffn_in['W1'], 'L0_ffn_b1': _L0_ffn_in['b1'], 'L0_ffn_W2': _L0_ffn_in['W2'], 'L0_ffn_b2': _L0_ffn_in['b2']}
    _x0 = _d['L0_attn_x']
    _d['L0_attn_x'] = jax.random.normal(jax.random.fold_in(jax.random.key(seed), 1), (2, 2048, 256), dtype=_x0.dtype)
    del _x0
    return _d

def reference(L0_attn_x, L0_attn_WQ, L0_attn_bQ, L0_attn_WK, L0_attn_bK, L0_attn_WV, L0_attn_bV, L0_attn_WO, L0_attn_bO, L0_attn_rel_pos_table, L0_ffn_Wr, L0_ffn_W1, L0_ffn_b1, L0_ffn_W2, L0_ffn_b2):

    def _L0_attn_ref(x, WQ, bQ, WK, bK, WV, bV, WO, bO, rel_pos_table):
        import jax, jax.numpy as jnp
        import numpy as np
        D_MODEL = 256
        N_HEADS = 16
        D_K = D_MODEL // N_HEADS
        MAX_LEN = 512
        B, T = (2, 512)
        b, t, d = x.shape
        q = (x @ WQ.T + bQ).reshape(b, t, N_HEADS, D_K).transpose(0, 2, 1, 3)
        k = (x @ WK.T + bK).reshape(b, t, N_HEADS, D_K).transpose(0, 2, 1, 3)
        v = (x @ WV.T + bV).reshape(b, t, N_HEADS, D_K).transpose(0, 2, 1, 3)
        scores = jnp.einsum('bhqd,bhkd->bhqk', q, k) / jnp.sqrt(jnp.float32(D_K))
        pos = jnp.arange(t)
        rel = pos[:, None] - pos[None, :] + (MAX_LEN - 1)
        rel = jnp.clip(rel, 0, 2 * MAX_LEN - 2)
        rel_bias = rel_pos_table[rel]
        scores = scores + rel_bias.transpose(2, 0, 1)[None]
        causal = pos[None, :] <= pos[:, None]
        scores = jnp.where(causal[None, None], scores, -jnp.inf)
        attn = jax.nn.softmax(scores, axis=-1)
        out = jnp.einsum('bhqk,bhkd->bhqd', attn, v)
        out = out.transpose(0, 2, 1, 3).reshape(b, t, d)
        return out @ WO.T + bO

    def _L0_ffn_ref(x, Wr, W1, b1, W2, b2):
        import jax, jax.numpy as jnp
        import numpy as np
        CAP_FACTOR = 1.5
        orig_shape = x.shape
        D = x.shape[-1]
        E = Wr.shape[0]
        xf = x.reshape(-1, D)
        T = xf.shape[0]
        cap = int(CAP_FACTOR * T / E)
        logits = xf @ Wr.T
        vals, idx = jax.lax.top_k(logits.T, cap)
        w = jax.nn.softmax(vals, axis=-1)
        xg = xf[idx]
        h = jax.nn.gelu(jnp.einsum('ecd,esdm->ecsm', xg, W1) + b1[:, None], approximate=False)
        y = jnp.einsum('ecsm,esmk->ecsk', h, W2) + b2[:, None]
        y = y.reshape(E, cap, D) * w[..., None]
        out = jnp.zeros_like(xf).at[idx.reshape(-1)].add(y.reshape(-1, D))
        return out.reshape(orig_shape)
    x = L0_attn_x
    x = _layernorm(x + _L0_attn_ref(x, L0_attn_WQ, L0_attn_bQ, L0_attn_WK, L0_attn_bK, L0_attn_WV, L0_attn_bV, L0_attn_WO, L0_attn_bO, L0_attn_rel_pos_table), axis=-1)
    x = _layernorm(x + _L0_ffn_ref(x, L0_ffn_Wr, L0_ffn_W1, L0_ffn_b1, L0_ffn_W2, L0_ffn_b2), axis=-1)
    return x

_drawn_inputs = setup_inputs


def setup_inputs(seed=0):
    import zlib

    import numpy as np

    out = dict(_drawn_inputs(seed))
    spreads = {'L0_ffn_b1': (0.0, 0.8), 'L0_ffn_b2': (0.0, 0.8)}
    factors = {'L0_attn_WQ': 4.843,
     'L0_attn_bQ': 8.0,
     'L0_attn_WK': 4.586,
     'L0_attn_bK': 8.0,
     'L0_attn_bV': 2.8,
     'L0_ffn_Wr': 2.89}
    for name, (base, spread) in spreads.items():
        noise = np.random.default_rng([zlib.crc32(name.encode()), seed]).standard_normal(out[name].shape)
        drawn = base * np.exp(spread * noise) if base else spread * noise
        out[name] = jnp.asarray(drawn.astype(out[name].dtype))
    for name, factor in factors.items():
        out[name] = (out[name] * factor).astype(out[name].dtype)
    return out
```

```python
import concourse.bass as bass
from concourse import mybir
from contextlib import ExitStack

F32 = mybir.dt.float32
BF16 = mybir.dt.bfloat16
F16 = mybir.dt.float16
U32 = mybir.dt.uint32
ALU = mybir.AluOpType
ACT = mybir.ActivationFunctionType
AX = mybir.AxisListType

P = 128
B, T, D = 2, 2048, 256
H, DK = 16, 16
NT = B * T
TILES = NT // P
DT = D // P
MAXLEN = 512
E, S, M = 48, 4, 256
KO = D // S
CAP = int(1.5 * NT / E)
EPS = 1e-5

HG = 4
GROUPS = B * H // HG
QB = 512
NQB = T // QB
KT = T // P
SPLIT_Q = (0, 0, 0, 1, 1, 2)
SPLIT_K = (0, 1, 2, 0, 1, 0)
C = len(SPLIT_Q)
ROWS = C * DK
MROWS = 3
BAND = 5 * P
MASKED = -60000.0
NEG = -1.0e30
WLEN = 1152
HALF = NT // 2
NBUF = 4
QFREE, VFREE = 4, 4
SCORE_STEPS = [0, 4, 12, 24]
GROUP_STEPS = 40


def wait(eng, sem, count):
    if isinstance(count, int) and count <= 0:
        return
    eng.wait_ge(sem, count)


def hold(eng, sem, count, passed):
    if isinstance(count, int) and count <= 0:
        return
    eng.wait_ge(sem, count)
    if not isinstance(count, int):
        eng.sem_inc(passed, 1)


def moe_layer(nc, x, WQ, bQ, WK, bK, WV, bV, WO, bO, table, Wr, W1, b1, W2, b2, out):
    ctx = ExitStack()
    with ctx:
        def sb_in(stack):
            return lambda name, shape, dt: stack.enter_context(nc.sbuf_tensor(name, shape, dt))

        def sem(name):
            return ctx.enter_context(nc.semaphore(name))

        def dram(name, shape, dt):
            return nc.dram_tensor(name, shape, dt, kind="Internal").ap()

        sb = sb_in(ctx)

        q_dram = dram("q_split", [B * H, DK, C, T], BF16)
        k_dram = dram("k_split", [B * H, DK, C, T], BF16)
        v_dram = dram("v_groups", [GROUPS, P, KT * HG * 32], F32)
        m_dram = dram("row_max", [GROUPS * NQB, MROWS * HG * 4, P], BF16)
        bias_dram = dram("bias_parts", [H, 2, 768], F16)
        biasr_dram = dram("bias_reversed", [H, WLEN], F32)
        biask_dram = dram("bias_by_key", [H, 2, P, BAND], F16)
        biasq_dram = dram("bias_by_query", [H, P, 1024], F32)
        att_dram = dram("attended", [GROUPS, T, HG * DK], F32)
        x1_dram = dram("normed", [NT, D], F32)
        acc_dram = dram("summed", [NT, D], F32)

        ps = ctx.enter_context(nc.psum_tensor("banks", [P, 8, 512], F32))

        ident = sb("ident", [P, P], F32)
        identb = sb("identb", [P, P], BF16)
        identh = sb("identh", [P, P], F16)
        ones_row = sb("ones_row", [1, P], F32)
        WOT = sb("WOT", [P, DT, D], F32)
        WrT = sb("WrT", [P, DT, E], F32)
        bO_b = sb("bO_b", [P, D], F32)
        b1T = sb("b1T", [P, E * S * 2], F32)
        w1_sb = sb("w1_sb", [P, NBUF, S, DT, M], F32)
        w2_sb = sb("w2_sb", [P, NBUF, S, 2 * KO], F32)
        b2_sb = sb("b2_sb", [1, NBUF, D], F32)

        names = """loaded_w loaded_b1 zeroed consts turned turned_copied ln_aggr fin_aggr dve_passed pool_passed pe_passed bias_step bias_stored
            x_loaded0 x_loaded1 xT_ready xT_copied qk_ready q32_done s1_done rest_done s2_done s3_done split_stored0
            split_stored1 v_ready v_copied v_stored0 v_stored1 pads
            biasq_loaded0 biasq_loaded1 group_loaded0 group_loaded1 mrow_stored
            s_ready exp_done max_ready max_done negmax_done msplit m_turned m_copied
            pv_done o_copied o_turned recip_done att_done att_stored0 att_stored1
            at_loaded0 at_loaded1 xr_loaded0 xr_loaded1 at_turned at_copied y_ready ln_step std_done x1_done
            x1_stored0 x1_stored1 x1_turned x1_copied lg_ready lg_copied xb_done
            top_step top_moved top_conv top_turned top_sel allmax wexp
            w_loaded0 w_loaded1 w_loaded2 w_loaded3 idx_copied gathered0 gathered1 gathered2 gathered3 small_copied
            xg_turned xg_copied h_ready gelu_done y2_ready y2_scaled scattered
            acc_loaded0 acc_loaded1 fin_step fin_std fin_done fin_stored0 fin_stored1""".split()
        s = {n: sem(n) for n in names}

        loaded_w, zeroed, consts = s["loaded_w"], s["zeroed"], s["consts"]
        turned, turned_copied = s["turned"], s["turned_copied"]
        x_loaded = [s["x_loaded0"], s["x_loaded1"]]
        split_stored = [s["split_stored0"], s["split_stored1"]]
        v_stored = [s["v_stored0"], s["v_stored1"]]
        qk_loaded = [[sem(f"qk_loaded{p}{c}") for c in range(4)] for p in range(2)]
        mrow_loaded = [sem(f"mrow_loaded{qb}") for qb in range(NQB)]
        biasq_loaded = [s["biasq_loaded0"], s["biasq_loaded1"]]
        group_loaded = [s["group_loaded0"], s["group_loaded1"]]
        att_stored = [s["att_stored0"], s["att_stored1"]]
        at_loaded = [s["at_loaded0"], s["at_loaded1"]]
        xr_loaded = [s["xr_loaded0"], s["xr_loaded1"]]
        x1_stored = [s["x1_stored0"], s["x1_stored1"]]
        w_loaded = [s[f"w_loaded{n}"] for n in range(NBUF)]
        gathered = [s[f"gathered{n}"] for n in range(NBUF)]
        acc_loaded = [s["acc_loaded0"], s["acc_loaded1"]]
        fin_stored = [s["fin_stored0"], s["fin_stored1"]]

        with ExitStack() as st:
            sp_ = sb_in(st)
            w_nat = sp_("w_nat", [P, 4, DT, D], F32)
            wr_nat = sp_("wr_nat", [E, D], F32)
            b1_nat = sp_("b1_nat", [96, 2, M], F32)
            tab_nat = sp_("tab_nat", [P, 4, H], F32)
            WT = sp_("WT", [P, 3, DT, D], F32)
            bqk = sp_("bqk", [P, 4], F32)
            bV_b = sp_("bV_b", [P, D], F32)
            tabT = sp_("tabT", [H, MAXLEN], F32)
            far = sp_("far", [H, 1], F32)
            wide = sp_("wide", [H, WLEN], F32)
            wide_r = sp_("wide_r", [H, WLEN], F32)
            wide_h = sp_("wide_h", [H, 2, 768], F16)
            x_sb = sp_("x_sb", [P, 2, 4, D], F32)
            xT = sp_("xT", [P, 2, DT, QB], F32)
            q32 = sp_("q32", [P, 2, QB], F32)
            rest = sp_("rest", [P, 2, QB], F32)
            parts = sp_("parts", [P, 2, 3, QB], BF16)
            v_st = sp_("v_st", [P, 2, 4, 4, HG, 32], F32)

        with ExitStack() as st:
            sa = sb_in(st)
            Qs = sa("Qs", [P, 2, HG, T], BF16)
            Ks = sa("Ks", [P, 2, HG, T], BF16)
            Vs = sa("Vs", [P, 2, KT, HG, 32], F32)
            bk_sb = sa("bk_sb", [P, 2, HG, 2, BAND], F16)
            bq_sb = sa("bq_sb", [P, 2, HG, 1024], F32)
            probs = sa("probs", [P, 2, 2, 2, QB], F32)
            dump = sa("dump", [P, 2, QB], F32)
            mpart = sa("mpart", [P, 2, HG, 4, 4], F32)
            negm = sa("negm", [P, HG * 4], F32)
            negm_rest = sa("negm_rest", [P, HG * 4], F32)
            m_parts = sa("m_parts", [P, MROWS, HG * 4], BF16)
            m_rows = sa("m_rows", [MROWS * HG * 4, P], BF16)
            o_sb = sa("o_sb", [P, QB], F32)
            recip = sa("recip", [P, 16], F32)
            att = sa("att", [P, 2, 4, HG * DK], F32)

        st = ctx.enter_context(ExitStack())
        sc = sb_in(st)
        at_in = sc("at_in", [P, 2, 4, HG * DK], F32)
        xr = sc("xr", [P, 2, D], F32)
        xb = sc("xb", [P, 2, D], F32)
        atT = sc("atT", [P, 2, DT, P], F32)
        res = sc("res", [P, 2, D], F32)
        x1 = sc("x1", [P, 2, D], F32)
        x1T = sc("x1T", [P, 2, DT, P], F32)
        stats = sc("stats", [P, 2, 6], F32)
        mv = sc("mv", [P, 2, 2], F32)
        std = sc("std", [P, 2, 2], F32)
        logits = sc("logits", [P, HALF], F32)
        top_v = sc("top_v", [P, P], F32)
        top_i = sc("top_i", [P, P], U32)
        top_f = sc("top_f", [P, P], F32)
        up_v = sc("up_v", [E, 2, P], F32)
        rev = sc("rev", [E, 2, P], F32)
        tr = sc("tr", [P, 4, E], F32)
        pick_m = sc("pick_m", [P, E], F32)
        pick_v = sc("pick_v", [P, E], F32)
        pick_d = sc("pick_d", [P, E], F32)
        pick_i = sc("pick_i", [P, E], F32)
        idx = sc("idx", [P, E], U32)
        allred = sc("allred", [P, 2, E], F32)
        pexp = sc("pexp", [P, E], F32)
        gate = sc("gate", [P, E], F32)
        idx_c = sc("idx_c", [P, NBUF, 1], U32)
        xg = sc("xg", [P, NBUF, D], F32)
        xgT = sc("xgT", [P, 2, DT, P], F32)
        hid = sc("hid", [P, 2, 2 * S, P], F32)
        b1_c = sc("b1_c", [P, NBUF, 2 * S], F32)
        gate_c = sc("gate_c", [P, NBUF, 1], F32)
        y_sb = sc("y_sb", [P, 2, D], F32)
        fin_in = sc("fin_in", [P, 2, D], F32)
        fin_out = sc("fin_out", [P, 2, D], F32)
        fstats = sc("fstats", [P, 2, 6], F32)
        fmv = sc("fmv", [P, 2, 2], F32)
        fstd = sc("fstd", [P, 2, 2], F32)

        block = ctx.enter_context(nc.Block())

        def expert_load(sp, e, n):
            sp.dma_start(w1_sb[:, n, :, :, :].rearrange("p s t m -> p (s t) m"),
                         W1[bass.ds(e, 1)].rearrange("e s (t p) m -> p (e s t) m", p=P)).then_inc(w_loaded[n], 16)
            sp.dma_start(w2_sb[:, n, :, :],
                         W2[bass.ds(e, 1)].rearrange("e s (p j) k -> p (e s) (j k)", p=P)).then_inc(w_loaded[n], 16)
            sp.dma_start(b2_sb[:, n, :],
                         b2[bass.ds(e, 1)].rearrange("e s k -> e (s k)")).then_inc(w_loaded[n], 16)

        @block.sync
        def _(sp):
            for n, w in enumerate((WQ, WK, WV, WO)):
                sp.dma_start(w_nat[:, n, :, :], w.rearrange("(t p) i -> p t i", p=P)).then_inc(loaded_w, 16)
            sp.dma_start(wr_nat[:, :], Wr).then_inc(loaded_w, 16)
            sp.dma_start(tab_nat[:, :, :],
                         table[MAXLEN - 1:2 * MAXLEN - 1, :].rearrange("(r p) h -> p r h", p=P)).then_inc(loaded_w, 16)
            sp.dma_start(b1_nat[:, :, :], b1.rearrange("e s m -> (e s) m").rearrange("(r p) m -> p r m", p=96)
                         ).then_inc(s["loaded_b1"], 16)
            with nc.allow_non_contiguous_dma(reason="two small bias vectors, one element to a partition"):
                for n, b in enumerate((bQ, bK)):
                    sp.dma_start(bqk[:, 2 * n:2 * n + 2], b.rearrange("(t p) -> p t", p=P)).then_inc(loaded_w, 16)
            for dst, b in ((bV_b, bV), (bO_b, bO)):
                sp.dma_start(dst[:, :], b.rearrange("(a n) -> a n", a=1).to_broadcast([P, D])).then_inc(loaded_w, 16)

            def load_x(n, u):
                sp.dma_start(x_sb[:, u], x.rearrange("b t d -> (b t) d")[bass.ds(n * QB, QB), :].rearrange(
                    "(a p) d -> p a d", p=P)).then_inc(x_loaded[u], 16)

            load_x(0, 0)
            load_x(1, 1)
            sp.wait_ge(s["bias_step"], 9)
            sp.dma_start(bias_dram[:, :, :], wide_h[:, :, :]).then_inc(s["bias_stored"], 16)
            sp.dma_start(biasr_dram[:, :], wide_r[:, :]).then_inc(s["bias_stored"], 16)
            sp.wait_ge(s["bias_stored"], 32)
            for part in range(2):
                sp.dma_start(biask_dram[:, part], bass.AP(
                    bias_dram.tensor, part * 768 + P, [[2 * 768, H], [-1, P], [1, BAND]])
                    ).then_inc(s["bias_stored"], 16)
            sp.dma_start(biasq_dram[:, :, :], bass.AP(
                biasr_dram.tensor, P - 1, [[WLEN, H], [-1, P], [1, 1024]])).then_inc(s["bias_stored"], 16)
            def store_pair(i, b, load_more):
                for u in range(2):
                    n = 2 * i + u + 4 * b
                    t0 = (2 * i + u) * QB
                    for j in range(4):
                        sp.wait_ge(s["s3_done"], 4 * n + j + 1)
                        dst = (q_dram, k_dram)[j // 2]
                        dst = dst[b * H + 8 * (j % 2):b * H + 8 * (j % 2) + 8, :, :, bass.ds(t0, QB)].rearrange(
                            "h d c t -> (h d) c t")
                        src = parts[:, j % 2]
                        if j // 2 == 0:
                            runs = ((0, 3, src[:, 0:1].to_broadcast([P, 3, QB])),
                                    (3, 5, src[:, 1:2].to_broadcast([P, 2, QB])), (5, 6, src[:, 2:3]))
                        else:
                            runs = ((0, 3, src[:, 0:3]), (3, 5, src[:, 0:2]), (5, 6, src[:, 0:1]))
                        for c0, c1, part in runs:
                            sp.dma_start(dst[:, c0:c1, :], part).then_inc(split_stored[j % 2], 16)
                    sp.wait_ge(s["v_copied"], VFREE + 4 * n + 4)
                    sp.dma_start(
                        v_dram[b * 4:b * 4 + 4, :, bass.ds((2 * i + u) * 4 * HG * 32, 4 * HG * 32)].rearrange(
                            "g p n -> p g n"),
                        v_st[:, u].rearrange("p g t h e -> p g (t h e)")).then_inc(v_stored[u], 16)
                    if load_more:
                        sp.wait_ge(s["xT_ready"], 2 * n + 2)
                        load_x(n + 2, u)

            with sp.Fori(0, 2) as i:
                store_pair(i, 0, True)
            store_pair(0, 1, True)
            store_pair(1, 1, False)
            for u in range(2):
                sp.wait_ge(split_stored[u], 48 + 48 * 2 * 8)
                sp.wait_ge(v_stored[u], 16 + 16 * 4)
            sp.wait_ge(s["bias_stored"], 80)

            def load_chunk(hg, p, c):
                for dst, src in ((Qs, q_dram), (Ks, k_dram)):
                    sp.dma_start(dst[0:ROWS, p, :, c * QB:(c + 1) * QB],
                                 src[bass.ds(p * H + hg * HG, HG), :, :, c * QB:(c + 1) * QB].rearrange(
                                     "h d c t -> (d c) h t")).then_inc(qk_loaded[p][c], 16)

            def load_bias_q(hg, p):
                sp.dma_start(bq_sb[:, p, :, :], biasq_dram[bass.ds(hg * HG, HG)].rearrange("h p c -> p h c")
                             ).then_inc(biasq_loaded[p], 16)

            def load_group(hg, p):
                sp.dma_start(bk_sb[:, p].rearrange("p h s c -> p (h s) c"),
                             biask_dram[bass.ds(hg * HG, HG)].rearrange("h s p c -> p (h s) c")
                             ).then_inc(group_loaded[p], 16)
                sp.dma_start(Vs[:, p].rearrange("p t h e -> p (t h e)"),
                             v_dram[bass.ds(p * 4 + hg, 1)].rearrange("g p n -> p (g n)")).then_inc(group_loaded[p], 16)

            def max_rows(g, p, qb):
                unit = NQB * g + qb
                sp.wait_ge(s["m_copied"], unit + 1)
                sp.dma_start(m_dram[bass.ds(unit, 1)].rearrange("u r t -> (u r) t"),
                             m_rows[:, :]).then_inc(s["mrow_stored"], 16)
                sp.wait_ge(s["mrow_stored"], 16 * unit + 16)
                sp.dma_start(Qs[ROWS:ROWS + MROWS, p, :, qb * QB:(qb + 1) * QB],
                             m_dram[bass.ds(unit, 1)].rearrange("u (s h i) t -> (u s) h (i t)", s=MROWS, h=HG)
                             ).then_inc(mrow_loaded[qb], 16)

            def store_att(g, hg, p, qb):
                sp.wait_ge(s["att_done"], NQB * g + qb + 1)
                sp.dma_start(
                    att_dram[bass.ds(p * 4 + hg, 1), qb * QB:(qb + 1) * QB, :].rearrange(
                        "g (i p) n -> p (g i) n", p=P), att[:, qb % 2]).then_inc(att_stored[qb % 2], 16)

            def first_maxima():
                for qb in range(NQB - 1):
                    max_rows(0, 0, qb)

            def phase(g, hg, p):
                static = isinstance(g, int)
                has_before, has_next, has_two_on = not (static and g == 0), not (static and g == GROUPS - 1), \
                    not (static and g >= GROUPS - 2)
                next_hg = hg + p
                for qb in range(NQB):
                    if qb == 0:
                        max_rows(g, p, NQB - 1)
                        if has_before:
                            store_att(g - 1, hg - 1 + p, 1 - p, NQB - 1)
                            if has_next:
                                sp.wait_ge(s["pv_done"], GROUP_STEPS * g)
                                load_group(next_hg, 1 - p)
                    else:
                        if has_next:
                            max_rows(g + 1, 1 - p, qb - 1)
                        store_att(g, hg, p, qb - 1)
                if has_two_on:
                    sp.wait_ge(s["negmax_done"], NQB * g + NQB)
                    load_bias_q(hg + 1, p)
                    for c in range(4):
                        sp.wait_ge(s["s_ready"], 2 * (GROUP_STEPS * g + SCORE_STEPS[3] + 4 * c + 4))
                        load_chunk(hg + 1, p, c)

            sp.wait_ge(s["pads"], 1)
            for p in range(2):
                for c in range(4):
                    load_chunk(0, p, c)
                    if c == 0:
                        load_bias_q(0, p)
                load_group(0, p)
            for n in range(NBUF):
                expert_load(sp, n, n)
            first_maxima()
            phase(0, 0, 0)
            with sp.Fori(0, 2) as i:
                phase(1 + 2 * i, i, 1)
                phase(2 + 2 * i, i + 1, 0)
            phase(5, 2, 1)
            phase(6, 3, 0)
            phase(7, 3, 1)
            store_att(7, 3, 1, 3)

            for u in range(2):
                sp.wait_ge(att_stored[u], 16 * 16)

            def load_token_tile(i, u):
                sp.dma_start(at_in[:, u], att_dram[u * 4:u * 4 + 4, bass.ds(i * P, P), :].rearrange(
                    "g p n -> p g n")).then_inc(at_loaded[u], 16)
                sp.dma_start(xr[:, u], x[u, bass.ds(i * P, P), :]).then_inc(xr_loaded[u], 16)

            for u in range(2):
                load_token_tile(0, u)

            def store_x1(i, u):
                sp.wait_ge(s["x1_done"], 2 * i + u + 1)
                for dst in (x1_dram, acc_dram):
                    sp.dma_start(dst[bass.ds(i * P + u * T, P), :], x1[:, u]).then_inc(x1_stored[u], 16)

            with sp.Fori(0, 15) as i:
                for u in range(2):
                    sp.wait_ge(s["at_turned"], 2 * i + u + 1)
                    sp.wait_ge(s["xb_done"], 2 * i + u + 1)
                    load_token_tile(i + 1, u)
                for u in range(2):
                    store_x1(i, u)
            for u in range(2):
                store_x1(15, u)

            sp.wait_ge(s["top_conv"], 1)
            sp.dma_start(up_v[:, 0, :], top_v[64:64 + E, :]).then_inc(s["top_moved"], 16)
            sp.dma_start(up_v[:, 1, :], top_f[64:64 + E, :]).then_inc(s["top_moved"], 16)

            with sp.Fori(0, E // NBUF - 1) as i:
                for n in range(NBUF):
                    sp.wait_ge(s["y2_ready"], NBUF * i + n + 1)
                    expert_load(sp, NBUF * i + NBUF + n, n)

            def load_sum(i, u):
                sp.dma_start(fin_in[:, u], acc_dram[bass.ds((2 * i + u) * P, P), :]).then_inc(acc_loaded[u], 16)

            out_flat = out.rearrange("b t d -> (b t) d")
            sp.wait_ge(s["scattered"], 16 * E)
            for u in range(2):
                load_sum(0, u)
            with sp.Fori(0, 15) as i:
                for u in range(2):
                    sp.wait_ge(s["fin_done"], 2 * i + u + 1)
                    sp.dma_start(out_flat[bass.ds((2 * i + u) * P, P), :], fin_out[:, u]).then_inc(fin_stored[u], 16)
                    load_sum(i + 1, u)
            for u in range(2):
                sp.wait_ge(s["fin_done"], 30 + u + 1)
                sp.dma_start(out_flat[(30 + u) * P:(31 + u) * P, :], fin_out[:, u]).then_inc(fin_stored[u], 16)
            for u in range(2):
                sp.wait_ge(fin_stored[u], 16 * 16)

        @block.gpsimd
        def _(pool):
            nc.gpsimd.memset(ident[:, :], 0.0).then_inc(zeroed, 1)
            nc.gpsimd.memset(ones_row[:, :], 1.0).then_inc(consts, 1)
            pool.wait_ge(zeroed, 1)
            nc.gpsimd.affine_select(out=ident[:, :], in_=ident[:, :], compare_op=ALU.not_equal, fill=1.0,
                                    base=0, pattern=[[-1, P]], channel_multiplier=1).then_inc(zeroed, 1)
            pool.wait_ge(zeroed, 2)
            nc.gpsimd.tensor_copy(identb[:, :], ident[:, :]).then_inc(consts, 1)
            nc.gpsimd.tensor_copy(identh[:, :], ident[:, :]).then_inc(consts, 1)
            nc.gpsimd.memset(v_st[:, :].rearrange("p u g t h e -> p (u g t h e)"), 0.0).then_inc(zeroed, 1)
            pool.wait_ge(zeroed, 3)
            nc.gpsimd.memset(v_st[:, :].rearrange("p u g t h e -> p (u g t h) e")[:, :, DK:DK + 1], 1.0
                             ).then_inc(consts, 1)

            for b in range(B):
                with pool.Fori(0, 2) as i:
                    for u in range(2):
                        for j in range(4):
                            t = 4 * (2 * i + u + 4 * b) + j
                            pool.wait_ge(s["s2_done"], t + 1)
                            nc.gpsimd.tensor_tensor(parts[:, j % 2, 2], rest[:, j % 2], parts[:, j % 2, 1],
                                                    ALU.subtract).then_inc(s["s3_done"], 1)

            def split_max(unit):
                step = 4 * unit
                wait(pool, s["m_turned"], unit)
                hold(pool, s["negmax_done"], unit + 1, s["pool_passed"])
                nc.gpsimd.tensor_copy(m_parts[:, 0], negm[:, :]).then_inc(s["msplit"], 1)
                pool.wait_ge(s["msplit"], step + 1)
                nc.gpsimd.tensor_tensor(negm_rest[:, :], negm[:, :], m_parts[:, 0], ALU.subtract
                                        ).then_inc(s["msplit"], 1)
                hold(pool, s["msplit"], step + 2, s["pool_passed"])
                nc.gpsimd.tensor_copy(m_parts[:, 1], negm_rest[:, :]).then_inc(s["msplit"], 1)
                pool.wait_ge(s["msplit"], step + 3)
                nc.gpsimd.tensor_tensor(m_parts[:, 2], negm_rest[:, :], m_parts[:, 1], ALU.subtract
                                        ).then_inc(s["msplit"], 1)

            pool.wait_ge(s["s3_done"], 32)
            for u in range(2):
                pool.wait_ge(split_stored[u], 48 + 48 * 2 * 8)
                pool.wait_ge(v_stored[u], 16 + 16 * 4)
            pool.wait_ge(s["bias_stored"], 80)
            nc.gpsimd.memset(Ks[ROWS:P, :, :, :].rearrange("p a h t -> p (a h t)"), 1.0).then_inc(s["pads"], 1)
            for unit in range(NQB):
                split_max(unit)
            with pool.Fori(NQB, NQB * GROUPS) as unit:
                split_max(unit)

            def add_output_bias(i):
                for u in range(2):
                    wait(pool, s["ln_step"], 8 * (i - 1) + 4 * u + 1)
                    pool.wait_ge(xr_loaded[u], 16 * i + 16)
                    nc.gpsimd.tensor_tensor(xb[:, u], xr[:, u], bO_b[:, :], ALU.add).then_inc(s["xb_done"], 1)

            add_output_bias(0)
            with pool.Fori(1, 16) as i:
                add_output_bias(i)

            pool.wait_ge(s["top_sel"], 2)
            nc.gpsimd.partition_all_reduce(allred[:, 0], pick_v[:, :], P, bass.bass_isa.ReduceOp.max).then_inc(s["allmax"], 1)
            pool.wait_ge(s["wexp"], 2)
            nc.gpsimd.partition_all_reduce(allred[:, 1], pexp[:, :], P, bass.bass_isa.ReduceOp.add).then_inc(s["allmax"], 1)

            def gather(e, n):
                nc.gpsimd.tensor_copy(idx_c[:, n, :], idx[:, bass.ds(e, 1)]).then_inc(s["idx_copied"], 1)
                hold(pool, s["idx_copied"], e + 1, s["pool_passed"])
                nc.gpsimd.indirect_dma_start(
                    out=xg[:, n], out_offset=None, in_=x1_dram,
                    in_offset=bass.IndirectOffsetOnAxis(ap=idx_c[:, n, :], axis=0)).then_inc(gathered[n], 16)

            def scatter(e, n):
                hold(pool, s["y2_scaled"], e + 1, s["pool_passed"])
                nc.gpsimd.indirect_dma_start(
                    out=acc_dram, out_offset=bass.IndirectOffsetOnAxis(ap=idx_c[:, n, :], axis=0),
                    in_=y_sb[:, n % 2], in_offset=None, compute_op=ALU.add).then_inc(s["scattered"], 16)
                hold(pool, s["scattered"], 16 * e + 16, s["pool_passed"])

            pool.wait_ge(s["top_sel"], 4)
            for u in range(2):
                pool.wait_ge(x1_stored[u], 32 * 16)
            for n in range(NBUF):
                gather(n, n)
            with pool.Fori(0, E // NBUF - 1) as i:
                for n in range(NBUF):
                    scatter(NBUF * i + n, n)
                    gather(NBUF * i + NBUF + n, n)
            for n in range(NBUF):
                scatter(E - NBUF + n, n)

        @block.scalar
        def _(act):
            for slot in range(2):
                act.sem_inc(split_stored[slot], 48)
            for b in range(B):
                with act.Fori(0, 2) as i:
                    for u in range(2):
                        n = 2 * i + u + 4 * b
                        for it in range(DT):
                            act.wait_ge(s["xT_ready"], 2 * n + it + 1)
                            nc.scalar.copy(xT[:, u, it], ps[:, it, :]).then_inc(s["xT_copied"], 1)
                        for j in range(4):
                            t = 4 * n + j
                            act.wait_ge(s["q32_done"], QFREE + t + 1)
                            act.wait_ge(split_stored[j % 2], 48 + 48 * (2 * n + j // 2))
                            nc.scalar.copy(parts[:, j % 2, 0], q32[:, j % 2]).then_inc(s["s1_done"], 1)
                            act.wait_ge(s["rest_done"], t + 1)
                            nc.scalar.copy(parts[:, j % 2, 1], rest[:, j % 2]).then_inc(s["s2_done"], 1)

            def exps(g, qb):
                for kt in range(4 * (qb + 1)):
                    step = GROUP_STEPS * g + SCORE_STEPS[qb] + kt
                    q0 = max(0, kt - 4 * qb) * P
                    for half in range(2):
                        act.wait_ge(s["s_ready"], 2 * step + half + 1)
                        if half == 0:
                            wait(act, s["pv_done"], step - 1)
                        nc.scalar.activation(probs[:, kt % 2, half, :, q0:QB],
                                             ps[:, 2 * half:2 * half + 2, q0:QB], ACT.Exp).then_inc(s["exp_done"], 1)

            def group(g):
                for qb in range(NQB):
                    exps(g, qb)

            group(0)
            with act.Fori(0, 3) as i:
                group(1 + 2 * i)
                group(2 + 2 * i)
            group(7)

            def turn_attended(i):
                for u in range(2):
                    act.wait_ge(s["at_turned"], 2 * i + u + 1)
                    nc.scalar.copy(atT[:, u], ps[:, u, 0:2 * P]).then_inc(s["at_copied"], 1)

            def turn_x1(i):
                for u in range(2):
                    act.wait_ge(s["x1_turned"], 2 * i + u + 1)
                    nc.scalar.copy(x1T[:, u], ps[:, 4 + u, 0:2 * P]).then_inc(s["x1_copied"], 1)

            def root(i):
                for u in range(2):
                    act.wait_ge(s["ln_step"], 8 * i + 4 * u + 3)
                    nc.scalar.activation(std[:, u, 0:1], std[:, u, 1:2], ACT.Sqrt).then_inc(s["std_done"], 1)

            def keep_logits(i):
                for u in range(2):
                    act.wait_ge(s["lg_ready"], 2 * i + u + 1)
                    nc.scalar.copy(logits[64 * u:64 * u + E, bass.ds(i * P, P)],
                                   ps[64 * u:64 * u + E, 6 + u, 0:P]).then_inc(s["lg_copied"], 1)

            turn_attended(0)
            root(0)
            with act.Fori(1, 16) as i:
                turn_attended(i)
                turn_x1(i - 1)
                root(i)
                keep_logits(i - 1)
            turn_x1(15)
            keep_logits(15)

            act.wait_ge(s["wexp"], 1)
            nc.scalar.activation(pexp[:, :], pick_d[:, :], ACT.Exp).then_inc(s["wexp"], 1)

            def gelus(e, n):
                for j in range(2 * S):
                    if j % 4 == 0:
                        act.wait_ge(s["h_ready"], 2 * e + j // 4 + 1)
                    if j == 0:
                        act.wait_ge(s["small_copied"], e + 1)
                    nc.scalar.activation(hid[:, n % 2, j, :], ps[:, 2 + 2 * (n % 2) + j // 4, (j % 4) * P:(j % 4 + 1) * P],
                                         ACT.Gelu, bias=b1_c[:, n, j:j + 1]).then_inc(s["gelu_done"], 1)

            with act.Fori(0, E // NBUF) as i:
                for n in range(NBUF):
                    gelus(NBUF * i + n, n)

            with act.Fori(0, 16) as i:
                for u in range(2):
                    act.wait_ge(s["fin_step"], 8 * i + 4 * u + 3)
                    nc.scalar.activation(fstd[:, u, 0:1], fstd[:, u, 1:2], ACT.Sqrt).then_inc(s["fin_std"], 1)

        @block.vector
        def _(dve):
            V = nc.vector
            for n in range(4):
                dve.wait_ge(turned, n + 1)
                dst = WT[:, n] if n < 3 else WOT
                V.tensor_copy(dst[:, :, :].rearrange("p t o -> p (t o)"), ps[:, n, :]).then_inc(turned_copied, 1)
            dve.wait_ge(turned, 5)
            V.tensor_copy(WrT[:, :, :].rearrange("p t e -> p (t e)"), ps[:, 4, 0:DT * E]).then_inc(turned_copied, 1)
            dve.wait_ge(turned, 6)
            V.tensor_copy(b1T[:, :].rearrange("p (n j) -> p j n", j=2),
                          ps[:, 5, 0:E * S * 2].rearrange("p (j n) -> p j n", j=2)).then_inc(turned_copied, 1)
            dve.wait_ge(turned, 7)
            V.tensor_copy(tabT[:, :], ps[0:H, 6, :]).then_inc(s["bias_step"], 1)
            V.memset(wide[:, :], 0.0).then_inc(s["bias_step"], 1)
            dve.wait_ge(s["bias_step"], 2)
            V.tensor_scalar(wide[:, P:P + MAXLEN], tabT[:, :], tabT[:, MAXLEN - 1:MAXLEN], None, ALU.subtract
                            ).then_inc(s["bias_step"], 1)
            dve.wait_ge(s["bias_step"], 3)
            V.tensor_copy(wide_h[:, 0, :], wide[:, 0:768]).then_inc(s["bias_step"], 1)
            dve.wait_ge(s["bias_step"], 4)
            V.tensor_tensor(wide_h[:, 1, :], wide[:, 0:768], wide_h[:, 0, :], ALU.subtract).then_inc(s["bias_step"], 1)
            dve.wait_ge(s["bias_step"], 5)
            V.memset(wide[:, 0:P], NEG).then_inc(s["bias_step"], 1)
            V.memset(wide_h[:, 0, 0:P], MASKED).then_inc(s["bias_step"], 1)
            V.memset(wide_h[:, 1, 0:P], 0.0).then_inc(s["bias_step"], 1)
            dve.wait_ge(s["bias_step"], 8)
            V.tensor_copy(wide_r[:, :], wide[:, ::-1]).then_inc(s["bias_step"], 1)

            dve.wait_ge(loaded_w, 16 * 10)
            dve.wait_ge(consts, 4)
            dve.sem_inc(s["q32_done"], QFREE)
            dve.sem_inc(s["v_copied"], VFREE)
            for u in range(2):
                dve.sem_inc(v_stored[u], 16)
            for b in range(B):
                with dve.Fori(0, 2) as i:
                    for u in range(2):
                        n = 2 * i + u + 4 * b
                        for j in range(4):
                            t = 4 * n + j
                            slot = j % 2
                            dve.wait_ge(s["qk_ready"], t + 1)
                            if j // 2 == 0:
                                V.tensor_scalar(q32[:, slot], ps[:, 2 + j, :], bqk[:, j:j + 1], DK ** -0.5,
                                                ALU.add, ALU.mult).then_inc(s["q32_done"], 1)
                            else:
                                V.tensor_scalar(q32[:, slot], ps[:, 2 + j, :], bqk[:, j:j + 1], None,
                                                ALU.add).then_inc(s["q32_done"], 1)
                            dve.wait_ge(s["s1_done"], t + 1)
                            V.tensor_tensor(rest[:, slot], q32[:, slot], parts[:, slot, 0], ALU.subtract
                                            ).then_inc(s["rest_done"], 1)
                        for tt in range(4):
                            if tt % 2 == 0:
                                dve.wait_ge(s["v_ready"], 2 * n + tt // 2 + 1)
                            if tt == 0:
                                dve.wait_ge(v_stored[u], 16 + 16 * (i + 2 * b))
                            V.tensor_tensor(v_st[:, u, :, tt, :, 0:DK],
                                            ps[:, 6 + tt // 2, (tt % 2) * D:(tt % 2 + 1) * D].rearrange(
                                                "p (g h d) -> p g h d", g=4, h=HG),
                                            bV_b[:, :].rearrange("p (g h d) -> p g h d", g=4, h=HG),
                                            ALU.add).then_inc(s["v_copied"], 1)

            def maxima(g, p, qb, kt):
                i_, c = divmod(kt, qb + 1)
                i = 4 * qb + i_
                lo = max(0, i - 4 * c - 3)
                width = (i - 4 * c - lo + 1) * P
                for h in range(HG):
                    a = 4 * (GROUP_STEPS * g + SCORE_STEPS[qb] + kt) + h
                    if c <= 1:
                        hold(dve, s["max_ready"], a + 1, s["dve_passed"])
                    else:
                        dve.wait_ge(s["max_ready"], a + 1)
                    dst = mpart[:, qb % 2, h, i_, c:c + 1]
                    if c <= 1:
                        col = (lo - i) * P + 896
                        V.tensor_tensor_reduce(out=dump[:, h % 2, 0:width], in0=ps[:, 4 + h % 2, 0:width],
                                               in1=bq_sb[:, p, h, col:col + width], scale=1.0, scalar=NEG,
                                               op0=ALU.add, op1=ALU.max, accum_out=dst).then_inc(s["max_done"], 1)
                    else:
                        V.reduce_max(dst, ps[:, 4 + h % 2, 0:width], AX.X).then_inc(s["max_done"], 1)

            def negate_max(g, qb):
                unit = NQB * g + qb
                wait(dve, s["msplit"], 4 * unit)
                dve.wait_ge(s["max_done"], 4 * (GROUP_STEPS * g + SCORE_STEPS[qb] + 4 * (qb + 1)))
                V.tensor_reduce(negm[:, :], mpart[:, qb % 2, :, :, 0:qb + 1].rearrange("p h i c -> p (h i) c"),
                                AX.X, ALU.max, negate=True).then_inc(s["negmax_done"], 1)

            def finish_rows(g, qb):
                unit = NQB * g + qb
                dve.wait_ge(s["m_turned"], unit + 1)
                wait(dve, s["mrow_stored"], 16 * unit)
                V.tensor_copy(m_rows[:, :], ps[:, 7, :].bitcast(BF16)[0:48, 0:P]).then_inc(s["m_copied"], 1)

            def take_output(g, qb):
                dve.wait_ge(s["pv_done"], GROUP_STEPS * g + SCORE_STEPS[qb] + 4 * (qb + 1))
                V.tensor_copy(o_sb[:, :], ps[:, 6, :]).then_inc(s["o_copied"], 1)

            def normalise(g, qb):
                unit = NQB * g + qb
                dve.wait_ge(s["o_turned"], unit + 1)
                o4 = ps[:, 7, :].rearrange("p (n e) -> p n e", e=32)
                V.reciprocal(recip[:, :].rearrange("p (n e) -> p n e", e=1), o4[:, :, DK:DK + 1]
                             ).then_inc(s["recip_done"], 1)
                wait(dve, att_stored[qb % 2], 16 * (2 * g + qb // 2))
                dve.wait_ge(s["recip_done"], unit + 1)
                V.tensor_tensor(att[:, qb % 2].rearrange("p i (h d) -> p (i h) d", h=HG), o4[:, :, 0:DK],
                                recip[:, :].rearrange("p (n e) -> p n e", e=1).to_broadcast([P, 16, DK]),
                                ALU.mult).then_inc(s["att_done"], 1)

            def unit_dve(gB, gA, pA, qb, prevB, prevA):
                if gA is not None and qb == 0:
                    dve.wait_ge(biasq_loaded[pA], 8 * (gA - pA) + 16)
                for kt in range(4 * (qb + 1)):
                    if gA is not None:
                        maxima(gA, pA, qb, kt)
                    if kt == 0 and prevB is not None:
                        take_output(*prevB)
                    if kt == 0 and prevA is not None:
                        finish_rows(*prevA)
                    if kt == 1 and prevB is not None:
                        normalise(*prevB)
                if gA is not None:
                    negate_max(gA, qb)

            def schedule(unit_of, g):
                gB, pB = g
                gA = 0 if gB is None else gB + 1
                pA = 0 if gB is None else 1 - pB
                if isinstance(gB, int) and gB == GROUPS - 1:
                    gA = None
                for qb in range(NQB):
                    if gB is None:
                        prevB, prevA = None, (gA, qb - 1) if qb else None
                    else:
                        prevA = (gB, NQB - 1) if qb == 0 else (gB + 1, qb - 1) if gA is not None else None
                        prevB = (gB, qb - 1) if qb else None if isinstance(gB, int) and gB == 0 else (gB - 1, NQB - 1)
                    unit_of(gB, pB, gA, pA, qb, prevB, prevA)

            def du(gB, pB, gA, pA, qb, prevB, prevA):
                unit_dve(gB, gA, pA, qb, prevB, prevA)

            schedule(du, (None, None))
            schedule(du, (0, 0))
            with dve.Fori(0, 3) as i:
                schedule(du, (1 + 2 * i, 1))
                schedule(du, (2 + 2 * i, 0))
            schedule(du, (7, 1))
            take_output(7, 3)
            normalise(7, 3)

            def layer_norm(i, u, y, xin, r, stt, mvt, sdt, step, stdsem, aggr, waits):
                for sm, v in waits:
                    dve.wait_ge(sm, v)
                base = 8 * i + 4 * u
                if y is not None:
                    V.tensor_tensor(r, y, xin, ALU.add).then_inc(step, 1)
                    dve.wait_ge(step, base + 1)
                    V.bn_stats(stt, r).then_inc(step, 1)
                else:
                    V.bn_stats(stt, r).then_inc(step, 2)
                hold(dve, step, base + 2, s["dve_passed"])
                V.bn_aggr(mvt, stt).then_inc(aggr, 1)
                dve.wait_ge(aggr, 2 * i + u + 1)
                V.tensor_scalar(sdt[:, 1:2], mvt[:, 1:2], EPS, None, ALU.add).then_inc(step, 1)
                dve.wait_ge(stdsem, 2 * i + u + 1)
                V.reciprocal(sdt[:, 1:2], sdt[:, 0:1]).then_inc(step, 1)
                dve.wait_ge(step, base + 4)

            V.memset(logits[:, :], 0.0).then_inc(s["lg_copied"], 1)

            def norm1(i):
                for u in range(2):
                    layer_norm(i, u, ps[:, 2 + u, 0:D], xb[:, u], res[:, u], stats[:, u], mv[:, u], std[:, u],
                               s["ln_step"], s["std_done"], s["ln_aggr"],
                               ((s["y_ready"], 2 * i + u + 1), (s["xb_done"], 2 * i + u + 1)))
                    if not (isinstance(i, int) and i == 0):
                        dve.wait_ge(x1_stored[u], 32 * i)
                        dve.wait_ge(s["x1_turned"], 2 * i + u - 1)
                    V.tensor_scalar(x1[:, u], res[:, u], mv[:, u, 0:1], std[:, u, 1:2], ALU.subtract, ALU.mult
                                    ).then_inc(s["x1_done"], 1)

            norm1(0)
            with dve.Fori(1, 16) as i:
                norm1(i)

            dve.wait_ge(s["lg_copied"], 33)
            lg = logits[0:64 + E, :]
            cnt = 0
            for r in range(CAP // 8):
                tv, ti = top_v[0:64 + E, 8 * r:8 * r + 8], top_i[0:64 + E, 8 * r:8 * r + 8]
                V.max(tv, lg).then_inc(s["top_step"], 1)
                cnt += 1
                dve.wait_ge(s["top_step"], cnt)
                V.max_index(ti, tv, lg).then_inc(s["top_step"], 1)
                cnt += 1
                dve.wait_ge(s["top_step"], cnt)
                V.match_replace(lg, tv, lg, NEG).then_inc(s["top_step"], 1)
                cnt += 1
                dve.wait_ge(s["top_step"], cnt)
            V.tensor_copy(top_f[0:64 + E, :], top_i[0:64 + E, :]).then_inc(s["top_step"], 1)
            cnt += 1
            dve.wait_ge(s["top_step"], cnt)
            V.tensor_scalar(top_f[64:64 + E, :], top_f[64:64 + E, :], float(HALF), None, ALU.add
                            ).then_inc(s["top_conv"], 1)
            dve.wait_ge(s["top_moved"], 32)
            V.tensor_copy(rev[:, 0, :], up_v[:, 0, ::-1]).then_inc(s["top_step"], 1)
            V.tensor_copy(rev[:, 1, :], up_v[:, 1, ::-1]).then_inc(s["top_conv"], 1)
            dve.wait_ge(s["top_turned"], 1)
            V.tensor_copy(tr[:, :, :].rearrange("p n e -> p (n e)"), ps[:, 0, 0:4 * E]).then_inc(s["top_step"], 1)
            cnt += 2
            dve.wait_ge(s["top_step"], cnt)
            V.tensor_tensor(pick_m[:, :], tr[:, 0], tr[:, 2], ALU.is_ge).then_inc(s["top_sel"], 1)
            V.tensor_tensor(pick_v[:, :], tr[:, 0], tr[:, 2], ALU.max).then_inc(s["top_sel"], 1)
            V.tensor_tensor(pick_i[:, :], tr[:, 1], tr[:, 3], ALU.subtract).then_inc(s["top_step"], 1)
            cnt += 1
            dve.wait_ge(s["top_step"], cnt)
            dve.wait_ge(s["top_sel"], 2)
            V.tensor_tensor(pick_d[:, :], pick_i[:, :], pick_m[:, :], ALU.mult).then_inc(s["top_step"], 1)
            cnt += 1
            dve.wait_ge(s["top_step"], cnt)
            V.tensor_tensor(pick_i[:, :], pick_d[:, :], tr[:, 3], ALU.add).then_inc(s["top_step"], 1)
            cnt += 1
            dve.wait_ge(s["top_step"], cnt)
            V.tensor_copy(idx[:, :], pick_i[:, :]).then_inc(s["top_sel"], 2)
            dve.wait_ge(s["allmax"], 1)
            V.tensor_tensor(pick_d[:, :], pick_v[:, :], allred[:, 0], ALU.subtract).then_inc(s["wexp"], 1)
            dve.wait_ge(s["allmax"], 2)
            V.reciprocal(pick_m[:, :], allred[:, 1]).then_inc(s["top_step"], 1)
            cnt += 1
            dve.wait_ge(s["top_step"], cnt)
            V.tensor_tensor(gate[:, :], pexp[:, :], pick_m[:, :], ALU.mult).then_inc(s["top_step"], 1)
            cnt += 1
            dve.wait_ge(s["top_step"], cnt)

            def small(e, n):
                V.tensor_copy(b1_c[:, n], b1T[:, bass.ds(e * 2 * S, 2 * S)])
                V.tensor_copy(gate_c[:, n], gate[:, bass.ds(e, 1)]).then_inc(s["small_copied"], 1)

            def turn_tokens(e, n):
                dve.wait_ge(s["xg_turned"], e + 1)
                V.tensor_copy(xgT[:, n % 2].rearrange("p t c -> p (t c)"), ps[:, 0, 0:2 * P]
                              ).then_inc(s["xg_copied"], 1)

            def scale_y(e, n):
                dve.wait_ge(s["y2_ready"], e + 1)
                dve.wait_ge(s["small_copied"], e + 1)
                if not (isinstance(e, int) and e < 2):
                    dve.wait_ge(s["scattered"], 16 * (e - 1))
                V.tensor_scalar(y_sb[:, n % 2], ps[:, 6 + n % 2, 0:D], gate_c[:, n], None, ALU.mult
                                ).then_inc(s["y2_scaled"], 1)

            small(0, 0)
            turn_tokens(0, 0)
            for n in range(NBUF):
                small(n + 1, (n + 1) % NBUF)
                turn_tokens(n + 1, (n + 1) % NBUF)
                scale_y(n, n)
            with dve.Fori(1, E // NBUF - 1) as i:
                for n in range(NBUF):
                    e = NBUF * i + n
                    small(e + 1, (n + 1) % NBUF)
                    turn_tokens(e + 1, (n + 1) % NBUF)
                    scale_y(e, n)
            for n in range(NBUF):
                e = E - NBUF + n
                if e + 1 < E:
                    small(e + 1, (n + 1) % NBUF)
                    turn_tokens(e + 1, (n + 1) % NBUF)
                scale_y(e, n)

            def norm2(i):
                for u in range(2):
                    layer_norm(i, u, None, None, fin_in[:, u], fstats[:, u], fmv[:, u], fstd[:, u],
                               s["fin_step"], s["fin_std"], s["fin_aggr"],
                               ((acc_loaded[u], 16 * i + 16),))
                    if not (isinstance(i, int) and i == 0):
                        dve.wait_ge(fin_stored[u], 16 * i)
                    V.tensor_scalar(fin_out[:, u], fin_in[:, u], fmv[:, u, 0:1], fstd[:, u, 1:2],
                                    ALU.subtract, ALU.mult).then_inc(s["fin_done"], 1)

            norm2(0)
            with dve.Fori(1, 16) as i:
                norm2(i)

        @block.tensor
        def _(pe):
            mm, tp = nc.tensor.matmul, nc.tensor.transpose
            pe.wait_ge(zeroed, 2)
            pe.wait_ge(consts, 3)
            pe.wait_ge(loaded_w, 16 * 10)
            for n in range(4):
                for it in range(DT):
                    for ot in range(DT):
                        last = tp(ps[:, n, it * D + ot * P:it * D + (ot + 1) * P],
                                  w_nat[:, n, ot, it * P:(it + 1) * P], ident[:, :])
                last.then_inc(turned, 1)
            for it in range(DT):
                last = tp(ps[:, 4, it * E:(it + 1) * E], wr_nat[:, it * P:(it + 1) * P], ident[0:E, 0:E])
            last.then_inc(turned, 1)
            pe.wait_ge(s["loaded_b1"], 16)
            for j in range(2):
                for r in range(2):
                    last = tp(ps[:, 5, (2 * j + r) * 96:(2 * j + r + 1) * 96], b1_nat[:, r, j::2], ident[0:96, 0:96])
            last.then_inc(turned, 1)
            for r in range(4):
                last = tp(ps[0:H, 6, r * P:(r + 1) * P], tab_nat[:, r, :], ident[:, :])
            last.then_inc(turned, 1)
            pe.wait_ge(turned_copied, 6)
            pe.wait_ge(s["bias_step"], 1)

            for b in range(B):
                with pe.Fori(0, 2) as i:
                    for u in range(2):
                        n = 2 * i + u + 4 * b
                        pe.wait_ge(x_loaded[u], 16 * (i + 2 * b) + 16)
                        for it in range(DT):
                            for a in range(4):
                                last = tp(ps[:, it, a * P:(a + 1) * P], x_sb[:, u, a, it * P:(it + 1) * P], ident[:, :])
                            last.then_inc(s["xT_ready"], 1)
                        pe.wait_ge(s["xT_copied"], 2 * n + 2)
                        for j in range(4):
                            pe.wait_ge(s["q32_done"], QFREE + 4 * (n - 1) + j + 1)
                            for it in range(DT):
                                last = mm(ps[:, 2 + j, :], lhsT=WT[:, j // 2, it, (j % 2) * P:(j % 2 + 1) * P],
                                          rhs=xT[:, u, it, :], start=it == 0, stop=it == DT - 1)
                            last.then_inc(s["qk_ready"], 1)
                        for vb in range(2):
                            pe.wait_ge(s["v_copied"], VFREE + 4 * (n - 1) + 2 * vb + 2)
                            for tt in (2 * vb, 2 * vb + 1):
                                for it in range(DT):
                                    last = mm(ps[:, 6 + vb, (tt % 2) * D:(tt % 2 + 1) * D],
                                              lhsT=xT[:, u, it, tt * P:(tt + 1) * P], rhs=WT[:, 2, it, :],
                                              start=it == 0, stop=it == DT - 1)
                            last.then_inc(s["v_ready"], 1)

            def scores(g, p, qb, kt, half):
                step = GROUP_STEPS * g + SCORE_STEPS[qb] + kt
                q0 = max(0, kt - 4 * qb) * P
                c0 = max(0, 4 * qb - kt) * P
                band = min(QB - q0, BAND - c0)
                wait(pe, s["exp_done"], 2 * step + half - 1)
                for hh in range(2):
                    h = 2 * half + hh
                    last = mm(ps[:, h, q0:QB], lhsT=Ks[0:ROWS + MROWS, p, h, kt * P:(kt + 1) * P],
                              rhs=Qs[0:ROWS + MROWS, p, h, qb * QB + q0:(qb + 1) * QB], start=True, stop=band <= 0)
                    if band > 0:
                        for part in range(2):
                            last = mm(ps[:, h, q0:q0 + band], lhsT=identh[:, :],
                                      rhs=bk_sb[:, p, h, part, c0:c0 + band], start=False, stop=part == 1)
                last.then_inc(s["s_ready"], 1)

            def max_scores(g, p, qb, kt, heads):
                i_, c = divmod(kt, qb + 1)
                i = 4 * qb + i_
                lo, hi = max(0, i - 4 * c - 3), i - 4 * c + 1
                for h in heads:
                    a = 4 * (GROUP_STEPS * g + SCORE_STEPS[qb] + kt) + h
                    wait(pe, s["max_done"], a - 1)
                    mm(ps[:, 4 + h % 2, 0:(hi - lo) * P], lhsT=Qs[0:ROWS, p, h, i * P:(i + 1) * P],
                       rhs=Ks[0:ROWS, p, h, lo * P:hi * P], start=True, stop=True).then_inc(s["max_ready"], 1)

            def values(g, p, qb, kt):
                step = GROUP_STEPS * g + SCORE_STEPS[qb] + kt
                q0 = max(0, kt - 4 * qb) * P
                if kt == 0:
                    wait(pe, s["o_copied"], NQB * g + qb)
                pe.wait_ge(s["exp_done"], 2 * step + 2)
                for h in range(HG):
                    last = mm(ps[32 * h:32 * h + 32, 6, q0:QB], lhsT=Vs[:, p, kt, h, :],
                              rhs=probs[:, kt % 2, h // 2, h % 2, q0:QB], start=kt == 0, stop=kt == 4 * qb + 3)
                last.then_inc(s["pv_done"], 1)

            def turn_max(g, qb):
                unit = NQB * g + qb
                wait(pe, s["m_copied"], unit)
                wait(pe, s["att_done"], unit - NQB)
                hold(pe, s["msplit"], 4 * unit + 4, s["pe_passed"])
                tp(ps[:, 7, :].bitcast(BF16)[0:48, 0:P], m_parts[:, :, :].rearrange("p s n -> p (s n)"),
                   identb[:, :]).then_inc(s["m_turned"], 1)

            def turn_output(g, qb, has_max):
                unit = NQB * g + qb
                pe.wait_ge(s["o_copied"], unit + 1)
                wait(pe, s["att_done"], unit)
                if has_max:
                    pe.wait_ge(s["m_copied"], unit + NQB + 1)
                for i_ in range(4):
                    last = tp(ps[:, 7, i_ * P:(i_ + 1) * P], o_sb[:, i_ * P:(i_ + 1) * P], ident[:, :])
                last.then_inc(s["o_turned"], 1)

            def unit_pe(gB, pB, gA, pA, qb, prevB, prevA):
                if gA is not None:
                    pe.wait_ge(qk_loaded[pA][qb], 16 * (gA - pA) + 32)
                if gB is not None:
                    pe.wait_ge(mrow_loaded[qb], 16 * gB + 16)
                    if qb == 0:
                        pe.wait_ge(group_loaded[pB], 16 * (gB - pB) + 32)
                for kt in range(4 * (qb + 1)):
                    for half in range(2):
                        if gB is not None:
                            scores(gB, pB, qb, kt, half)
                        if gA is not None:
                            max_scores(gA, pA, qb, kt, (2 * half, 2 * half + 1))
                    if kt == 0 and prevB is not None:
                        gP, qP = prevB
                        values(gP, pB if qb else 1 - pB, qP, 4 * qP + 3)
                    if kt == 0 and prevA is not None:
                        turn_max(*prevA)
                    if kt == 1 and prevB is not None:
                        turn_output(*prevB, prevA is not None)
                    if gB is not None and kt > 0:
                        values(gB, pB, qb, kt - 1)

            def schedule(g):
                gB, pB = g
                gA = 0 if gB is None else gB + 1
                pA = 0 if gB is None else 1 - pB
                if isinstance(gB, int) and gB == GROUPS - 1:
                    gA = None
                for qb in range(NQB):
                    if gB is None:
                        prevB, prevA = None, (gA, qb - 1) if qb else None
                    else:
                        prevA = (gB, NQB - 1) if qb == 0 else (gB + 1, qb - 1) if gA is not None else None
                        prevB = (gB, qb - 1) if qb else None if isinstance(gB, int) and gB == 0 else (gB - 1, NQB - 1)
                    unit_pe(gB, pB, gA, pA, qb, prevB, prevA)

            pe.wait_ge(s["v_copied"], VFREE + 32)
            schedule((None, None))
            schedule((0, 0))
            with pe.Fori(0, 3) as i:
                schedule((1 + 2 * i, 1))
                schedule((2 + 2 * i, 0))
            schedule((7, 1))
            values(7, 1, 3, 15)
            turn_output(7, 3, False)

            def attended(i):
                for u in range(2):
                    pe.wait_ge(at_loaded[u], 16 * i + 16)
                    for it in range(DT):
                        last = tp(ps[:, u, it * P:(it + 1) * P],
                                  at_in[:, u].rearrange("p g n -> p (g n)")[:, it * P:(it + 1) * P], ident[:, :])
                    last.then_inc(s["at_turned"], 1)

            def project_out(i):
                for u in range(2):
                    pe.wait_ge(s["at_copied"], 2 * i + u + 1)
                    for it in range(DT):
                        last = mm(ps[:, 2 + u, 0:D], lhsT=atT[:, u, it, :], rhs=WOT[:, it, :],
                                  start=it == 0, stop=it == DT - 1)
                    last.then_inc(s["y_ready"], 1)

            def turn_x1(i):
                for u in range(2):
                    pe.wait_ge(s["x1_done"], 2 * i + u + 1)
                    for it in range(DT):
                        last = tp(ps[:, 4 + u, it * P:(it + 1) * P], x1[:, u, it * P:(it + 1) * P], ident[:, :])
                    last.then_inc(s["x1_turned"], 1)

            def route(i):
                for u in range(2):
                    pe.wait_ge(s["x1_copied"], 2 * i + u + 1)
                    if not (isinstance(i, int) and i == 0):
                        pe.wait_ge(s["lg_copied"], 2 * i + u)
                    for it in range(DT):
                        last = mm(ps[64 * u:64 * u + E, 6 + u, 0:P], lhsT=WrT[:, it, :], rhs=x1T[:, u, it, :],
                                  start=it == 0, stop=it == DT - 1)
                    last.then_inc(s["lg_ready"], 1)

            pe.wait_ge(s["att_done"], 32)
            attended(0)
            project_out(0)
            with pe.Fori(1, 16) as i:
                attended(i)
                turn_x1(i - 1)
                project_out(i)
                route(i - 1)
            turn_x1(15)
            route(15)

            pe.wait_ge(s["top_conv"], 2)
            pe.wait_ge(s["lg_copied"], 33)
            for n, src in enumerate((top_v[0:E, :], top_f[0:E, :], rev[:, 0, :], rev[:, 1, :])):
                last = tp(ps[:, 0, n * E:(n + 1) * E], src, ident[0:E, 0:E])
            last.then_inc(s["top_turned"], 1)
            pe.wait_ge(s["top_sel"], 1)

            def turn_tokens(e, n):
                pe.wait_ge(gathered[n], 4 * (e - n) + 16)
                if not (isinstance(e, int) and e == 0):
                    pe.wait_ge(s["xg_copied"], e)
                for it in range(DT):
                    last = tp(ps[:, 0, it * P:(it + 1) * P], xg[:, n, it * P:(it + 1) * P], ident[:, :])
                last.then_inc(s["xg_turned"], 1)

            def hidden(e, n):
                pe.wait_ge(w_loaded[n], 12 * (e - n) + 48)
                pe.wait_ge(s["xg_copied"], e + 1)
                for sl in range(S):
                    for j in range(2):
                        m = 2 * sl + j
                        for it in range(DT):
                            last = mm(ps[:, 2 + 2 * (n % 2) + m // 4, (m % 4) * P:(m % 4 + 1) * P],
                                      lhsT=w1_sb[:, n, sl, it, :].rearrange("p (c j) -> p c j", j=2)[:, :, j],
                                      rhs=xgT[:, n % 2, it, :], start=it == 0, stop=it == DT - 1)
                    if sl % 2 == 1:
                        last.then_inc(s["h_ready"], 1)

            def outputs(e, n):
                bank = ps[:, 6 + n % 2, 0:D]
                if not (isinstance(e, int) and e < 2):
                    pe.wait_ge(s["y2_scaled"], e - 1)
                mm(bank, lhsT=ones_row[:, :], rhs=b2_sb[:, n, :], start=True, stop=True)
                for sl in range(S):
                    for j in range(2):
                        pe.wait_ge(s["gelu_done"], 8 * e + 2 * sl + j + 1)
                        last = mm(bank[:, sl * KO:(sl + 1) * KO], lhsT=hid[:, n % 2, 2 * sl + j, :],
                                  rhs=w2_sb[:, n, sl, j * KO:(j + 1) * KO], start=False,
                                  stop=j == 1, skip_group_check=True)
                last.then_inc(s["y2_ready"], 1)

            turn_tokens(0, 0)
            for n in range(NBUF):
                hidden(n, n)
                turn_tokens(n + 1, (n + 1) % NBUF)
                outputs(n, n)
            with pe.Fori(1, E // NBUF - 1) as i:
                for n in range(NBUF):
                    e = NBUF * i + n
                    hidden(e, n)
                    turn_tokens(e + 1, (n + 1) % NBUF)
                    outputs(e, n)
            for n in range(NBUF):
                e = E - NBUF + n
                hidden(e, n)
                if e + 1 < E:
                    turn_tokens(e + 1, (n + 1) % NBUF)
                outputs(e, n)


_INS = ["L0_attn_x", "L0_attn_WQ", "L0_attn_bQ", "L0_attn_WK", "L0_attn_bK", "L0_attn_WV", "L0_attn_bV",
        "L0_attn_WO", "L0_attn_bO", "L0_attn_rel_pos_table", "L0_ffn_Wr", "L0_ffn_W1", "L0_ffn_b1",
        "L0_ffn_W2", "L0_ffn_b2"]


def kernel(**inputs):
    import numpy as np
    import concourse.bacc as bacc
    from concourse.bass_utils import run_bass_kernel_spmd

    nc = bacc.Bacc("TRN2", target_bir_lowering=False, num_devices=1)
    arrays, args = {}, []
    for name in _INS:
        a = np.ascontiguousarray(inputs[name])
        arrays[name] = a
        args.append(nc.dram_tensor(name, a.shape, mybir.dt.from_np(a.dtype), kind="ExternalInput").ap())
    result = nc.dram_tensor("result", (B, T, D), F32, kind="ExternalOutput").ap()
    moe_layer(nc, *args, result)
    r = run_bass_kernel_spmd(nc, [arrays], core_ids=[0])
    return r.results[0]["result"]
```

```python
import concourse.bass as bass
from concourse import mybir
from contextlib import ExitStack

F32 = mybir.dt.float32
BF16 = mybir.dt.bfloat16
F16 = mybir.dt.float16
U32 = mybir.dt.uint32
ALU = mybir.AluOpType
ACT = mybir.ActivationFunctionType
AX = mybir.AxisListType

P = 128
B, T, D = 2, 2048, 256
H, DK = 16, 16
NT = B * T
TILES = NT // P
DT = D // P
MAXLEN = 512
E, S, M = 48, 4, 256
KO = D // S
CAP = int(1.5 * NT / E)
EPS = 1e-5

HG = 4
GROUPS = B * H // HG
QB = 512
NQB = T // QB
KT = T // P
SPLIT_Q = (0, 0, 0, 1, 1, 2)
SPLIT_K = (0, 1, 2, 0, 1, 0)
C = len(SPLIT_Q)
ROWS = C * DK
MROWS = 3
BAND = 5 * P
MASKED = -60000.0
NEG = -1.0e30
WLEN = 1152
HALF = NT // 2
NBUF = 4
WLOADS = S + 2
PAIR = 2 * P
PAIRS = T // PAIR
FBUF, FT = 4, 4
CHUNKS = TILES // FT
QFREE, VFREE, RFREE = 4, 4, 2
SCORE_STEPS = [0, 4, 12, 24]
GROUP_STEPS = 40


def wait(eng, sem, count):
    if isinstance(count, int) and count <= 0:
        return
    eng.wait_ge(sem, count)


def hold(eng, sem, count, passed):
    if isinstance(count, int) and count <= 0:
        return
    eng.wait_ge(sem, count)
    if not isinstance(count, int):
        eng.sem_inc(passed, 1)


def moe_layer(nc, x, WQ, bQ, WK, bK, WV, bV, WO, bO, table, Wr, W1, b1, W2, b2, out):
    ctx = ExitStack()
    with ctx:
        def sb_in(stack):
            return lambda name, shape, dt: stack.enter_context(nc.sbuf_tensor(name, shape, dt))

        def sem(name):
            return ctx.enter_context(nc.semaphore(name))

        def dram(name, shape, dt):
            return nc.dram_tensor(name, shape, dt, kind="Internal").ap()

        sb = sb_in(ctx)

        q_dram = dram("q_split", [B * H, DK, C, T], BF16)
        k_dram = dram("k_split", [B * H, DK, C, T], BF16)
        v_dram = dram("v_groups", [GROUPS, P, KT * HG * 32], F32)
        m_dram = dram("row_max", [GROUPS * NQB, MROWS * HG * 4, P], BF16)
        bias_dram = dram("bias_parts", [H, 2, 768], F16)
        biasw_dram = dram("bias_wide", [H, WLEN], F32)
        att_dram = dram("attended", [B, T, D], F32)
        b2_dram = dram("b2_split", [E, 3, D], BF16)
        x1_dram = dram("normed", [NT, D], F32)
        acc_dram = dram("summed", [NT, D], F32)

        bias_by_key = bass.AP(bias_dram.tensor, 1, [[2 * 768, H], [1, P // 2], [768, 2], [64, 2], [1, BAND]])
        bias_by_query = bass.AP(biasw_dram.tensor, 1, [[WLEN, H], [1, P], [1, 1024]])

        ps = ctx.enter_context(nc.psum_tensor("banks", [P, 8, 512], F32))

        ident = sb("ident", [P, P], F32)
        identb = sb("identb", [P, P], BF16)
        flip = sb("flip", [P, P // 2], F16)
        ones_rows = sb("ones_rows", [3, P], BF16)
        WOT = sb("WOT", [P, DT, D], F32)
        WrT = sb("WrT", [P, DT, E], F32)
        bO_b = sb("bO_b", [P, D], F32)
        b1T = sb("b1T", [P, E * S * 2], F32)
        b2_sb = sb("b2_sb", [3, NBUF, D], BF16)

        names = """v_cleared loaded_w loaded_b1 loaded_b2 b2_step b2_stored zeroed consts turned turned_copied ln_aggr fin_aggr dve_passed pool_passed pe_passed bias_step bias_stored
            x_loaded0 x_loaded1 xT_ready xT_copied qk_ready q32_done s1_done rest_done s2_done s3_done 
            v_ready v_copied v_stored0 v_stored1 pads
            biasq_loaded0 biasq_loaded1 group_loaded0 group_loaded1 mrow_stored
            s_ready exp_done max_ready max_done negmax_done msplit m_turned m_copied
            pv_done o_copied o_turned recip_done att_done att_stored0 att_stored1
            at_loaded0 at_loaded1 xr_loaded0 xr_loaded1 at_turned at_copied y_ready std_done x1_done
            x1_stored0 x1_stored1 acc_copied res_done ln_stats ln_rstd var_done x1_turned x1_copied lg_ready lg_copied xb_done
            top_step top_moved top_conv top_turned top_sel allmax wexp
            w_loaded0 w_loaded1 w_loaded2 w_loaded3 idx_copied idx_kept gathered0 gathered1 gathered2 gathered3 small_copied
            xg_turned xg_copied h_ready gelu_done y2_ready y2_scaled scattered
            acc_loaded0 acc_loaded1 acc_loaded2 acc_loaded3 fin_bn fin_var fin_rstd fin_std fin_done fin_stored""".split()
        s = {n: sem(n) for n in names}

        loaded_w, zeroed, consts = s["loaded_w"], s["zeroed"], s["consts"]
        turned, turned_copied = s["turned"], s["turned_copied"]
        x_loaded = [s["x_loaded0"], s["x_loaded1"]]
        split_stored = [sem(f"split_stored{j}") for j in range(4)]
        v_stored = [s["v_stored0"], s["v_stored1"]]
        qk_loaded = [[sem(f"qk_loaded{p}{c}") for c in range(4)] for p in range(2)]
        mrow_loaded = [sem(f"mrow_loaded{qb}") for qb in range(NQB)]
        biasq_loaded = [s["biasq_loaded0"], s["biasq_loaded1"]]
        group_loaded = [s["group_loaded0"], s["group_loaded1"]]
        att_stored = [s["att_stored0"], s["att_stored1"]]
        at_loaded = [s["at_loaded0"], s["at_loaded1"]]
        xr_loaded = [s["xr_loaded0"], s["xr_loaded1"]]
        x1_stored = [s["x1_stored0"], s["x1_stored1"]]
        w_loaded = [s[f"w_loaded{n}"] for n in range(NBUF)]
        gathered = [s[f"gathered{n}"] for n in range(NBUF)]
        acc_loaded = [s[f"acc_loaded{n}"] for n in range(FBUF)]

        with ExitStack() as st:
            sp_ = sb_in(st)
            w_nat = sp_("w_nat", [P, 4, DT, D], F32)
            wr_nat = sp_("wr_nat", [E, D], F32)
            b2_nat = sp_("b2_nat", [E, D], F32)
            b2_rest = sp_("b2_rest", [E, D], F32)
            b2_parts = sp_("b2_parts", [E, 3, D], BF16)
            b1_nat = sp_("b1_nat", [96, 2, M], F32)
            tab_nat = sp_("tab_nat", [P, 4, H], F32)
            WT = sp_("WT", [P, 3, DT, D], F32)
            bqk = sp_("bqk", [P, 4], F32)
            bV_b = sp_("bV_b", [P, D], F32)
            tabT = sp_("tabT", [H, MAXLEN], F32)
            far = sp_("far", [H, 1], F32)
            wide = sp_("wide", [H, WLEN], F32)
            wide_h = sp_("wide_h", [H, 2, 768], F16)
            x_sb = sp_("x_sb", [P, 2, 4, D], F32)
            xT = sp_("xT", [P, 2, DT, QB], F32)
            q32 = sp_("q32", [P, 2, QB], F32)
            rest = sp_("rest", [P, 2, QB], F32)
            parts = sp_("parts", [P, 4, 3, QB], BF16)
            v_st = sp_("v_st", [P, 2, 4, 4, HG, 32], F32)

        w1_sb = sb("w1_sb", [P, NBUF, S, DT, M], F32)
        w2_sb = sb("w2_sb", [P, NBUF, S, 2 * KO], F32)

        with ExitStack() as st:
            sa = sb_in(st)
            Q1 = sa("Q1", [P, HG, T], BF16)
            K1 = sa("K1", [P, HG, T], BF16)
            probs = sa("probs", [P, 2, 2, 2, QB], F32)
            o_sb = sa("o_sb", [P, QB], F32)
            recip = sa("recip", [P, 16], F32)
            att = sa("att", [P, 2, 4, HG * DK], F32)
            Q0 = sa("Q0", [P, HG, T], BF16)
            K0 = sa("K0", [P, HG, T], BF16)
            Qs, Ks = (Q0, Q1), (K0, K1)
            dump = sa("dump", [P, 2, QB], F32)
            mpart = sa("mpart", [P, 2, HG, 4, 4], F32)
            negm = sa("negm", [P, HG * 4], F32)
            negm_rest = sa("negm_rest", [P, HG * 4], F32)
            m_parts = sa("m_parts", [P, MROWS, HG * 4], BF16)
            m_rows = sa("m_rows", [MROWS * HG * 4, P], BF16)
            bq_sb = sa("bq_sb", [P, 2, HG, 1024], F32)
            bk_sb = sa("bk_sb", [P, 2, HG, 2, BAND], F16)
            Vs = sa("Vs", [P, 2, KT, HG, 32], F32)

        st = ctx.enter_context(ExitStack())
        sc = sb_in(st)
        at_in = sc("at_in", [P, 2, 2, D], F32)
        xr = sc("xr", [P, 2, 2, D], F32)
        xb = sc("xb", [P, 2, 2, D], F32)
        atT = sc("atT", [P, 2, DT, PAIR], F32)
        res = sc("res", [P, 2, 2, D], F32)
        x1 = sc("x1", [P, 2, 2, D], F32)
        x1T = sc("x1T", [P, 2, DT, PAIR], F32)
        stats = sc("stats", [P, 4, 6], F32)
        mv = sc("mv", [P, 4, 2], F32)
        var = sc("var", [P, 4], F32)
        std = sc("std", [P, 4], F32)
        rstd = sc("rstd", [P, 4], F32)
        logits = sc("logits", [P, HALF], F32)
        top_v = sc("top_v", [P, P], F32)
        top_i = sc("top_i", [P, P], U32)
        top_f = sc("top_f", [P, P], F32)
        up_v = sc("up_v", [E, 2, P], F32)
        rev = sc("rev", [E, 2, P], F32)
        tr = sc("tr", [P, 4, E], F32)
        pick_m = sc("pick_m", [P, E], F32)
        pick_v = sc("pick_v", [P, E], F32)
        pick_d = sc("pick_d", [P, E], F32)
        pick_i = sc("pick_i", [P, E], F32)
        idx = sc("idx", [P, E], U32)
        allred = sc("allred", [P, 2, E], F32)
        pexp = sc("pexp", [P, E], F32)
        gate = sc("gate", [P, E], F32)
        idx_c = sc("idx_c", [P, NBUF, 1], U32)
        idx_s = sc("idx_s", [P, NBUF, 1], U32)
        xg = sc("xg", [P, NBUF, D], F32)
        xgT = sc("xgT", [P, 2, DT, P], F32)
        hid = sc("hid", [P, 2, 2 * S, P], F32)
        b1_c = sc("b1_c", [P, NBUF, 2 * S], F32)
        gate_c = sc("gate_c", [P, NBUF, 1], F32)
        y_sb = sc("y_sb", [P, 2, D], F32)
        fin_in = sc("fin_in", [P, FBUF, FT, D], F32)
        fin_out = sc("fin_out", [P, FBUF, FT, D], F32)
        fstats = sc("fstats", [P, 2, FT, 6], F32)
        fmv = sc("fmv", [P, 2, FT, 2], F32)
        fvar = sc("fvar", [P, 2, FT], F32)
        fstd = sc("fstd", [P, 2, FT], F32)
        frstd = sc("frstd", [P, 2, FT], F32)

        block = ctx.enter_context(nc.Block())

        def expert_load(sp, e, n):
            for sl in range(S):
                sp.dma_start(w1_sb[:, n, sl, :, :],
                             W1[bass.ds(e, 1), sl].rearrange("e (t p) m -> p (e t) m", p=P)).then_inc(w_loaded[n], 16)
            sp.dma_start(w2_sb[:, n, :, :],
                         W2[bass.ds(e, 1)].rearrange("e s (p j) k -> p (e s) (j k)", p=P)).then_inc(w_loaded[n], 16)
            sp.dma_start(b2_sb[:, n, :],
                         b2_dram[bass.ds(e, 1)].rearrange("e r k -> (e r) k")).then_inc(w_loaded[n], 16)

        @block.sync
        def _(sp):
            for n, w in enumerate((WQ, WK, WV, WO)):
                sp.dma_start(w_nat[:, n, :, :], w.rearrange("(t p) i -> p t i", p=P)).then_inc(loaded_w, 16)
            sp.dma_start(wr_nat[:, :], Wr).then_inc(loaded_w, 16)
            sp.dma_start(tab_nat[:, :, :],
                         table[MAXLEN - 1:2 * MAXLEN - 1, :].rearrange("(r p) h -> p r h", p=P)).then_inc(loaded_w, 16)
            sp.dma_start(b1_nat[:, :, :], b1.rearrange("e s m -> (e s) m").rearrange("(r p) m -> p r m", p=96)
                         ).then_inc(s["loaded_b1"], 16)
            sp.dma_start(b2_nat[:, :], b2.rearrange("e s k -> e (s k)")).then_inc(s["loaded_b2"], 16)
            with nc.allow_non_contiguous_dma(reason="two small bias vectors, one element to a partition"):
                for n, b in enumerate((bQ, bK)):
                    sp.dma_start(bqk[:, 2 * n:2 * n + 2], b.rearrange("(t p) -> p t", p=P)).then_inc(loaded_w, 16)
            for dst, b in ((bV_b, bV), (bO_b, bO)):
                sp.dma_start(dst[:, :], b.rearrange("(a n) -> a n", a=1).to_broadcast([P, D])).then_inc(loaded_w, 16)

            def load_x(n, u):
                sp.dma_start(x_sb[:, u], x.rearrange("b t d -> (b t) d")[bass.ds(n * QB, QB), :].rearrange(
                    "(a p) d -> p a d", p=P)).then_inc(x_loaded[u], 16)

            load_x(0, 0)
            load_x(1, 1)
            sp.wait_ge(s["bias_step"], 8)
            sp.dma_start(bias_dram[:, :, :], wide_h[:, :, :]).then_inc(s["bias_stored"], 16)
            sp.dma_start(biasw_dram[:, :], wide[:, :]).then_inc(s["bias_stored"], 16)

            def load_chunk(hg, p, c):
                for dst, src in ((Qs, q_dram), (Ks, k_dram)):
                    sp.dma_start(dst[p][0:ROWS, :, c * QB:(c + 1) * QB],
                                 src[bass.ds(p * H + hg * HG, HG), :, :, c * QB:(c + 1) * QB].rearrange(
                                     "h d c t -> (d c) h t")).then_inc(qk_loaded[p][c], 16)

            def load_bias_k(hg, p):
                for part in range(2):
                    for half in range(2):
                        sp.dma_start(bk_sb[64 * part:64 * part + 64, p, :, half, :],
                                     bias_by_key[bass.ds(hg * HG, HG), :, part, half, :].rearrange("h p c -> p h c")
                                     ).then_inc(group_loaded[p], 16)

            def load_values(hg, p):
                sp.dma_start(Vs[:, p].rearrange("p t h e -> p (t h e)"),
                             v_dram[bass.ds(p * 4 + hg, 1)].rearrange("g p n -> p (g n)")).then_inc(group_loaded[p], 16)

            def load_bias_q(hg, p):
                sp.dma_start(bq_sb[:, p, :, :], bias_by_query[bass.ds(hg * HG, HG)].rearrange("h p c -> p h c")
                             ).then_inc(biasq_loaded[p], 16)

            sp.wait_ge(s["b2_step"], 4)
            sp.dma_start(b2_dram[:, :, :], b2_parts[:, :, :]).then_inc(s["b2_stored"], 16)
            sp.wait_ge(s["bias_stored"], 32)
            load_bias_q(0, 0)
            load_bias_k(0, 0)

            def store_pair(i, b, load_more):
                for u in range(2):
                    n = 2 * i + u + 4 * b
                    t0 = (2 * i + u) * QB
                    for j in range(4):
                        sp.wait_ge(s["s3_done"], RFREE + 4 * n + j + 1)
                        dst = (q_dram, k_dram)[j // 2]
                        dst = dst[b * H + 8 * (j % 2):b * H + 8 * (j % 2) + 8, :, :, bass.ds(t0, QB)].rearrange(
                            "h d c t -> (h d) c t")
                        src = parts[:, j]
                        if j // 2 == 0:
                            runs = ((0, 3, src[:, 0:1].to_broadcast([P, 3, QB])),
                                    (3, 5, src[:, 1:2].to_broadcast([P, 2, QB])), (5, 6, src[:, 2:3]))
                        else:
                            runs = ((0, 3, src[:, 0:3]), (3, 5, src[:, 0:2]), (5, 6, src[:, 0:1]))
                        for c0, c1, part in runs:
                            sp.dma_start(dst[:, c0:c1, :], part).then_inc(split_stored[j], 16)
                    sp.wait_ge(s["v_copied"], VFREE + 4 * n + 4)
                    sp.dma_start(
                        v_dram[b * 4:b * 4 + 4, :, bass.ds((2 * i + u) * 4 * HG * 32, 4 * HG * 32)].rearrange(
                            "g p n -> p g n"),
                        v_st[:, u].rearrange("p g t h e -> p g (t h e)")).then_inc(v_stored[u], 16)
                    if load_more:
                        sp.wait_ge(s["xT_ready"], 2 * n + 2)
                        load_x(n + 2, u)

            with sp.Fori(0, 2) as i:
                store_pair(i, 0, True)
            store_pair(0, 1, True)
            for j in range(4):
                sp.wait_ge(split_stored[j], 48 + 48 * 6)
            for u in range(2):
                sp.wait_ge(v_stored[u], 16 + 16 * 3)
            sp.wait_ge(s["pads"], 1)
            for c in range(4):
                load_chunk(0, 0, c)
            load_values(0, 0)
            store_pair(1, 1, False)
            for j in range(4):
                sp.wait_ge(split_stored[j], 48 + 48 * 8)
            for u in range(2):
                sp.wait_ge(v_stored[u], 16 + 16 * 4)
            sp.wait_ge(s["bias_stored"], 32)
            sp.wait_ge(s["b2_stored"], 16)

            def max_rows(g, p, qb):
                unit = NQB * g + qb
                sp.wait_ge(s["m_copied"], unit + 1)
                sp.dma_start(m_dram[bass.ds(unit, 1)].rearrange("u r t -> (u r) t"),
                             m_rows[:, :]).then_inc(s["mrow_stored"], 16)
                sp.wait_ge(s["mrow_stored"], 16 * unit + 16)
                sp.dma_start(Qs[p][ROWS:ROWS + MROWS, :, qb * QB:(qb + 1) * QB],
                             m_dram[bass.ds(unit, 1)].rearrange("u (s h i) t -> (u s) h (i t)", s=MROWS, h=HG)
                             ).then_inc(mrow_loaded[qb], 16)

            def store_att(g, hg, p, qb):
                sp.wait_ge(s["att_done"], NQB * g + qb + 1)
                sp.dma_start(
                    att_dram[p, qb * QB:(qb + 1) * QB, bass.ds(hg * HG * DK, HG * DK)].rearrange(
                        "(i p) n -> p i n", p=P), att[:, qb % 2]).then_inc(att_stored[qb % 2], 16)

            def phase(g, hg, p):
                static = isinstance(g, int)
                has_before, has_next, has_two_on = not (static and g == 0), not (static and g == GROUPS - 1), \
                    not (static and g >= GROUPS - 2)
                next_hg = hg + p
                for qb in range(NQB):
                    if qb == 0:
                        max_rows(g, p, NQB - 1)
                        if has_before:
                            store_att(g - 1, hg - 1 + p, 1 - p, NQB - 1)
                            if has_next:
                                sp.wait_ge(s["pv_done"], GROUP_STEPS * g)
                                load_bias_k(next_hg, 1 - p)
                                load_values(next_hg, 1 - p)
                    else:
                        if has_next:
                            max_rows(g + 1, 1 - p, qb - 1)
                        store_att(g, hg, p, qb - 1)
                if has_two_on:
                    sp.wait_ge(s["negmax_done"], NQB * g + NQB)
                    load_bias_q(hg + 1, p)
                    for c in range(4):
                        sp.wait_ge(s["s_ready"], 2 * (GROUP_STEPS * g + SCORE_STEPS[3] + 4 * c + 4))
                        load_chunk(hg + 1, p, c)

            sp.wait_ge(s["pads"], 2)
            max_rows(0, 0, 0)
            for c in range(4):
                load_chunk(0, 1, c)
            load_bias_q(0, 1)
            max_rows(0, 0, 1)
            load_bias_k(0, 1)
            load_values(0, 1)
            for n in range(NBUF // 2):
                expert_load(sp, n, n)
            max_rows(0, 0, 2)
            for n in range(NBUF // 2, NBUF):
                expert_load(sp, n, n)
            phase(0, 0, 0)
            with sp.Fori(0, 2) as i:
                phase(1 + 2 * i, i, 1)
                phase(2 + 2 * i, i + 1, 0)
            phase(5, 2, 1)
            phase(6, 3, 0)
            phase(7, 3, 1)
            store_att(7, 3, 1, 3)

            for u in range(2):
                sp.wait_ge(att_stored[u], 16 * 16)

            def load_tokens(i, u):
                for dst, src, sm in ((at_in, att_dram, at_loaded[u]), (xr, x, xr_loaded[u])):
                    sp.dma_start(dst[:, u], src[u, bass.ds(i * PAIR, PAIR), :].rearrange("(v p) n -> p v n", p=P)
                                 ).then_inc(sm, 16)

            def store_x1(i, u):
                sp.wait_ge(s["x1_done"], 2 * i + u + 1)
                sp.dma_start(x1_dram[bass.ds(i * PAIR + u * T, PAIR), :].rearrange("(v p) n -> p v n", p=P),
                             x1[:, u]).then_inc(x1_stored[u], 16)

            for u in range(2):
                load_tokens(0, u)
            with sp.Fori(0, PAIRS - 1) as i:
                for u in range(2):
                    sp.wait_ge(s["at_turned"], 2 * i + u + 1)
                    sp.wait_ge(s["xb_done"], 2 * i + u + 1)
                    load_tokens(i + 1, u)
                for u in range(2):
                    store_x1(i, u)
            for u in range(2):
                store_x1(PAIRS - 1, u)

            for u in range(2):
                sp.wait_ge(x1_stored[u], 16 * PAIRS)
            sp.dma_start(acc_dram[:, :], x1_dram[:, :]).then_inc(s["acc_copied"], 16)

            sp.wait_ge(s["top_conv"], 1)
            sp.dma_start(up_v[:, 0, :], top_v[64:64 + E, :]).then_inc(s["top_moved"], 16)
            sp.dma_start(up_v[:, 1, :], top_f[64:64 + E, :]).then_inc(s["top_moved"], 16)

            with sp.Fori(0, E // NBUF - 1) as i:
                for n in range(NBUF):
                    sp.wait_ge(s["y2_ready"], NBUF * i + n + 1)
                    expert_load(sp, NBUF * i + NBUF + n, n)

            def sum_rows(flat, c):
                return flat[bass.ds(c * FT * P, FT * P), :].rearrange("(v p) n -> p v n", p=P)

            out_flat = out.rearrange("b t d -> (b t) d")
            sp.wait_ge(s["scattered"], 16 * E)
            for n in range(FBUF):
                sp.dma_start(fin_in[:, n], sum_rows(acc_dram, n)).then_inc(acc_loaded[n], 16)
            for n in range(FBUF):
                sp.wait_ge(s["fin_done"], n + 1)
                sp.dma_start(sum_rows(out_flat, n), fin_out[:, n]).then_inc(s["fin_stored"], 16)
                sp.dma_start(fin_in[:, n], sum_rows(acc_dram, FBUF + n)).then_inc(acc_loaded[n], 16)
            for n in range(FBUF):
                sp.wait_ge(s["fin_done"], FBUF + n + 1)
                sp.dma_start(sum_rows(out_flat, FBUF + n), fin_out[:, n]).then_inc(s["fin_stored"], 16)
            sp.wait_ge(s["fin_stored"], 16 * CHUNKS)

        @block.gpsimd
        def _(pool):
            nc.gpsimd.memset(ident[:, :], 0.0).then_inc(zeroed, 1)
            nc.gpsimd.memset(ones_rows[:, :], 1.0).then_inc(consts, 1)
            pool.wait_ge(zeroed, 1)
            nc.gpsimd.affine_select(out=ident[:, :], in_=ident[:, :], compare_op=ALU.not_equal, fill=1.0,
                                    base=0, pattern=[[-1, P]], channel_multiplier=1).then_inc(zeroed, 1)
            pool.wait_ge(zeroed, 2)
            nc.gpsimd.tensor_copy(identb[:, :], ident[:, :]).then_inc(consts, 1)
            nc.gpsimd.tensor_tensor(flip[:, :], ident[:, P // 2 - 1::-1], ident[:, :P // 2 - 1:-1], ALU.add).then_inc(consts, 1)
            pool.wait_ge(consts, 3)
            nc.gpsimd.memset(K0[ROWS:P, :, :].rearrange("p h t -> p (h t)"), 1.0).then_inc(s["pads"], 1)

            pool.wait_ge(s["pads"], 1)

            for b in range(B):
                with pool.Fori(0, 2) as i:
                    for u in range(2):
                        for j in range(4):
                            t = 4 * (2 * i + u + 4 * b) + j
                            pool.wait_ge(s["s2_done"], t + 1)
                            nc.gpsimd.tensor_tensor(parts[:, j, 2], rest[:, j % 2], parts[:, j, 1],
                                                    ALU.subtract).then_inc(s["s3_done"], 1)

            def split_max(unit):
                step = 4 * unit
                wait(pool, s["m_turned"], unit)
                hold(pool, s["negmax_done"], unit + 1, s["pool_passed"])
                nc.gpsimd.tensor_copy(m_parts[:, 0], negm[:, :]).then_inc(s["msplit"], 1)
                pool.wait_ge(s["msplit"], step + 1)
                nc.gpsimd.tensor_tensor(negm_rest[:, :], negm[:, :], m_parts[:, 0], ALU.subtract
                                        ).then_inc(s["msplit"], 1)
                hold(pool, s["msplit"], step + 2, s["pool_passed"])
                nc.gpsimd.tensor_copy(m_parts[:, 1], negm_rest[:, :]).then_inc(s["msplit"], 1)
                pool.wait_ge(s["msplit"], step + 3)
                nc.gpsimd.tensor_tensor(m_parts[:, 2], negm_rest[:, :], m_parts[:, 1], ALU.subtract
                                        ).then_inc(s["msplit"], 1)

            split_max(0)
            pool.wait_ge(s["msplit"], 4)
            pool.wait_ge(s["s3_done"], RFREE + 32)
            for j in range(4):
                pool.wait_ge(split_stored[j], 48 + 48 * 8)
            for u in range(2):
                pool.wait_ge(v_stored[u], 16 + 16 * 4)
            pool.wait_ge(s["bias_stored"], 32)
            pool.wait_ge(s["b2_stored"], 16)
            nc.gpsimd.memset(K1[ROWS:P, :, :].rearrange("p h t -> p (h t)"), 1.0).then_inc(s["pads"], 1)
            pool.wait_ge(s["pads"], 2)
            for unit in range(1, NQB):
                split_max(unit)
            with pool.Fori(NQB, NQB * GROUPS) as unit:
                split_max(unit)

            def add_output_bias(i):
                for u in range(2):
                    wait(pool, s["res_done"], 2 * (i - 1) + u + 1)
                    pool.wait_ge(xr_loaded[u], 16 * i + 16)
                    nc.gpsimd.tensor_tensor(xb[:, u], xr[:, u], bO_b[:, :].rearrange("p (a n) -> p a n", a=1
                                            ).to_broadcast([P, 2, D]), ALU.add).then_inc(s["xb_done"], 1)

            add_output_bias(0)
            with pool.Fori(1, PAIRS) as i:
                add_output_bias(i)

            pool.wait_ge(s["top_sel"], 2)
            nc.gpsimd.partition_all_reduce(allred[:, 0], pick_v[:, :], P, bass.bass_isa.ReduceOp.max).then_inc(s["allmax"], 1)
            pool.wait_ge(s["wexp"], 2)
            nc.gpsimd.partition_all_reduce(allred[:, 1], pexp[:, :], P, bass.bass_isa.ReduceOp.add).then_inc(s["allmax"], 1)

            def gather(e, n):
                nc.gpsimd.tensor_copy(idx_c[:, n, :], idx[:, bass.ds(e, 1)]).then_inc(s["idx_copied"], 1)
                hold(pool, s["idx_copied"], e + 1, s["pool_passed"])
                nc.gpsimd.indirect_dma_start(
                    out=xg[:, n], out_offset=None, in_=x1_dram,
                    in_offset=bass.IndirectOffsetOnAxis(ap=idx_c[:, n, :], axis=0)).then_inc(gathered[n], 16)

            def scatter(e, n, more):
                nc.gpsimd.tensor_copy(idx_s[:, n, :], idx[:, bass.ds(e, 1)]).then_inc(s["idx_kept"], 1)
                hold(pool, s["idx_kept"], e + 1, s["pool_passed"])
                hold(pool, s["y2_scaled"], e + 1, s["pool_passed"])
                hold(pool, s["scattered"], 16 * e, s["pool_passed"])
                nc.gpsimd.indirect_dma_start(
                    out=acc_dram, out_offset=bass.IndirectOffsetOnAxis(ap=idx_s[:, n, :], axis=0),
                    in_=y_sb[:, n % 2], in_offset=None, compute_op=ALU.add).then_inc(s["scattered"], 16)
                if more:
                    gather(e + NBUF, n)

            pool.wait_ge(s["top_sel"], 4)
            for u in range(2):
                pool.wait_ge(x1_stored[u], 16 * PAIRS)
            for n in range(NBUF):
                gather(n, n)
            pool.wait_ge(s["acc_copied"], 16)
            with pool.Fori(0, E // NBUF - 1) as i:
                for n in range(NBUF):
                    scatter(NBUF * i + n, n, True)
            for n in range(NBUF):
                scatter(E - NBUF + n, n, False)

        @block.scalar
        def _(act):
            for j in range(4):
                act.sem_inc(split_stored[j], 48)
            for b in range(B):
                with act.Fori(0, 2) as i:
                    for u in range(2):
                        n = 2 * i + u + 4 * b
                        for it in range(DT):
                            act.wait_ge(s["xT_ready"], 2 * n + it + 1)
                            nc.scalar.copy(xT[:, u, it], ps[:, it, :]).then_inc(s["xT_copied"], 1)
                        for j in range(4):
                            t = 4 * n + j
                            act.wait_ge(s["q32_done"], QFREE + t + 1)
                            act.wait_ge(split_stored[j], 48 + 48 * n)
                            nc.scalar.copy(parts[:, j, 0], q32[:, j % 2]).then_inc(s["s1_done"], 1)
                            act.wait_ge(s["rest_done"], t + 1)
                            nc.scalar.copy(parts[:, j, 1], rest[:, j % 2]).then_inc(s["s2_done"], 1)

            def exps(g, qb):
                for kt in range(4 * (qb + 1)):
                    step = GROUP_STEPS * g + SCORE_STEPS[qb] + kt
                    q0 = max(0, kt - 4 * qb) * P
                    for half in range(2):
                        act.wait_ge(s["s_ready"], 2 * step + half + 1)
                        if half == 0:
                            wait(act, s["pv_done"], step - 1)
                        nc.scalar.activation(probs[:, kt % 2, half, :, q0:QB],
                                             ps[:, 2 * half:2 * half + 2, q0:QB], ACT.Exp).then_inc(s["exp_done"], 1)

            def group(g):
                for qb in range(NQB):
                    exps(g, qb)

            group(0)
            with act.Fori(0, 3) as i:
                group(1 + 2 * i)
                group(2 + 2 * i)
            group(7)

            def turn_attended(i):
                for u in range(2):
                    act.wait_ge(s["at_turned"], 2 * i + u + 1)
                    nc.scalar.copy(atT[:, u], ps[:, u, :]).then_inc(s["at_copied"], 1)

            def turn_x1(i):
                for u in range(2):
                    act.wait_ge(s["x1_turned"], 2 * i + u + 1)
                    nc.scalar.copy(x1T[:, u], ps[:, 4 + u, :]).then_inc(s["x1_copied"], 1)

            def root(i):
                act.wait_ge(s["var_done"], i + 1)
                nc.scalar.activation(std[:, :], var[:, :], ACT.Sqrt).then_inc(s["std_done"], 1)

            def keep_logits(i):
                for u in range(2):
                    act.wait_ge(s["lg_ready"], 2 * i + u + 1)
                    nc.scalar.copy(logits[64 * u:64 * u + E, bass.ds(i * PAIR, PAIR)],
                                   ps[64 * u:64 * u + E, 6 + u, 0:PAIR]).then_inc(s["lg_copied"], 1)

            turn_attended(0)
            root(0)
            with act.Fori(1, PAIRS) as i:
                turn_attended(i)
                turn_x1(i - 1)
                root(i)
                keep_logits(i - 1)
            turn_x1(PAIRS - 1)
            keep_logits(PAIRS - 1)

            act.wait_ge(s["wexp"], 1)
            nc.scalar.activation(pexp[:, :], pick_d[:, :], ACT.Exp).then_inc(s["wexp"], 1)

            def gelus(e, n):
                for j in range(2 * S):
                    if j % 4 == 0:
                        act.wait_ge(s["h_ready"], 2 * e + j // 4 + 1)
                    if j == 0:
                        act.wait_ge(s["small_copied"], e + 1)
                    nc.scalar.activation(hid[:, n % 2, j, :], ps[:, 2 + 2 * (n % 2) + j // 4, (j % 4) * P:(j % 4 + 1) * P],
                                         ACT.Gelu, bias=b1_c[:, n, j:j + 1]).then_inc(s["gelu_done"], 1)

            with act.Fori(0, E // NBUF) as i:
                for n in range(NBUF):
                    gelus(NBUF * i + n, n)

            for c in range(CHUNKS):
                act.wait_ge(s["fin_var"], c + 1)
                nc.scalar.activation(fstd[:, c % 2], fvar[:, c % 2], ACT.Sqrt).then_inc(s["fin_std"], 1)

        @block.vector
        def _(dve):
            V = nc.vector
            V.memset(v_st[:, :].rearrange("p u g t h e -> p (u g t h e)"), 0.0).then_inc(s["v_cleared"], 1)
            dve.wait_ge(s["v_cleared"], 1)
            V.memset(v_st[:, :].rearrange("p u g t h e -> p (u g t h) e")[:, :, DK:DK + 1], 1.0
                     ).then_inc(s["v_cleared"], 1)
            for n in range(4):
                dve.wait_ge(turned, n + 1)
                dst = WT[:, n] if n < 3 else WOT
                V.tensor_copy(dst[:, :, :].rearrange("p t o -> p (t o)"), ps[:, n, :]).then_inc(turned_copied, 1)
            dve.wait_ge(turned, 5)
            V.tensor_copy(WrT[:, :, :].rearrange("p t e -> p (t e)"), ps[:, 4, 0:DT * E]).then_inc(turned_copied, 1)
            dve.wait_ge(turned, 6)
            V.tensor_copy(b1T[:, :].rearrange("p (n j) -> p j n", j=2),
                          ps[:, 5, 0:E * S * 2].rearrange("p (j n) -> p j n", j=2)).then_inc(turned_copied, 1)
            dve.wait_ge(turned, 7)
            V.tensor_copy(tabT[:, :], ps[0:H, 6, :]).then_inc(s["bias_step"], 1)
            V.memset(wide[:, :], 0.0).then_inc(s["bias_step"], 1)
            dve.wait_ge(s["bias_step"], 2)
            V.tensor_scalar(wide[:, P:P + MAXLEN], tabT[:, :], tabT[:, MAXLEN - 1:MAXLEN], None, ALU.subtract
                            ).then_inc(s["bias_step"], 1)
            dve.wait_ge(s["bias_step"], 3)
            V.tensor_copy(wide_h[:, 0, :], wide[:, 0:768]).then_inc(s["bias_step"], 1)
            dve.wait_ge(s["bias_step"], 4)
            V.tensor_tensor(wide_h[:, 1, :], wide[:, 0:768], wide_h[:, 0, :], ALU.subtract).then_inc(s["bias_step"], 1)
            dve.wait_ge(s["bias_step"], 5)
            V.memset(wide[:, 0:P], NEG).then_inc(s["bias_step"], 1)
            V.memset(wide_h[:, 0, 0:P], MASKED).then_inc(s["bias_step"], 1)
            V.memset(wide_h[:, 1, 0:P], 0.0).then_inc(s["bias_step"], 1)

            dve.wait_ge(s["loaded_b2"], 16)
            V.tensor_copy(b2_parts[:, 0, :], b2_nat[:, :]).then_inc(s["b2_step"], 1)
            dve.wait_ge(s["b2_step"], 1)
            V.tensor_tensor(b2_rest[:, :], b2_nat[:, :], b2_parts[:, 0, :], ALU.subtract).then_inc(s["b2_step"], 1)
            dve.wait_ge(s["b2_step"], 2)
            V.tensor_copy(b2_parts[:, 1, :], b2_rest[:, :]).then_inc(s["b2_step"], 1)
            dve.wait_ge(s["b2_step"], 3)
            V.tensor_tensor(b2_parts[:, 2, :], b2_rest[:, :], b2_parts[:, 1, :], ALU.subtract
                            ).then_inc(s["b2_step"], 1)

            dve.wait_ge(loaded_w, 16 * 10)
            dve.wait_ge(s["v_cleared"], 2)
            dve.sem_inc(s["q32_done"], QFREE)
            dve.sem_inc(s["v_copied"], VFREE)
            dve.sem_inc(s["s3_done"], RFREE)
            for u in range(2):
                dve.sem_inc(v_stored[u], 16)
            for b in range(B):
                with dve.Fori(0, 2) as i:
                    for u in range(2):
                        n = 2 * i + u + 4 * b
                        for j in range(4):
                            t = 4 * n + j
                            slot = j % 2
                            dve.wait_ge(s["qk_ready"], t + 1)
                            if j // 2 == 0:
                                V.tensor_scalar(q32[:, slot], ps[:, 2 + j, :], bqk[:, j:j + 1], DK ** -0.5,
                                                ALU.add, ALU.mult).then_inc(s["q32_done"], 1)
                            else:
                                V.tensor_scalar(q32[:, slot], ps[:, 2 + j, :], bqk[:, j:j + 1], None,
                                                ALU.add).then_inc(s["q32_done"], 1)
                            dve.wait_ge(s["s1_done"], t + 1)
                            dve.wait_ge(s["s3_done"], RFREE + t - 1)
                            V.tensor_tensor(rest[:, slot], q32[:, slot], parts[:, j, 0], ALU.subtract
                                            ).then_inc(s["rest_done"], 1)
                        for tt in range(4):
                            if tt % 2 == 0:
                                dve.wait_ge(s["v_ready"], 2 * n + tt // 2 + 1)
                            if tt == 0:
                                dve.wait_ge(v_stored[u], 16 + 16 * (i + 2 * b))
                            V.tensor_tensor(v_st[:, u, :, tt, :, 0:DK],
                                            ps[:, 6 + tt // 2, (tt % 2) * D:(tt % 2 + 1) * D].rearrange(
                                                "p (g h d) -> p g h d", g=4, h=HG),
                                            bV_b[:, :].rearrange("p (g h d) -> p g h d", g=4, h=HG),
                                            ALU.add).then_inc(s["v_copied"], 1)

            def maxima(g, p, qb, kt):
                i_, c = divmod(kt, qb + 1)
                i = 4 * qb + i_
                lo = max(0, i - 4 * c - 3)
                width = (i - 4 * c - lo + 1) * P
                for h in range(HG):
                    a = 4 * (GROUP_STEPS * g + SCORE_STEPS[qb] + kt) + h
                    if c <= 1:
                        hold(dve, s["max_ready"], a + 1, s["dve_passed"])
                    else:
                        dve.wait_ge(s["max_ready"], a + 1)
                    dst = mpart[:, qb % 2, h, i_, c:c + 1]
                    if c <= 1:
                        col = (i + 1) * P - lo * P - width
                        V.tensor_tensor_reduce(out=dump[:, h % 2, 0:width], in0=ps[:, 4 + h % 2, 0:width],
                                               in1=bq_sb[:, p, h, col:col + width][:, ::-1], scale=1.0, scalar=NEG,
                                               op0=ALU.add, op1=ALU.max, accum_out=dst).then_inc(s["max_done"], 1)
                    else:
                        V.reduce_max(dst, ps[:, 4 + h % 2, 0:width], AX.X).then_inc(s["max_done"], 1)

            def negate_max(g, qb):
                unit = NQB * g + qb
                wait(dve, s["msplit"], 4 * unit)
                dve.wait_ge(s["max_done"], 4 * (GROUP_STEPS * g + SCORE_STEPS[qb] + 4 * (qb + 1)))
                V.tensor_reduce(negm[:, :], mpart[:, qb % 2, :, :, 0:qb + 1].rearrange("p h i c -> p (h i) c"),
                                AX.X, ALU.max, negate=True).then_inc(s["negmax_done"], 1)

            def finish_rows(g, qb):
                unit = NQB * g + qb
                dve.wait_ge(s["m_turned"], unit + 1)
                wait(dve, s["mrow_stored"], 16 * unit)
                V.tensor_copy(m_rows[:, :], ps[:, 7, :].bitcast(BF16)[0:48, 0:P]).then_inc(s["m_copied"], 1)

            def take_output(g, qb):
                dve.wait_ge(s["pv_done"], GROUP_STEPS * g + SCORE_STEPS[qb] + 4 * (qb + 1))
                V.tensor_copy(o_sb[:, :], ps[:, 6, :]).then_inc(s["o_copied"], 1)

            def normalise(g, qb):
                unit = NQB * g + qb
                dve.wait_ge(s["o_turned"], unit + 1)
                o4 = ps[:, 7, :].rearrange("p (n e) -> p n e", e=32)
                V.reciprocal(recip[:, :].rearrange("p (n e) -> p n e", e=1), o4[:, :, DK:DK + 1]
                             ).then_inc(s["recip_done"], 1)
                wait(dve, att_stored[qb % 2], 16 * (2 * g + qb // 2))
                dve.wait_ge(s["recip_done"], unit + 1)
                V.tensor_tensor(att[:, qb % 2].rearrange("p i (h d) -> p (i h) d", h=HG), o4[:, :, 0:DK],
                                recip[:, :].rearrange("p (n e) -> p n e", e=1).to_broadcast([P, 16, DK]),
                                ALU.mult).then_inc(s["att_done"], 1)

            def unit_dve(gB, gA, pA, qb, prevB, prevA):
                if gA is not None and qb == 0:
                    dve.wait_ge(biasq_loaded[pA], 8 * (gA - pA) + 16)
                for kt in range(4 * (qb + 1)):
                    if gA is not None:
                        maxima(gA, pA, qb, kt)
                    if kt == 0 and prevB is not None:
                        take_output(*prevB)
                    if kt == 0 and prevA is not None:
                        finish_rows(*prevA)
                    if kt == 1 and prevB is not None:
                        normalise(*prevB)
                if gA is not None:
                    negate_max(gA, qb)

            def schedule(unit_of, g):
                gB, pB = g
                gA = 0 if gB is None else gB + 1
                pA = 0 if gB is None else 1 - pB
                if isinstance(gB, int) and gB == GROUPS - 1:
                    gA = None
                for qb in range(NQB):
                    if gB is None:
                        prevB, prevA = None, (gA, qb - 1) if qb else None
                    else:
                        prevA = (gB, NQB - 1) if qb == 0 else (gB + 1, qb - 1) if gA is not None else None
                        prevB = (gB, qb - 1) if qb else None if isinstance(gB, int) and gB == 0 else (gB - 1, NQB - 1)
                    unit_of(gB, pB, gA, pA, qb, prevB, prevA)

            def du(gB, pB, gA, pA, qb, prevB, prevA):
                unit_dve(gB, gA, pA, qb, prevB, prevA)

            schedule(du, (None, None))
            schedule(du, (0, 0))
            with dve.Fori(0, 3) as i:
                schedule(du, (1 + 2 * i, 1))
                schedule(du, (2 + 2 * i, 0))
            schedule(du, (7, 1))
            take_output(7, 3)
            normalise(7, 3)

            V.memset(logits[:, :], 0.0).then_inc(s["lg_copied"], 1)

            def norm1(i):
                wait(dve, s["x1_done"], 2 * i)
                for u in range(2):
                    dve.wait_ge(s["y_ready"], 2 * i + u + 1)
                    dve.wait_ge(s["xb_done"], 2 * i + u + 1)
                    V.tensor_tensor(res[:, u], ps[:, 2 + u, :].rearrange("p (v n) -> p v n", v=2), xb[:, u], ALU.add
                                    ).then_inc(s["res_done"], 1)
                for u in range(2):
                    dve.wait_ge(s["res_done"], 2 * i + u + 1)
                    for v in range(2):
                        V.bn_stats(stats[:, 2 * u + v], res[:, u, v]).then_inc(s["ln_stats"], 1)
                hold(dve, s["ln_stats"], 4 * i + 4, s["dve_passed"])
                for uv in range(4):
                    V.bn_aggr(mv[:, uv], stats[:, uv]).then_inc(s["ln_aggr"], 1)
                dve.wait_ge(s["ln_aggr"], 4 * i + 4)
                V.tensor_scalar(var[:, :], mv[:, :, 1], EPS, None, ALU.add).then_inc(s["var_done"], 1)
                dve.wait_ge(s["std_done"], i + 1)
                V.reciprocal(rstd[:, :], std[:, :]).then_inc(s["ln_rstd"], 1)
                dve.wait_ge(s["ln_rstd"], i + 1)
                for u in range(2):
                    if not (isinstance(i, int) and i == 0):
                        dve.wait_ge(x1_stored[u], 16 * i)
                        dve.wait_ge(s["x1_turned"], 2 * i + u - 1)
                    for v in range(2):
                        last = V.tensor_scalar(x1[:, u, v], res[:, u, v], mv[:, 2 * u + v, 0:1],
                                               rstd[:, 2 * u + v:2 * u + v + 1], ALU.subtract, ALU.mult)
                    last.then_inc(s["x1_done"], 1)

            norm1(0)
            with dve.Fori(1, PAIRS) as i:
                norm1(i)

            dve.wait_ge(s["lg_copied"], 2 * PAIRS + 1)
            lg = logits[0:64 + E, :]
            cnt = 0
            for r in range(CAP // 8):
                tv, ti = top_v[0:64 + E, 8 * r:8 * r + 8], top_i[0:64 + E, 8 * r:8 * r + 8]
                V.max(tv, lg).then_inc(s["top_step"], 1)
                cnt += 1
                dve.wait_ge(s["top_step"], cnt)
                V.max_index(ti, tv, lg).then_inc(s["top_step"], 1)
                cnt += 1
                dve.wait_ge(s["top_step"], cnt)
                V.match_replace(lg, tv, lg, NEG).then_inc(s["top_step"], 1)
                cnt += 1
                dve.wait_ge(s["top_step"], cnt)
            V.tensor_copy(top_f[0:64 + E, :], top_i[0:64 + E, :]).then_inc(s["top_step"], 1)
            cnt += 1
            dve.wait_ge(s["top_step"], cnt)
            V.tensor_scalar(top_f[64:64 + E, :], top_f[64:64 + E, :], float(HALF), None, ALU.add
                            ).then_inc(s["top_conv"], 1)
            dve.wait_ge(s["top_moved"], 32)
            V.tensor_copy(rev[:, 0, :], up_v[:, 0, ::-1]).then_inc(s["top_step"], 1)
            V.tensor_copy(rev[:, 1, :], up_v[:, 1, ::-1]).then_inc(s["top_conv"], 1)
            dve.wait_ge(s["top_turned"], 1)
            V.tensor_copy(tr[:, :, :].rearrange("p n e -> p (n e)"), ps[:, 0, 0:4 * E]).then_inc(s["top_step"], 1)
            cnt += 2
            dve.wait_ge(s["top_step"], cnt)
            V.tensor_tensor(pick_m[:, :], tr[:, 0], tr[:, 2], ALU.is_ge).then_inc(s["top_sel"], 1)
            V.tensor_tensor(pick_v[:, :], tr[:, 0], tr[:, 2], ALU.max).then_inc(s["top_sel"], 1)
            V.tensor_tensor(pick_i[:, :], tr[:, 1], tr[:, 3], ALU.subtract).then_inc(s["top_step"], 1)
            cnt += 1
            dve.wait_ge(s["top_step"], cnt)
            dve.wait_ge(s["top_sel"], 2)
            V.tensor_tensor(pick_d[:, :], pick_i[:, :], pick_m[:, :], ALU.mult).then_inc(s["top_step"], 1)
            cnt += 1
            dve.wait_ge(s["top_step"], cnt)
            V.tensor_tensor(pick_i[:, :], pick_d[:, :], tr[:, 3], ALU.add).then_inc(s["top_step"], 1)
            cnt += 1
            dve.wait_ge(s["top_step"], cnt)
            V.tensor_copy(idx[:, :], pick_i[:, :]).then_inc(s["top_sel"], 2)
            dve.wait_ge(s["allmax"], 1)
            V.tensor_tensor(pick_d[:, :], pick_v[:, :], allred[:, 0], ALU.subtract).then_inc(s["wexp"], 1)
            dve.wait_ge(s["allmax"], 2)
            V.reciprocal(pick_m[:, :], allred[:, 1]).then_inc(s["top_step"], 1)
            cnt += 1
            dve.wait_ge(s["top_step"], cnt)
            V.tensor_tensor(gate[:, :], pexp[:, :], pick_m[:, :], ALU.mult).then_inc(s["top_step"], 1)
            cnt += 1
            dve.wait_ge(s["top_step"], cnt)

            def small(e, n):
                wait(dve, s["y2_scaled"], e - NBUF + 1)
                V.tensor_copy(b1_c[:, n], b1T[:, bass.ds(e * 2 * S, 2 * S)])
                V.tensor_copy(gate_c[:, n], gate[:, bass.ds(e, 1)]).then_inc(s["small_copied"], 1)

            def turn_tokens(e, n):
                dve.wait_ge(s["xg_turned"], e + 1)
                V.tensor_copy(xgT[:, n % 2].rearrange("p t c -> p (t c)"), ps[:, 0, 0:2 * P]
                              ).then_inc(s["xg_copied"], 1)

            def scale_y(e, n):
                dve.wait_ge(s["y2_ready"], e + 1)
                dve.wait_ge(s["small_copied"], e + 1)
                if not (isinstance(e, int) and e < 2):
                    dve.wait_ge(s["scattered"], 16 * (e - 1))
                V.tensor_scalar(y_sb[:, n % 2], ps[:, 6 + n % 2, 0:D], gate_c[:, n], None, ALU.mult
                                ).then_inc(s["y2_scaled"], 1)

            small(0, 0)
            turn_tokens(0, 0)
            for n in range(NBUF):
                small(n + 1, (n + 1) % NBUF)
                turn_tokens(n + 1, (n + 1) % NBUF)
                if n > 0:
                    scale_y(n - 1, n - 1)
            with dve.Fori(1, E // NBUF - 1) as i:
                for n in range(NBUF):
                    e = NBUF * i + n
                    small(e + 1, (n + 1) % NBUF)
                    turn_tokens(e + 1, (n + 1) % NBUF)
                    scale_y(e - 1, (n - 1) % NBUF)
            for n in range(NBUF):
                e = E - NBUF + n
                if e + 1 < E:
                    small(e + 1, (n + 1) % NBUF)
                    turn_tokens(e + 1, (n + 1) % NBUF)
                scale_y(e - 1, (n - 1) % NBUF)
            scale_y(E - 1, NBUF - 1)

            def fin_stats(c):
                wait(dve, s["fin_done"], c - 1)
                dve.wait_ge(acc_loaded[c % FBUF], 16 * (c // FBUF) + 16)
                for v in range(FT):
                    V.bn_stats(fstats[:, c % 2, v], fin_in[:, c % FBUF, v]).then_inc(s["fin_bn"], 1)
                for v in range(FT):
                    dve.wait_ge(s["fin_bn"], FT * c + v + 1)
                    V.bn_aggr(fmv[:, c % 2, v], fstats[:, c % 2, v]).then_inc(s["fin_aggr"], 1)
                dve.wait_ge(s["fin_aggr"], FT * c + FT)
                V.tensor_scalar(fvar[:, c % 2], fmv[:, c % 2, :, 1], EPS, None, ALU.add).then_inc(s["fin_var"], 1)

            def fin_norm(c):
                dve.wait_ge(s["fin_std"], c + 1)
                V.reciprocal(frstd[:, c % 2], fstd[:, c % 2]).then_inc(s["fin_rstd"], 1)
                dve.wait_ge(s["fin_rstd"], c + 1)
                wait(dve, s["fin_stored"], 16 * (c - FBUF + 1))
                for v in range(FT):
                    last = V.tensor_scalar(fin_out[:, c % FBUF, v], fin_in[:, c % FBUF, v], fmv[:, c % 2, v, 0:1],
                                           frstd[:, c % 2, v:v + 1], ALU.subtract, ALU.mult)
                last.then_inc(s["fin_done"], 1)

            fin_stats(0)
            for c in range(CHUNKS):
                if c + 1 < CHUNKS:
                    fin_stats(c + 1)
                fin_norm(c)

        @block.tensor
        def _(pe):
            mm, tp = nc.tensor.matmul, nc.tensor.transpose
            pe.wait_ge(zeroed, 2)
            pe.wait_ge(consts, 3)
            pe.wait_ge(loaded_w, 16 * 10)
            for n in range(4):
                for it in range(DT):
                    for ot in range(DT):
                        last = tp(ps[:, n, it * D + ot * P:it * D + (ot + 1) * P],
                                  w_nat[:, n, ot, it * P:(it + 1) * P], ident[:, :])
                last.then_inc(turned, 1)
            for it in range(DT):
                last = tp(ps[:, 4, it * E:(it + 1) * E], wr_nat[:, it * P:(it + 1) * P], ident[0:E, 0:E])
            last.then_inc(turned, 1)
            pe.wait_ge(s["loaded_b1"], 16)
            for j in range(2):
                for r in range(2):
                    last = tp(ps[:, 5, (2 * j + r) * 96:(2 * j + r + 1) * 96], b1_nat[:, r, j::2], ident[0:96, 0:96])
            last.then_inc(turned, 1)
            for r in range(4):
                last = tp(ps[0:H, 6, r * P:(r + 1) * P], tab_nat[:, r, :], ident[:, :])
            last.then_inc(turned, 1)
            pe.wait_ge(turned_copied, 6)
            pe.wait_ge(s["bias_step"], 1)

            for b in range(B):
                with pe.Fori(0, 2) as i:
                    for u in range(2):
                        n = 2 * i + u + 4 * b
                        pe.wait_ge(x_loaded[u], 16 * (i + 2 * b) + 16)
                        for it in range(DT):
                            for a in range(4):
                                last = tp(ps[:, it, a * P:(a + 1) * P], x_sb[:, u, a, it * P:(it + 1) * P], ident[:, :])
                            last.then_inc(s["xT_ready"], 1)
                        pe.wait_ge(s["xT_copied"], 2 * n + 2)
                        for j in range(4):
                            pe.wait_ge(s["q32_done"], QFREE + 4 * (n - 1) + j + 1)
                            for it in range(DT):
                                last = mm(ps[:, 2 + j, :], lhsT=WT[:, j // 2, it, (j % 2) * P:(j % 2 + 1) * P],
                                          rhs=xT[:, u, it, :], start=it == 0, stop=it == DT - 1)
                            last.then_inc(s["qk_ready"], 1)
                        for vb in range(2):
                            pe.wait_ge(s["v_copied"], VFREE + 4 * (n - 1) + 2 * vb + 2)
                            for tt in (2 * vb, 2 * vb + 1):
                                for it in range(DT):
                                    last = mm(ps[:, 6 + vb, (tt % 2) * D:(tt % 2 + 1) * D],
                                              lhsT=xT[:, u, it, tt * P:(tt + 1) * P], rhs=WT[:, 2, it, :],
                                              start=it == 0, stop=it == DT - 1)
                            last.then_inc(s["v_ready"], 1)

            def scores(g, p, qb, kt, half):
                step = GROUP_STEPS * g + SCORE_STEPS[qb] + kt
                q0 = max(0, kt - 4 * qb) * P
                c0 = max(0, 4 * qb - kt) * P
                band = min(QB - q0, BAND - c0)
                wait(pe, s["exp_done"], 2 * step + half - 1)
                for hh in range(2):
                    h = 2 * half + hh
                    last = mm(ps[:, h, q0:QB], lhsT=Ks[p][0:ROWS + MROWS, h, kt * P:(kt + 1) * P],
                              rhs=Qs[p][0:ROWS + MROWS, h, qb * QB + q0:(qb + 1) * QB], start=True, stop=band <= 0)
                    if band > 0:
                        for half_keys in range(2):
                            k0 = 64 * (1 - half_keys)
                            last = mm(ps[k0:k0 + 64, h, q0:q0 + band], lhsT=flip[:, :],
                                      rhs=bk_sb[:, p, h, half_keys, c0:c0 + band], start=False, stop=True)
                last.then_inc(s["s_ready"], 1)

            def max_scores(g, p, qb, kt, heads):
                i_, c = divmod(kt, qb + 1)
                i = 4 * qb + i_
                lo, hi = max(0, i - 4 * c - 3), i - 4 * c + 1
                for h in heads:
                    a = 4 * (GROUP_STEPS * g + SCORE_STEPS[qb] + kt) + h
                    wait(pe, s["max_done"], a - 1)
                    mm(ps[:, 4 + h % 2, 0:(hi - lo) * P], lhsT=Qs[p][0:ROWS, h, i * P:(i + 1) * P],
                       rhs=Ks[p][0:ROWS, h, lo * P:hi * P], start=True, stop=True).then_inc(s["max_ready"], 1)

            def values(g, p, qb, kt):
                step = GROUP_STEPS * g + SCORE_STEPS[qb] + kt
                q0 = max(0, kt - 4 * qb) * P
                if kt == 0:
                    wait(pe, s["o_copied"], NQB * g + qb)
                pe.wait_ge(s["exp_done"], 2 * step + 2)
                for h in range(HG):
                    last = mm(ps[32 * h:32 * h + 32, 6, q0:QB], lhsT=Vs[:, p, kt, h, :],
                              rhs=probs[:, kt % 2, h // 2, h % 2, q0:QB], start=kt == 0, stop=kt == 4 * qb + 3)
                last.then_inc(s["pv_done"], 1)

            def turn_max(g, qb):
                unit = NQB * g + qb
                wait(pe, s["m_copied"], unit)
                wait(pe, s["att_done"], unit - NQB)
                hold(pe, s["msplit"], 4 * unit + 4, s["pe_passed"])
                tp(ps[:, 7, :].bitcast(BF16)[0:48, 0:P], m_parts[:, :, :].rearrange("p s n -> p (s n)"),
                   identb[:, :]).then_inc(s["m_turned"], 1)

            def turn_output(g, qb, has_max):
                unit = NQB * g + qb
                pe.wait_ge(s["o_copied"], unit + 1)
                wait(pe, s["att_done"], unit)
                if has_max:
                    pe.wait_ge(s["m_copied"], unit + NQB + 1)
                for i_ in range(4):
                    last = tp(ps[:, 7, i_ * P:(i_ + 1) * P], o_sb[:, i_ * P:(i_ + 1) * P], ident[:, :])
                last.then_inc(s["o_turned"], 1)

            def unit_pe(gB, pB, gA, pA, qb, prevB, prevA):
                if gA is not None:
                    pe.wait_ge(qk_loaded[pA][qb], 16 * (gA - pA) + 32)
                if gB is not None:
                    pe.wait_ge(mrow_loaded[qb], 16 * gB + 16)
                    if qb == 0:
                        pe.wait_ge(group_loaded[pB], 40 * (gB - pB) + 80)
                for kt in range(4 * (qb + 1)):
                    if gB is not None:
                        scores(gB, pB, qb, kt, 0)
                    if gA is not None:
                        max_scores(gA, pA, qb, kt, (0,))
                    if gB is not None:
                        scores(gB, pB, qb, kt, 1)
                    if gA is not None:
                        max_scores(gA, pA, qb, kt, (1,))
                    if kt == 0 and prevB is not None:
                        gP, qP = prevB
                        values(gP, pB if qb else 1 - pB, qP, 4 * qP + 3)
                    if gB is not None and kt > 0:
                        values(gB, pB, qb, kt - 1)
                    if gA is not None:
                        max_scores(gA, pA, qb, kt, (2, 3))
                    if kt == 0 and prevA is not None:
                        turn_max(*prevA)
                    if kt == 1 and prevB is not None:
                        turn_output(*prevB, prevA is not None)

            def schedule(g):
                gB, pB = g
                gA = 0 if gB is None else gB + 1
                pA = 0 if gB is None else 1 - pB
                if isinstance(gB, int) and gB == GROUPS - 1:
                    gA = None
                for qb in range(NQB):
                    if gB is None:
                        prevB, prevA = None, (gA, qb - 1) if qb else None
                    else:
                        prevA = (gB, NQB - 1) if qb == 0 else (gB + 1, qb - 1) if gA is not None else None
                        prevB = (gB, qb - 1) if qb else None if isinstance(gB, int) and gB == 0 else (gB - 1, NQB - 1)
                    unit_pe(gB, pB, gA, pA, qb, prevB, prevA)

            pe.wait_ge(s["v_copied"], VFREE + 32)
            schedule((None, None))
            schedule((0, 0))
            with pe.Fori(0, 3) as i:
                schedule((1 + 2 * i, 1))
                schedule((2 + 2 * i, 0))
            schedule((7, 1))
            values(7, 1, 3, 15)
            turn_output(7, 3, False)

            def attended(i):
                for u in range(2):
                    pe.wait_ge(at_loaded[u], 16 * i + 16)
                    for it in range(DT):
                        for v in range(2):
                            last = tp(ps[:, u, it * PAIR + v * P:it * PAIR + (v + 1) * P],
                                      at_in[:, u, v, it * P:(it + 1) * P], ident[:, :])
                    last.then_inc(s["at_turned"], 1)

            def project_out(i):
                for u in range(2):
                    pe.wait_ge(s["at_copied"], 2 * i + u + 1)
                    wait(pe, s["res_done"], 2 * (i - 1) + u + 1)
                    for v in range(2):
                        for it in range(DT):
                            last = mm(ps[:, 2 + u, v * D:(v + 1) * D], lhsT=atT[:, u, it, v * P:(v + 1) * P],
                                      rhs=WOT[:, it, :], start=it == 0, stop=it == DT - 1)
                    last.then_inc(s["y_ready"], 1)

            def turn_x1(i):
                for u in range(2):
                    pe.wait_ge(s["x1_done"], 2 * i + u + 1)
                    for it in range(DT):
                        for v in range(2):
                            last = tp(ps[:, 4 + u, it * PAIR + v * P:it * PAIR + (v + 1) * P],
                                      x1[:, u, v, it * P:(it + 1) * P], ident[:, :])
                    last.then_inc(s["x1_turned"], 1)

            def route(i):
                for u in range(2):
                    pe.wait_ge(s["x1_copied"], 2 * i + u + 1)
                    if not (isinstance(i, int) and i == 0):
                        pe.wait_ge(s["lg_copied"], 2 * i + u)
                    for it in range(DT):
                        last = mm(ps[64 * u:64 * u + E, 6 + u, 0:PAIR], lhsT=WrT[:, it, :], rhs=x1T[:, u, it, :],
                                  start=it == 0, stop=it == DT - 1)
                    last.then_inc(s["lg_ready"], 1)

            pe.wait_ge(s["att_done"], 32)
            attended(0)
            project_out(0)
            with pe.Fori(1, PAIRS) as i:
                attended(i)
                project_out(i)
                turn_x1(i - 1)
                route(i - 1)
            turn_x1(PAIRS - 1)
            route(PAIRS - 1)

            pe.wait_ge(s["top_conv"], 2)
            pe.wait_ge(s["lg_copied"], 2 * PAIRS + 1)
            for n, src in enumerate((top_v[0:E, :], top_f[0:E, :], rev[:, 0, :], rev[:, 1, :])):
                last = tp(ps[:, 0, n * E:(n + 1) * E], src, ident[0:E, 0:E])
            last.then_inc(s["top_turned"], 1)
            pe.wait_ge(s["top_sel"], 1)

            def turn_tokens(e, n):
                pe.wait_ge(gathered[n], 4 * (e - n) + 16)
                if not (isinstance(e, int) and e == 0):
                    pe.wait_ge(s["xg_copied"], e)
                for it in range(DT):
                    last = tp(ps[:, 0, it * P:(it + 1) * P], xg[:, n, it * P:(it + 1) * P], ident[:, :])
                last.then_inc(s["xg_turned"], 1)

            def hidden(e, n):
                pe.wait_ge(w_loaded[n], WLOADS * 4 * (e - n) + WLOADS * 16)
                pe.wait_ge(s["xg_copied"], e + 1)
                for sl in range(S):
                    for j in range(2):
                        m = 2 * sl + j
                        for it in range(DT):
                            last = mm(ps[:, 2 + 2 * (n % 2) + m // 4, (m % 4) * P:(m % 4 + 1) * P],
                                      lhsT=w1_sb[:, n, sl, it, :].rearrange("p (c j) -> p c j", j=2)[:, :, j],
                                      rhs=xgT[:, n % 2, it, :], start=it == 0, stop=it == DT - 1)
                    if sl % 2 == 1:
                        last.then_inc(s["h_ready"], 1)

            def outputs(e, n):
                bank = ps[:, 6 + n % 2, 0:D]
                if not (isinstance(e, int) and e < 2):
                    pe.wait_ge(s["y2_scaled"], e - 1)
                mm(bank, lhsT=ones_rows[:, :], rhs=b2_sb[:, n, :], start=True, stop=True)
                for sl in range(S):
                    for j in range(2):
                        pe.wait_ge(s["gelu_done"], 8 * e + 2 * sl + j + 1)
                        last = mm(bank[:, sl * KO:(sl + 1) * KO], lhsT=hid[:, n % 2, 2 * sl + j, :],
                                  rhs=w2_sb[:, n, sl, j * KO:(j + 1) * KO], start=False,
                                  stop=j == 1, skip_group_check=True)
                last.then_inc(s["y2_ready"], 1)

            turn_tokens(0, 0)
            for n in range(NBUF):
                hidden(n, n)
                turn_tokens(n + 1, (n + 1) % NBUF)
                if n > 0:
                    outputs(n - 1, n - 1)
            with pe.Fori(1, E // NBUF - 1) as i:
                for n in range(NBUF):
                    e = NBUF * i + n
                    hidden(e, n)
                    turn_tokens(e + 1, (n + 1) % NBUF)
                    outputs(e - 1, (n - 1) % NBUF)
            for n in range(NBUF):
                e = E - NBUF + n
                hidden(e, n)
                if e + 1 < E:
                    turn_tokens(e + 1, (n + 1) % NBUF)
                outputs(e - 1, (n - 1) % NBUF)
            outputs(E - 1, NBUF - 1)


_INS = ["L0_attn_x", "L0_attn_WQ", "L0_attn_bQ", "L0_attn_WK", "L0_attn_bK", "L0_attn_WV", "L0_attn_bV",
        "L0_attn_WO", "L0_attn_bO", "L0_attn_rel_pos_table", "L0_ffn_Wr", "L0_ffn_W1", "L0_ffn_b1",
        "L0_ffn_W2", "L0_ffn_b2"]


def kernel(**inputs):
    import numpy as np
    import concourse.bacc as bacc
    from concourse.bass_utils import run_bass_kernel_spmd

    nc = bacc.Bacc("TRN2", target_bir_lowering=False, num_devices=1)
    arrays, args = {}, []
    for name in _INS:
        a = np.ascontiguousarray(inputs[name])
        arrays[name] = a
        args.append(nc.dram_tensor(name, a.shape, mybir.dt.from_np(a.dtype), kind="ExternalInput").ap())
    result = nc.dram_tensor("result", (B, T, D), F32, kind="ExternalOutput").ap()
    moe_layer(nc, *args, result)
    r = run_bass_kernel_spmd(nc, [arrays], core_ids=[0])
    return r.results[0]["result"]
```

```python
import concourse.bass as bass
from concourse import mybir
from contextlib import ExitStack

F32 = mybir.dt.float32
BF16 = mybir.dt.bfloat16
F16 = mybir.dt.float16
U32 = mybir.dt.uint32
ALU = mybir.AluOpType
ACT = mybir.ActivationFunctionType
AX = mybir.AxisListType

P = 128
B, T, D = 2, 2048, 256
H, DK = 16, 16
NT = B * T
TILES = NT // P
DT = D // P
MAXLEN = 512
E, S, M = 48, 4, 256
KO = D // S
CAP = int(1.5 * NT / E)
EPS = 1e-5

HG = 4
GROUPS = B * H // HG
QB = 512
NQB = T // QB
KT = T // P
SPLIT_Q = (0, 0, 0, 1, 1, 2)
SPLIT_K = (0, 1, 2, 0, 1, 0)
C = len(SPLIT_Q)
ROWS = C * DK
MROWS = 3
BAND = 5 * P
MASKED = -60000.0
NEG = -1.0e30
WLEN = 1152
HALF = NT // 2
NBUF = 4
WLOADS = S + 1
PAIR = 2 * P
PAIRS = T // PAIR
FBUF, FT = 4, 4
CHUNKS = TILES // FT
QFREE, VFREE, RFREE = 4, 4, 2
SCORE_STEPS = [0, 4, 12, 24]
GROUP_STEPS = 40


def wait(eng, sem, count):
    if isinstance(count, int) and count <= 0:
        return
    eng.wait_ge(sem, count)


def hold(eng, sem, count, passed):
    if isinstance(count, int) and count <= 0:
        return
    eng.wait_ge(sem, count)
    if not isinstance(count, int):
        eng.sem_inc(passed, 1)


def max_chunk(qb, kt):
    return (kt % 4, kt // 4) if kt < 4 * qb else (4 * qb + 3 - kt, qb)


def ring_places(first_rows, rows, first_out, out, has_max, shift):
    order = []
    for qb in range(NQB):
        for kt in range(4 * (qb + 1)):
            if has_max:
                order += [(qb, kt, h) for h in range(HG)]
            if kt == 0 and (rows if qb else first_rows):
                order.append(("rows", qb))
            if kt == 1 and (out if qb else first_out):
                order.append(("out", qb))
    return {key: ((r + shift) % 3, order[r - 3] if r >= 3 else 3 - r) for r, key in enumerate(order)}


BEFORE = ring_places(False, True, False, False, True, 0)
FIRST = ring_places(True, True, False, True, True, len(BEFORE))
STEADY = ring_places(True, True, True, True, True, 0)
LAST = ring_places(True, False, True, True, False, 0)
assert (len(BEFORE) + len(FIRST)) % 3 == 0 and len(STEADY) % 3 == 0
RING = (4, 5, 7)


def places_of(g):
    if not isinstance(g, int):
        return STEADY
    return {-1: BEFORE, 0: FIRST, GROUPS - 1: LAST}.get(g, STEADY)


def moe_layer(nc, x, WQ, bQ, WK, bK, WV, bV, WO, bO, table, Wr, W1, b1, W2, b2, out):
    ctx = ExitStack()
    with ctx:
        def sb_in(stack):
            return lambda name, shape, dt: stack.enter_context(nc.sbuf_tensor(name, shape, dt))

        def sem(name):
            return ctx.enter_context(nc.semaphore(name))

        def dram(name, shape, dt):
            return nc.dram_tensor(name, shape, dt, kind="Internal").ap()

        sb = sb_in(ctx)

        q_dram = dram("q_split", [B * H, DK, C, T], BF16)
        k_dram = dram("k_split", [B * H, DK, C, T], BF16)
        v_dram = dram("v_groups", [GROUPS, P, KT * HG * 32], F32)
        m_dram = dram("row_max", [GROUPS * NQB, MROWS * HG * 4, P], BF16)
        bias_dram = dram("bias_parts", [H, 2, 768], F16)
        biasw_dram = dram("bias_wide", [H, WLEN], F32)
        att_dram = dram("attended", [B, T, D], F32)
        x1_dram = dram("normed", [NT, D], F32)
        acc_dram = dram("summed", [NT, D], F32)

        bias_by_key = bass.AP(bias_dram.tensor, 1, [[2 * 768, H], [1, P // 2], [768, 2], [64, 2], [1, BAND]])
        bias_by_query = bass.AP(biasw_dram.tensor, 1, [[WLEN, H], [1, P], [1, 1024]])

        ps = ctx.enter_context(nc.psum_tensor("banks", [P, 8, 512], F32))

        ident = sb("ident", [P, P], F32)
        identb = sb("identb", [P, P], BF16)
        flip = sb("flip", [P, P // 2], F16)
        WOT = sb("WOT", [P, DT, D], F32)
        WrT = sb("WrT", [P, DT, E], F32)
        bO_b = sb("bO_b", [P, D], F32)
        b1T = sb("b1T", [P, E * S * 2], F32)
        b2T = sb("b2T", [P, E * 2], F32)

        names = """dve_passed pool_passed pe_passed
            loaded_w loaded_b1 loaded_b2 zeroed consts v_cleared turned turned_copied bias_step bias_stored
            x_loaded0 x_loaded1 xT_ready xT_copied qk_ready q32_done s1_done rest_done s2_done s3_done
            v_ready v_copied v_stored0 v_stored1 pads
            biasq_loaded0 biasq_loaded1 group_loaded0 group_loaded1 mrow_stored
            s_ready exp_done max_ready max_done negmax_done msplit m_turned m_copied
            pv_done o_copied o_turned recip_done att_done att_stored0 att_stored1
            at_loaded0 at_loaded1 xr_loaded0 xr_loaded1 at_turned at_copied y_ready std_done x1_done
            x1_stored0 x1_stored1 acc_copied x1_turned x1_copied lg_ready lg_copied xb_done
            res_done ln_stats ln_aggr ln_rstd var_done
            top_step top_moved top_conv top_turned top_sel allmax wexp
            w_loaded0 w_loaded1 w_loaded2 w_loaded3 idx_copied idx_kept gathered0 gathered1 gathered2 gathered3 small_copied
            xg_turned xg_copied h_ready gelu_done yT_ready yT_copied y2_ready y2_scaled scattered
            acc_loaded0 acc_loaded1 acc_loaded2 acc_loaded3 fin_bn fin_aggr fin_var fin_rstd fin_std fin_done fin_stored""".split()
        s = {n: sem(n) for n in names}

        loaded_w, zeroed, consts = s["loaded_w"], s["zeroed"], s["consts"]
        turned, turned_copied = s["turned"], s["turned_copied"]
        x_loaded = [s["x_loaded0"], s["x_loaded1"]]
        split_stored = [sem(f"split_stored{j}") for j in range(4)]
        v_stored = [s["v_stored0"], s["v_stored1"]]
        qk_loaded = [[sem(f"qk_loaded{p}{c}") for c in range(4)] for p in range(2)]
        mrow_loaded = [sem(f"mrow_loaded{qb}") for qb in range(NQB)]
        biasq_loaded = [s["biasq_loaded0"], s["biasq_loaded1"]]
        group_loaded = [s["group_loaded0"], s["group_loaded1"]]
        att_stored = [s["att_stored0"], s["att_stored1"]]
        at_loaded = [s["at_loaded0"], s["at_loaded1"]]
        xr_loaded = [s["xr_loaded0"], s["xr_loaded1"]]
        x1_stored = [s["x1_stored0"], s["x1_stored1"]]
        w_loaded = [s[f"w_loaded{n}"] for n in range(NBUF)]
        gathered = [s[f"gathered{n}"] for n in range(NBUF)]
        acc_loaded = [s[f"acc_loaded{n}"] for n in range(FBUF)]

        with ExitStack() as st:
            sp_ = sb_in(st)
            w_nat = sp_("w_nat", [P, 4, DT, D], F32)
            wr_nat = sp_("wr_nat", [E, D], F32)
            b2_nat = sp_("b2_nat", [E, D], F32)
            b1_nat = sp_("b1_nat", [96, 2, M], F32)
            tab_nat = sp_("tab_nat", [P, 4, H], F32)
            WT = sp_("WT", [P, 3, DT, D], F32)
            bqk = sp_("bqk", [P, 4], F32)
            bV_b = sp_("bV_b", [P, D], F32)
            tabT = sp_("tabT", [H, MAXLEN], F32)
            wide = sp_("wide", [H, WLEN], F32)
            wide_h = sp_("wide_h", [H, 2, 768], F16)
            x_sb = sp_("x_sb", [P, 2, 4, D], F32)
            xT = sp_("xT", [P, 2, DT, QB], F32)
            q32 = sp_("q32", [P, 2, QB], F32)
            rest = sp_("rest", [P, 2, QB], F32)
            parts = sp_("parts", [P, 4, 3, QB], BF16)
            v_st = sp_("v_st", [P, 2, 4, 4, HG, 32], F32)

        w1_sb = sb("w1_sb", [P, NBUF, S, DT, M], F32)
        w2_sb = sb("w2_sb", [P, NBUF, S, 2 * KO], F32)

        with ExitStack() as st:
            sa = sb_in(st)
            Q1 = sa("Q1", [P, HG, T], BF16)
            K1 = sa("K1", [P, HG, T], BF16)
            probs = sa("probs", [P, 2, 2, 2, QB], F32)
            o_sb = sa("o_sb", [P, QB], F32)
            recip = sa("recip", [P, 16], F32)
            att = sa("att", [P, 2, 4, HG * DK], F32)
            Q0 = sa("Q0", [P, HG, T], BF16)
            K0 = sa("K0", [P, HG, T], BF16)
            Qs, Ks = (Q0, Q1), (K0, K1)
            dump = sa("dump", [P, 3, QB], F32)
            mpart = sa("mpart", [P, 2, HG, 4, 4], F32)
            negm = sa("negm", [P, HG * 4], F32)
            negm_rest = sa("negm_rest", [P, HG * 4], F32)
            m_parts = sa("m_parts", [P, MROWS, HG * 4], BF16)
            m_rows = sa("m_rows", [MROWS * HG * 4, P], BF16)
            bq_sb = sa("bq_sb", [P, 2, HG, 1024], F32)
            bk_sb = sa("bk_sb", [P, 2, HG, 2, BAND], F16)
            Vs = sa("Vs", [P, 2, KT, HG, 32], F32)

        st = ctx.enter_context(ExitStack())
        sc = sb_in(st)
        at_in = sc("at_in", [P, 2, 2, D], F32)
        xr = sc("xr", [P, 2, 2, D], F32)
        xb = sc("xb", [P, 2, 2, D], F32)
        atT = sc("atT", [P, 2, DT, PAIR], F32)
        res = sc("res", [P, 2, 2, D], F32)
        x1 = sc("x1", [P, 2, 2, D], F32)
        x1T = sc("x1T", [P, 2, DT, PAIR], F32)
        stats = sc("stats", [P, 4, 6], F32)
        mv = sc("mv", [P, 4, 2], F32)
        var = sc("var", [P, 4], F32)
        std = sc("std", [P, 4], F32)
        rstd = sc("rstd", [P, 4], F32)
        logits = sc("logits", [P, HALF], F32)
        top_v = sc("top_v", [P, P], F32)
        top_i = sc("top_i", [P, P], U32)
        top_f = sc("top_f", [P, P], F32)
        up_v = sc("up_v", [E, 2, P], F32)
        rev = sc("rev", [E, 2, P], F32)
        tr = sc("tr", [P, 4, E], F32)
        pick_m = sc("pick_m", [P, E], F32)
        pick_v = sc("pick_v", [P, E], F32)
        pick_d = sc("pick_d", [P, E], F32)
        pick_i = sc("pick_i", [P, E], F32)
        idx = sc("idx", [P, E], U32)
        allred = sc("allred", [P, 2, E], F32)
        pexp = sc("pexp", [P, E], F32)
        gate = sc("gate", [P, E], F32)
        idx_c = sc("idx_c", [P, NBUF, 1], U32)
        idx_s = sc("idx_s", [P, NBUF, 1], U32)
        xg = sc("xg", [P, NBUF, D], F32)
        xgT = sc("xgT", [P, 2, DT, P], F32)
        hid = sc("hid", [P, 2, 2 * S, P], F32)
        b1_c = sc("b1_c", [P, NBUF, 2 * S], F32)
        b2_c = sc("b2_c", [P, NBUF, 2], F32)
        yT = sc("yT", [P, 2, 2, P], F32)
        gate_c = sc("gate_c", [P, NBUF, 1], F32)
        y_sb = sc("y_sb", [P, 2, D], F32)
        fin_in = sc("fin_in", [P, FBUF, FT, D], F32)
        fin_out = sc("fin_out", [P, FBUF, FT, D], F32)
        fstats = sc("fstats", [P, 2, FT, 6], F32)
        fmv = sc("fmv", [P, 2, FT, 2], F32)
        fvar = sc("fvar", [P, 2, FT], F32)
        fstd = sc("fstd", [P, 2, FT], F32)
        frstd = sc("frstd", [P, 2, FT], F32)

        block = ctx.enter_context(nc.Block())

        def expert_load(sp, e, n):
            for sl in range(S):
                sp.dma_start(w1_sb[:, n, sl, :, :],
                             W1[bass.ds(e, 1), sl].rearrange("e (t p) m -> p (e t) m", p=P)).then_inc(w_loaded[n], 16)
            sp.dma_start(w2_sb[:, n, :, :],
                         W2[bass.ds(e, 1)].rearrange("e s (p j) k -> p (e s) (j k)", p=P)).then_inc(w_loaded[n], 16)
        @block.sync
        def _(sp):
            for n, w in enumerate((WQ, WK, WV, WO)):
                sp.dma_start(w_nat[:, n, :, :], w.rearrange("(t p) i -> p t i", p=P)).then_inc(loaded_w, 16)
            sp.dma_start(wr_nat[:, :], Wr).then_inc(loaded_w, 16)
            sp.dma_start(tab_nat[:, :, :],
                         table[MAXLEN - 1:2 * MAXLEN - 1, :].rearrange("(r p) h -> p r h", p=P)).then_inc(loaded_w, 16)
            sp.dma_start(b1_nat[:, :, :], b1.rearrange("e s m -> (e s) m").rearrange("(r p) m -> p r m", p=96)
                         ).then_inc(s["loaded_b1"], 16)
            sp.dma_start(b2_nat[:, :], b2.rearrange("e s k -> e (s k)")).then_inc(s["loaded_b2"], 16)
            with nc.allow_non_contiguous_dma(reason="two small bias vectors, one element to a partition"):
                for n, b in enumerate((bQ, bK)):
                    sp.dma_start(bqk[:, 2 * n:2 * n + 2], b.rearrange("(t p) -> p t", p=P)).then_inc(loaded_w, 16)
            for dst, b in ((bV_b, bV), (bO_b, bO)):
                sp.dma_start(dst[:, :], b.rearrange("(a n) -> a n", a=1).to_broadcast([P, D])).then_inc(loaded_w, 16)

            def load_x(n, u):
                sp.dma_start(x_sb[:, u], x.rearrange("b t d -> (b t) d")[bass.ds(n * QB, QB), :].rearrange(
                    "(a p) d -> p a d", p=P)).then_inc(x_loaded[u], 16)

            load_x(0, 0)
            load_x(1, 1)
            sp.wait_ge(s["bias_step"], 8)
            sp.dma_start(bias_dram[:, :, :], wide_h[:, :, :]).then_inc(s["bias_stored"], 16)
            sp.dma_start(biasw_dram[:, :], wide[:, :]).then_inc(s["bias_stored"], 16)

            def load_chunk(hg, p, c):
                for dst, src in ((Qs, q_dram), (Ks, k_dram)):
                    sp.dma_start(dst[p][0:ROWS, :, c * QB:(c + 1) * QB],
                                 src[bass.ds(p * H + hg * HG, HG), :, :, c * QB:(c + 1) * QB].rearrange(
                                     "h d c t -> (d c) h t")).then_inc(qk_loaded[p][c], 16)

            def load_bias_k(hg, p):
                for part in range(2):
                    for half in range(2):
                        sp.dma_start(bk_sb[64 * part:64 * part + 64, p, :, half, :],
                                     bias_by_key[bass.ds(hg * HG, HG), :, part, half, :].rearrange("h p c -> p h c")
                                     ).then_inc(group_loaded[p], 16)

            def load_values(hg, p):
                sp.dma_start(Vs[:, p].rearrange("p t h e -> p (t h e)"),
                             v_dram[bass.ds(p * 4 + hg, 1)].rearrange("g p n -> p (g n)")).then_inc(group_loaded[p], 16)

            def load_bias_q(hg, p):
                sp.dma_start(bq_sb[:, p, :, :], bias_by_query[bass.ds(hg * HG, HG)].rearrange("h p c -> p h c")
                             ).then_inc(biasq_loaded[p], 16)

            sp.wait_ge(s["bias_stored"], 32)
            load_bias_q(0, 0)

            def store_pair(i, b, load_more):
                for u in range(2):
                    n = 2 * i + u + 4 * b
                    t0 = (2 * i + u) * QB
                    for j in range(4):
                        sp.wait_ge(s["s3_done"], RFREE + 4 * n + j + 1)
                        dst = (q_dram, k_dram)[j // 2]
                        dst = dst[b * H + 8 * (j % 2):b * H + 8 * (j % 2) + 8, :, :, bass.ds(t0, QB)].rearrange(
                            "h d c t -> (h d) c t")
                        src = parts[:, j]
                        if j // 2 == 0:
                            runs = ((0, 3, src[:, 0:1].to_broadcast([P, 3, QB])),
                                    (3, 5, src[:, 1:2].to_broadcast([P, 2, QB])), (5, 6, src[:, 2:3]))
                        else:
                            runs = ((0, 3, src[:, 0:3]), (3, 5, src[:, 0:2]), (5, 6, src[:, 0:1]))
                        for c0, c1, part in runs:
                            sp.dma_start(dst[:, c0:c1, :], part).then_inc(split_stored[j], 16)
                    sp.wait_ge(s["v_copied"], VFREE + 4 * n + 4)
                    sp.dma_start(
                        v_dram[b * 4:b * 4 + 4, :, bass.ds((2 * i + u) * 4 * HG * 32, 4 * HG * 32)].rearrange(
                            "g p n -> p g n"),
                        v_st[:, u].rearrange("p g t h e -> p g (t h e)")).then_inc(v_stored[u], 16)
                    if load_more:
                        sp.wait_ge(s["xT_ready"], 2 * n + 2)
                        load_x(n + 2, u)

            with sp.Fori(0, 2) as i:
                store_pair(i, 0, True)
            store_pair(0, 1, True)
            for j in range(4):
                sp.wait_ge(split_stored[j], 48 + 48 * 5)
            sp.wait_ge(s["pads"], 1)
            for c in range(2):
                load_chunk(0, 0, c)
            store_pair(1, 1, False)
            for c in range(2, 4):
                load_chunk(0, 0, c)
            load_bias_k(0, 0)
            load_values(0, 0)
            for j in range(4):
                sp.wait_ge(split_stored[j], 48 + 48 * 8)
            for u in range(2):
                sp.wait_ge(v_stored[u], 16 + 16 * 4)
            sp.wait_ge(s["bias_stored"], 32)

            def max_rows(g, p, qb):
                unit = NQB * g + qb
                sp.wait_ge(s["m_copied"], unit + 1)
                sp.dma_start(m_dram[bass.ds(unit, 1)].rearrange("u r t -> (u r) t"),
                             m_rows[:, :]).then_inc(s["mrow_stored"], 16)
                sp.wait_ge(s["mrow_stored"], 16 * unit + 16)
                sp.dma_start(Qs[p][ROWS:ROWS + MROWS, :, qb * QB:(qb + 1) * QB],
                             m_dram[bass.ds(unit, 1)].rearrange("u (s h i) t -> (u s) h (i t)", s=MROWS, h=HG)
                             ).then_inc(mrow_loaded[qb], 16)

            def store_att(g, hg, p, qb):
                sp.wait_ge(s["att_done"], NQB * g + qb + 1)
                sp.dma_start(
                    att_dram[p, qb * QB:(qb + 1) * QB, bass.ds(hg * HG * DK, HG * DK)].rearrange(
                        "(i p) n -> p i n", p=P), att[:, qb % 2]).then_inc(att_stored[qb % 2], 16)

            def phase(g, hg, p):
                static = isinstance(g, int)
                has_before, has_next, has_two_on = not (static and g == 0), not (static and g == GROUPS - 1), \
                    not (static and g >= GROUPS - 2)
                next_hg = hg + p
                for qb in range(NQB):
                    if qb == 0:
                        max_rows(g, p, NQB - 1)
                        if has_before:
                            store_att(g - 1, hg - 1 + p, 1 - p, NQB - 1)
                            if has_next:
                                sp.wait_ge(s["pv_done"], GROUP_STEPS * g)
                                load_bias_k(next_hg, 1 - p)
                                load_values(next_hg, 1 - p)
                    else:
                        if has_next:
                            max_rows(g + 1, 1 - p, qb - 1)
                        store_att(g, hg, p, qb - 1)
                if has_two_on:
                    sp.wait_ge(s["negmax_done"], NQB * g + NQB)
                    load_bias_q(hg + 1, p)
                    for c in range(4):
                        sp.wait_ge(s["s_ready"], 2 * (GROUP_STEPS * g + SCORE_STEPS[3] + 4 * c + 4))
                        load_chunk(hg + 1, p, c)

            sp.wait_ge(s["pads"], 2)
            max_rows(0, 0, 0)
            for c in range(4):
                load_chunk(0, 1, c)
            load_bias_q(0, 1)
            max_rows(0, 0, 1)
            load_bias_k(0, 1)
            load_values(0, 1)
            for n in range(NBUF // 2):
                expert_load(sp, n, n)
            max_rows(0, 0, 2)
            for n in range(NBUF // 2, NBUF):
                expert_load(sp, n, n)
            phase(0, 0, 0)
            with sp.Fori(0, 2) as i:
                phase(1 + 2 * i, i, 1)
                phase(2 + 2 * i, i + 1, 0)
            phase(5, 2, 1)
            phase(6, 3, 0)
            phase(7, 3, 1)
            store_att(7, 3, 1, 3)

            for u in range(2):
                sp.wait_ge(att_stored[u], 16 * 16)

            def load_tokens(i, u):
                for dst, src, sm in ((at_in, att_dram, at_loaded[u]), (xr, x, xr_loaded[u])):
                    sp.dma_start(dst[:, u], src[u, bass.ds(i * PAIR, PAIR), :].rearrange("(v p) n -> p v n", p=P)
                                 ).then_inc(sm, 16)

            def store_x1(i, u):
                sp.wait_ge(s["x1_done"], 2 * i + u + 1)
                sp.dma_start(x1_dram[bass.ds(i * PAIR + u * T, PAIR), :].rearrange("(v p) n -> p v n", p=P),
                             x1[:, u]).then_inc(x1_stored[u], 16)

            def next_tokens(i):
                for u in range(2):
                    sp.wait_ge(s["at_turned"], 2 * (i - 1) + u + 1)
                    sp.wait_ge(s["xb_done"], 2 * (i - 1) + u + 1)
                    load_tokens(i, u)

            for u in range(2):
                load_tokens(0, u)
            next_tokens(1)
            with sp.Fori(0, PAIRS - 2) as i:
                next_tokens(i + 2)
                for u in range(2):
                    store_x1(i, u)
            for i in (PAIRS - 2, PAIRS - 1):
                for u in range(2):
                    store_x1(i, u)

            for u in range(2):
                sp.wait_ge(x1_stored[u], 16 * PAIRS)
            sp.dma_start(acc_dram[:, :], x1_dram[:, :]).then_inc(s["acc_copied"], 16)

            sp.wait_ge(s["top_conv"], 1)
            sp.dma_start(up_v[:, 0, :], top_v[64:64 + E, :]).then_inc(s["top_moved"], 16)
            sp.dma_start(up_v[:, 1, :], top_f[64:64 + E, :]).then_inc(s["top_moved"], 16)

            with sp.Fori(0, E // NBUF - 1) as i:
                for n in range(NBUF):
                    sp.wait_ge(s["yT_ready"], NBUF * i + n + 1)
                    expert_load(sp, NBUF * i + NBUF + n, n)

            def sum_rows(flat, c):
                return flat[bass.ds(c * FT * P, FT * P), :].rearrange("(v p) n -> p v n", p=P)

            out_flat = out.rearrange("b t d -> (b t) d")
            sp.wait_ge(s["scattered"], 16 * E)
            for n in range(FBUF):
                sp.dma_start(fin_in[:, n], sum_rows(acc_dram, n)).then_inc(acc_loaded[n], 16)
            for n in range(FBUF):
                sp.wait_ge(s["fin_done"], n + 1)
                sp.dma_start(sum_rows(out_flat, n), fin_out[:, n]).then_inc(s["fin_stored"], 16)
                sp.dma_start(fin_in[:, n], sum_rows(acc_dram, FBUF + n)).then_inc(acc_loaded[n], 16)
            for n in range(FBUF):
                sp.wait_ge(s["fin_done"], FBUF + n + 1)
                sp.dma_start(sum_rows(out_flat, FBUF + n), fin_out[:, n]).then_inc(s["fin_stored"], 16)
            sp.wait_ge(s["fin_stored"], 16 * CHUNKS)

        @block.gpsimd
        def _(pool):
            nc.gpsimd.memset(ident[:, :], 0.0).then_inc(zeroed, 1)
            pool.wait_ge(zeroed, 1)
            nc.gpsimd.affine_select(out=ident[:, :], in_=ident[:, :], compare_op=ALU.not_equal, fill=1.0,
                                    base=0, pattern=[[-1, P]], channel_multiplier=1).then_inc(zeroed, 1)
            pool.wait_ge(zeroed, 2)
            nc.gpsimd.tensor_copy(identb[:, :], ident[:, :]).then_inc(consts, 1)
            nc.gpsimd.tensor_tensor(flip[:, :], ident[:, P // 2 - 1::-1], ident[:, :P // 2 - 1:-1], ALU.add).then_inc(consts, 1)
            pool.wait_ge(consts, 2)
            nc.gpsimd.memset(K0[ROWS:P, :, :].rearrange("p h t -> p (h t)"), 1.0).then_inc(s["pads"], 1)

            pool.wait_ge(s["pads"], 1)

            for b in range(B):
                with pool.Fori(0, 2) as i:
                    for u in range(2):
                        for j in range(4):
                            t = 4 * (2 * i + u + 4 * b) + j
                            pool.wait_ge(s["s2_done"], t + 1)
                            nc.gpsimd.tensor_tensor(parts[:, j, 2], rest[:, j % 2], parts[:, j, 1],
                                                    ALU.subtract).then_inc(s["s3_done"], 1)

            def split_max(unit):
                step = 4 * unit
                wait(pool, s["m_turned"], unit)
                hold(pool, s["negmax_done"], unit + 1, s["pool_passed"])
                nc.gpsimd.tensor_copy(m_parts[:, 0], negm[:, :]).then_inc(s["msplit"], 1)
                pool.wait_ge(s["msplit"], step + 1)
                nc.gpsimd.tensor_tensor(negm_rest[:, :], negm[:, :], m_parts[:, 0], ALU.subtract
                                        ).then_inc(s["msplit"], 1)
                hold(pool, s["msplit"], step + 2, s["pool_passed"])
                nc.gpsimd.tensor_copy(m_parts[:, 1], negm_rest[:, :]).then_inc(s["msplit"], 1)
                pool.wait_ge(s["msplit"], step + 3)
                nc.gpsimd.tensor_tensor(m_parts[:, 2], negm_rest[:, :], m_parts[:, 1], ALU.subtract
                                        ).then_inc(s["msplit"], 1)

            split_max(0)
            pool.wait_ge(s["msplit"], 4)
            pool.wait_ge(s["s3_done"], RFREE + 32)
            for j in range(4):
                pool.wait_ge(split_stored[j], 48 + 48 * 8)
            for u in range(2):
                pool.wait_ge(v_stored[u], 16 + 16 * 4)
            pool.wait_ge(s["bias_stored"], 32)
            nc.gpsimd.memset(K1[ROWS:P, :, :].rearrange("p h t -> p (h t)"), 1.0).then_inc(s["pads"], 1)
            pool.wait_ge(s["pads"], 2)
            for unit in range(1, NQB):
                split_max(unit)
            with pool.Fori(NQB, NQB * GROUPS) as unit:
                split_max(unit)

            def add_output_bias(i):
                for u in range(2):
                    wait(pool, s["res_done"], 2 * (i - 1) + u + 1)
                    pool.wait_ge(xr_loaded[u], 16 * i + 16)
                    nc.gpsimd.tensor_tensor(xb[:, u], xr[:, u], bO_b[:, :].rearrange("p (a n) -> p a n", a=1
                                            ).to_broadcast([P, 2, D]), ALU.add).then_inc(s["xb_done"], 1)

            add_output_bias(0)
            with pool.Fori(1, PAIRS) as i:
                add_output_bias(i)

            pool.wait_ge(s["top_sel"], 2)
            nc.gpsimd.partition_all_reduce(allred[:, 0], pick_v[:, :], P, bass.bass_isa.ReduceOp.max).then_inc(s["allmax"], 1)

            def gather(e, n):
                nc.gpsimd.tensor_copy(idx_c[:, n, :], idx[:, bass.ds(e, 1)]).then_inc(s["idx_copied"], 1)
                hold(pool, s["idx_copied"], e + 1, s["pool_passed"])
                nc.gpsimd.indirect_dma_start(
                    out=xg[:, n], out_offset=None, in_=x1_dram,
                    in_offset=bass.IndirectOffsetOnAxis(ap=idx_c[:, n, :], axis=0)).then_inc(gathered[n], 16)

            def scatter(e, n, more):
                nc.gpsimd.tensor_copy(idx_s[:, n, :], idx[:, bass.ds(e, 1)]).then_inc(s["idx_kept"], 1)
                if more:
                    hold(pool, s["xg_turned"], e + 1, s["pool_passed"])
                    gather(e + NBUF, n)
                hold(pool, s["idx_kept"], e + 1, s["pool_passed"])
                hold(pool, s["y2_scaled"], e + 1, s["pool_passed"])
                hold(pool, s["scattered"], 16 * e, s["pool_passed"])
                nc.gpsimd.indirect_dma_start(
                    out=acc_dram, out_offset=bass.IndirectOffsetOnAxis(ap=idx_s[:, n, :], axis=0),
                    in_=y_sb[:, n % 2], in_offset=None, compute_op=ALU.add).then_inc(s["scattered"], 16)

            pool.wait_ge(s["top_sel"], 4)
            for u in range(2):
                pool.wait_ge(x1_stored[u], 16 * PAIRS)
            gather(0, 0)
            pool.wait_ge(s["wexp"], 2)
            nc.gpsimd.partition_all_reduce(allred[:, 1], pexp[:, :], P, bass.bass_isa.ReduceOp.add).then_inc(s["allmax"], 1)
            for n in range(1, NBUF):
                gather(n, n)
            pool.wait_ge(s["acc_copied"], 16)
            for n in range(NBUF):
                scatter(n, n, True)
            with pool.Fori(1, E // NBUF - 1) as i:
                for n in range(NBUF):
                    scatter(NBUF * i + n, n, True)
            for n in range(NBUF):
                scatter(E - NBUF + n, n, False)

        @block.scalar
        def _(act):
            for j in range(4):
                act.sem_inc(split_stored[j], 48)
            for b in range(B):
                with act.Fori(0, 2) as i:
                    for u in range(2):
                        n = 2 * i + u + 4 * b
                        for it in range(DT):
                            act.wait_ge(s["xT_ready"], 2 * n + it + 1)
                            nc.scalar.copy(xT[:, u, it], ps[:, it, :]).then_inc(s["xT_copied"], 1)
                        for j in range(4):
                            t = 4 * n + j
                            act.wait_ge(s["q32_done"], QFREE + t + 1)
                            act.wait_ge(split_stored[j], 48 + 48 * n)
                            nc.scalar.copy(parts[:, j, 0], q32[:, j % 2]).then_inc(s["s1_done"], 1)
                            act.wait_ge(s["rest_done"], t + 1)
                            nc.scalar.copy(parts[:, j, 1], rest[:, j % 2]).then_inc(s["s2_done"], 1)

            def exps(g, qb):
                for kt in range(4 * (qb + 1)):
                    step = GROUP_STEPS * g + SCORE_STEPS[qb] + kt
                    q0 = max(0, kt - 4 * qb) * P
                    for half in range(2):
                        act.wait_ge(s["s_ready"], 2 * step + half + 1)
                        if half == 0:
                            wait(act, s["pv_done"], step - 1)
                        nc.scalar.activation(probs[:, kt % 2, half, :, q0:QB],
                                             ps[:, 2 * half:2 * half + 2, q0:QB], ACT.Exp).then_inc(s["exp_done"], 1)

            def group(g):
                for qb in range(NQB):
                    exps(g, qb)

            group(0)
            with act.Fori(0, 3) as i:
                group(1 + 2 * i)
                group(2 + 2 * i)
            group(7)

            def turn_attended(i):
                for u in range(2):
                    act.wait_ge(s["at_turned"], 2 * i + u + 1)
                    nc.scalar.copy(atT[:, u], ps[:, u, :]).then_inc(s["at_copied"], 1)

            def turn_x1(i):
                for u in range(2):
                    act.wait_ge(s["x1_turned"], 2 * i + u + 1)
                    nc.scalar.copy(x1T[:, u], ps[:, 4 + u, :]).then_inc(s["x1_copied"], 1)

            def root(i):
                act.wait_ge(s["var_done"], i + 1)
                nc.scalar.activation(std[:, :], var[:, :], ACT.Sqrt).then_inc(s["std_done"], 1)

            def keep_logits(i):
                for u in range(2):
                    act.wait_ge(s["lg_ready"], 2 * i + u + 1)
                    nc.scalar.copy(logits[64 * u:64 * u + E, bass.ds(i * PAIR, PAIR)],
                                   ps[64 * u:64 * u + E, 6 + u, 0:PAIR]).then_inc(s["lg_copied"], 1)

            turn_attended(0)
            turn_attended(1)
            root(0)
            with act.Fori(1, PAIRS - 1) as i:
                turn_x1(i - 1)
                turn_attended(i + 1)
                root(i)
                keep_logits(i - 1)
            turn_x1(PAIRS - 2)
            root(PAIRS - 1)
            keep_logits(PAIRS - 2)
            turn_x1(PAIRS - 1)
            keep_logits(PAIRS - 1)

            act.wait_ge(s["wexp"], 1)
            nc.scalar.activation(pexp[:, :], pick_d[:, :], ACT.Exp).then_inc(s["wexp"], 1)

            def gelus(e, n):
                for j in range(2 * S):
                    if j % 4 == 0:
                        act.wait_ge(s["h_ready"], 2 * e + j // 4 + 1)
                    if j == 0:
                        act.wait_ge(s["small_copied"], e + 1)
                    nc.scalar.activation(hid[:, n % 2, j, :], ps[:, 2 + 2 * (n % 2) + j // 4, (j % 4) * P:(j % 4 + 1) * P],
                                         ACT.Gelu, bias=b1_c[:, n, j:j + 1]).then_inc(s["gelu_done"], 1)

            with act.Fori(0, E // NBUF) as i:
                for n in range(NBUF):
                    gelus(NBUF * i + n, n)

            for c in range(CHUNKS):
                act.wait_ge(s["fin_var"], c + 1)
                nc.scalar.activation(fstd[:, c % 2], fvar[:, c % 2], ACT.Sqrt).then_inc(s["fin_std"], 1)

        @block.vector
        def _(dve):
            V = nc.vector
            dve.sem_inc(s["q32_done"], QFREE)
            dve.sem_inc(s["v_copied"], VFREE)
            dve.sem_inc(s["s3_done"], RFREE)
            for u in range(2):
                dve.sem_inc(v_stored[u], 16)
            V.memset(v_st[:, :].rearrange("p u g t h e -> p (u g t h e)"), 0.0).then_inc(s["v_cleared"], 1)
            dve.wait_ge(s["v_cleared"], 1)
            V.memset(v_st[:, :].rearrange("p u g t h e -> p (u g t h) e")[:, :, DK:DK + 1], 1.0
                     ).then_inc(s["v_cleared"], 1)
            for n in range(4):
                dve.wait_ge(turned, n + 1)
                dst = WT[:, n] if n < 3 else WOT
                V.tensor_copy(dst[:, :, :].rearrange("p t o -> p (t o)"), ps[:, n, :]).then_inc(turned_copied, 1)
            dve.wait_ge(turned, 5)
            V.tensor_copy(WrT[:, :, :].rearrange("p t e -> p (t e)"), ps[:, 4, 0:DT * E]).then_inc(turned_copied, 1)
            dve.wait_ge(turned, 6)
            V.tensor_copy(b1T[:, :].rearrange("p (n j) -> p j n", j=2),
                          ps[:, 5, 0:E * S * 2].rearrange("p (j n) -> p j n", j=2)).then_inc(turned_copied, 1)
            V.tensor_copy(b2T[:, :].rearrange("p (n h) -> p h n", h=2),
                          ps[:, 5, 4 * 96:4 * 96 + 2 * E].rearrange("p (h n) -> p h n", h=2)).then_inc(turned_copied, 1)
            dve.wait_ge(turned, 7)
            V.tensor_copy(tabT[:, :], ps[0:H, 6, :]).then_inc(s["bias_step"], 1)
            V.memset(wide[:, :], 0.0).then_inc(s["bias_step"], 1)
            dve.wait_ge(s["bias_step"], 2)
            V.tensor_scalar(wide[:, P:P + MAXLEN], tabT[:, :], tabT[:, MAXLEN - 1:MAXLEN], None, ALU.subtract
                            ).then_inc(s["bias_step"], 1)
            dve.wait_ge(s["bias_step"], 3)
            V.tensor_copy(wide_h[:, 0, :], wide[:, 0:768]).then_inc(s["bias_step"], 1)
            dve.wait_ge(s["bias_step"], 4)
            V.tensor_tensor(wide_h[:, 1, :], wide[:, 0:768], wide_h[:, 0, :], ALU.subtract).then_inc(s["bias_step"], 1)
            dve.wait_ge(s["bias_step"], 5)
            V.memset(wide[:, 0:P], NEG).then_inc(s["bias_step"], 1)
            V.memset(wide_h[:, 0, 0:P], MASKED).then_inc(s["bias_step"], 1)
            V.memset(wide_h[:, 1, 0:P], 0.0).then_inc(s["bias_step"], 1)

            dve.wait_ge(loaded_w, 16 * 10)
            dve.wait_ge(s["v_cleared"], 2)
            for b in range(B):
                with dve.Fori(0, 2) as i:
                    for u in range(2):
                        n = 2 * i + u + 4 * b
                        for j in range(4):
                            t = 4 * n + j
                            slot = j % 2
                            dve.wait_ge(s["qk_ready"], t + 1)
                            if j // 2 == 0:
                                V.tensor_scalar(q32[:, slot], ps[:, 2 + j, :], bqk[:, j:j + 1], DK ** -0.5,
                                                ALU.add, ALU.mult).then_inc(s["q32_done"], 1)
                            else:
                                V.tensor_scalar(q32[:, slot], ps[:, 2 + j, :], bqk[:, j:j + 1], None,
                                                ALU.add).then_inc(s["q32_done"], 1)
                            dve.wait_ge(s["s1_done"], t + 1)
                            dve.wait_ge(s["s3_done"], RFREE + t - 1)
                            V.tensor_tensor(rest[:, slot], q32[:, slot], parts[:, j, 0], ALU.subtract
                                            ).then_inc(s["rest_done"], 1)
                        for tt in range(4):
                            if tt % 2 == 0:
                                dve.wait_ge(s["v_ready"], 2 * n + tt // 2 + 1)
                            if tt == 0:
                                dve.wait_ge(v_stored[u], 16 + 16 * (i + 2 * b))
                            V.tensor_tensor(v_st[:, u, :, tt, :, 0:DK],
                                            ps[:, 6 + tt // 2, (tt % 2) * D:(tt % 2 + 1) * D].rearrange(
                                                "p (g h d) -> p g h d", g=4, h=HG),
                                            bV_b[:, :].rearrange("p (g h d) -> p g h d", g=4, h=HG),
                                            ALU.add).then_inc(s["v_copied"], 1)

            def ring_bank(g, key):
                return ps[:, RING[places_of(g)[key][0]], :]

            def maxima(g, p, qb, kt):
                i_, c = max_chunk(qb, kt)
                i = 4 * qb + i_
                lo = max(0, i - 4 * c - 3)
                width = (i - 4 * c - lo + 1) * P
                for h in range(HG):
                    a = 4 * (GROUP_STEPS * g + SCORE_STEPS[qb] + kt) + h
                    bank = ring_bank(g - 1, (qb, kt, h))
                    place = places_of(g - 1)[(qb, kt, h)][0]
                    if c <= 1:
                        hold(dve, s["max_ready"], a + 1, s["dve_passed"])
                    else:
                        dve.wait_ge(s["max_ready"], a + 1)
                    dst = mpart[:, qb % 2, h, i_, c:c + 1]
                    if c <= 1:
                        col = (i + 1) * P - lo * P - width
                        V.tensor_tensor_reduce(out=dump[:, place, 0:width], in0=bank[:, 0:width],
                                               in1=bq_sb[:, p, h, col:col + width][:, ::-1], scale=1.0, scalar=NEG,
                                               op0=ALU.add, op1=ALU.max, accum_out=dst).then_inc(s["max_done"], 1)
                    else:
                        V.reduce_max(dst, bank[:, 0:width], AX.X).then_inc(s["max_done"], 1)

            def negate_max(g, qb):
                unit = NQB * g + qb
                wait(dve, s["msplit"], 4 * unit)
                dve.wait_ge(s["max_done"], 4 * (GROUP_STEPS * g + SCORE_STEPS[qb] + 4 * (qb + 1)))
                V.tensor_reduce(negm[:, :], mpart[:, qb % 2, :, :, 0:qb + 1].rearrange("p h i c -> p (h i) c"),
                                AX.X, ALU.max, negate=True).then_inc(s["negmax_done"], 1)

            def finish_rows(g, qb, bank):
                unit = NQB * g + qb
                dve.wait_ge(s["m_turned"], unit + 1)
                wait(dve, s["mrow_stored"], 16 * unit)
                V.tensor_copy(m_rows[:, :], bank.bitcast(BF16)[0:48, 0:P]).then_inc(s["m_copied"], 1)

            def take_output(g, qb):
                dve.wait_ge(s["pv_done"], GROUP_STEPS * g + SCORE_STEPS[qb] + 4 * (qb + 1))
                V.tensor_copy(o_sb[:, :], ps[:, 6, :]).then_inc(s["o_copied"], 1)

            def normalise(g, qb, bank):
                unit = NQB * g + qb
                dve.wait_ge(s["o_turned"], unit + 1)
                o4 = bank.rearrange("p (n e) -> p n e", e=32)
                V.reciprocal(recip[:, :].rearrange("p (n e) -> p n e", e=1), o4[:, :, DK:DK + 1]
                             ).then_inc(s["recip_done"], 1)
                wait(dve, att_stored[qb % 2], 16 * (2 * g + qb // 2))
                dve.wait_ge(s["recip_done"], unit + 1)
                V.tensor_tensor(att[:, qb % 2].rearrange("p i (h d) -> p (i h) d", h=HG), o4[:, :, 0:DK],
                                recip[:, :].rearrange("p (n e) -> p n e", e=1).to_broadcast([P, 16, DK]),
                                ALU.mult).then_inc(s["att_done"], 1)

            def unit_dve(gB, gA, pA, qb, prevB, prevA):
                g = -1 if gB is None else gB
                if gA is not None and qb == 0:
                    dve.wait_ge(biasq_loaded[pA], 8 * (gA - pA) + 16)
                for kt in range(4 * (qb + 1)):
                    if gA is not None:
                        maxima(gA, pA, qb, kt)
                    if kt == 0 and prevB is not None:
                        take_output(*prevB)
                    if kt == 0 and prevA is not None:
                        finish_rows(*prevA, ring_bank(g, ("rows", qb)))
                    if kt == 1 and prevB is not None:
                        normalise(*prevB, ring_bank(g, ("out", qb)))
                if gA is not None:
                    negate_max(gA, qb)

            def schedule(unit_of, g):
                gB, pB = g
                gA = 0 if gB is None else gB + 1
                pA = 0 if gB is None else 1 - pB
                if isinstance(gB, int) and gB == GROUPS - 1:
                    gA = None
                for qb in range(NQB):
                    if gB is None:
                        prevB, prevA = None, (gA, qb - 1) if qb else None
                    else:
                        prevA = (gB, NQB - 1) if qb == 0 else (gB + 1, qb - 1) if gA is not None else None
                        prevB = (gB, qb - 1) if qb else None if isinstance(gB, int) and gB == 0 else (gB - 1, NQB - 1)
                    unit_of(gB, pB, gA, pA, qb, prevB, prevA)

            def du(gB, pB, gA, pA, qb, prevB, prevA):
                unit_dve(gB, gA, pA, qb, prevB, prevA)

            schedule(du, (None, None))
            schedule(du, (0, 0))
            with dve.Fori(0, 3) as i:
                schedule(du, (1 + 2 * i, 1))
                schedule(du, (2 + 2 * i, 0))
            schedule(du, (7, 1))
            take_output(7, 3)
            normalise(7, 3, ps[:, RING[len(LAST) % 3], :])

            V.memset(logits[:, :], 0.0).then_inc(s["lg_copied"], 1)

            def norm1(i):
                wait(dve, s["x1_done"], 2 * i)
                for u in range(2):
                    dve.wait_ge(s["y_ready"], 2 * i + u + 1)
                    dve.wait_ge(s["xb_done"], 2 * i + u + 1)
                    V.tensor_tensor(res[:, u], ps[:, 2 + u, :].rearrange("p (v n) -> p v n", v=2), xb[:, u], ALU.add
                                    ).then_inc(s["res_done"], 1)
                for u in range(2):
                    dve.wait_ge(s["res_done"], 2 * i + u + 1)
                    for v in range(2):
                        V.bn_stats(stats[:, 2 * u + v], res[:, u, v]).then_inc(s["ln_stats"], 1)
                hold(dve, s["ln_stats"], 4 * i + 4, s["dve_passed"])
                for uv in range(4):
                    V.bn_aggr(mv[:, uv], stats[:, uv]).then_inc(s["ln_aggr"], 1)
                dve.wait_ge(s["ln_aggr"], 4 * i + 4)
                V.tensor_scalar(var[:, :], mv[:, :, 1], EPS, None, ALU.add).then_inc(s["var_done"], 1)
                dve.wait_ge(s["std_done"], i + 1)
                V.reciprocal(rstd[:, :], std[:, :]).then_inc(s["ln_rstd"], 1)
                dve.wait_ge(s["ln_rstd"], i + 1)
                for u in range(2):
                    if not (isinstance(i, int) and i == 0):
                        dve.wait_ge(x1_stored[u], 16 * i)
                        dve.wait_ge(s["x1_turned"], 2 * i + u - 1)
                    for v in range(2):
                        last = V.tensor_scalar(x1[:, u, v], res[:, u, v], mv[:, 2 * u + v, 0:1],
                                               rstd[:, 2 * u + v:2 * u + v + 1], ALU.subtract, ALU.mult)
                    last.then_inc(s["x1_done"], 1)

            norm1(0)
            with dve.Fori(1, PAIRS) as i:
                norm1(i)

            dve.wait_ge(s["lg_copied"], 2 * PAIRS + 1)
            lg = logits[0:64 + E, :]
            cnt = 0
            for r in range(CAP // 8):
                tv, ti = top_v[0:64 + E, 8 * r:8 * r + 8], top_i[0:64 + E, 8 * r:8 * r + 8]
                V.max(tv, lg).then_inc(s["top_step"], 1)
                cnt += 1
                dve.wait_ge(s["top_step"], cnt)
                V.max_index(ti, tv, lg).then_inc(s["top_step"], 1)
                cnt += 1
                dve.wait_ge(s["top_step"], cnt)
                if r < CAP // 8 - 1:
                    V.match_replace(lg, tv, lg, NEG).then_inc(s["top_step"], 1)
                    cnt += 1
                    dve.wait_ge(s["top_step"], cnt)
            V.tensor_copy(top_f[0:64 + E, :], top_i[0:64 + E, :]).then_inc(s["top_step"], 1)
            cnt += 1
            dve.wait_ge(s["top_step"], cnt)
            V.tensor_scalar(top_f[64:64 + E, :], top_f[64:64 + E, :], float(HALF), None, ALU.add
                            ).then_inc(s["top_conv"], 1)
            dve.wait_ge(s["top_moved"], 32)
            V.tensor_copy(rev[:, 0, :], up_v[:, 0, ::-1]).then_inc(s["top_step"], 1)
            V.tensor_copy(rev[:, 1, :], up_v[:, 1, ::-1]).then_inc(s["top_conv"], 1)
            dve.wait_ge(s["top_turned"], 1)
            V.tensor_copy(tr[:, :, :].rearrange("p n e -> p (n e)"), ps[:, 0, 0:4 * E]).then_inc(s["top_step"], 1)
            cnt += 2
            dve.wait_ge(s["top_step"], cnt)
            V.tensor_tensor(pick_m[:, :], tr[:, 0], tr[:, 2], ALU.is_ge).then_inc(s["top_sel"], 1)
            V.tensor_tensor(pick_v[:, :], tr[:, 0], tr[:, 2], ALU.max).then_inc(s["top_sel"], 1)
            V.tensor_tensor(pick_i[:, :], tr[:, 1], tr[:, 3], ALU.subtract).then_inc(s["top_step"], 1)
            cnt += 1
            dve.wait_ge(s["top_step"], cnt)
            dve.wait_ge(s["top_sel"], 2)
            V.tensor_tensor(pick_d[:, :], pick_i[:, :], pick_m[:, :], ALU.mult).then_inc(s["top_step"], 1)
            cnt += 1
            dve.wait_ge(s["top_step"], cnt)
            V.tensor_tensor(pick_i[:, :], pick_d[:, :], tr[:, 3], ALU.add).then_inc(s["top_step"], 1)
            cnt += 1
            dve.wait_ge(s["top_step"], cnt)
            V.tensor_copy(idx[:, :], pick_i[:, :]).then_inc(s["top_sel"], 2)
            dve.wait_ge(s["allmax"], 1)
            V.tensor_tensor(pick_d[:, :], pick_v[:, :], allred[:, 0], ALU.subtract).then_inc(s["wexp"], 1)
            dve.wait_ge(s["allmax"], 2)
            V.reciprocal(pick_m[:, :], allred[:, 1]).then_inc(s["top_step"], 1)
            cnt += 1
            dve.wait_ge(s["top_step"], cnt)
            V.tensor_tensor(gate[:, :], pexp[:, :], pick_m[:, :], ALU.mult).then_inc(s["top_step"], 1)
            cnt += 1
            dve.wait_ge(s["top_step"], cnt)

            def small(e, n):
                wait(dve, s["y2_scaled"], e - NBUF + 1)
                V.tensor_copy(b1_c[:, n], b1T[:, bass.ds(e * 2 * S, 2 * S)])
                V.tensor_copy(b2_c[:, n], b2T[:, bass.ds(2 * e, 2)])
                V.tensor_copy(gate_c[:, n], gate[:, bass.ds(e, 1)]).then_inc(s["small_copied"], 1)

            def turn_tokens(e, n):
                dve.wait_ge(s["xg_turned"], e + 1)
                V.tensor_copy(xgT[:, n % 2].rearrange("p t c -> p (t c)"), ps[:, 0, 0:2 * P]
                              ).then_inc(s["xg_copied"], 1)

            def keep_yT(e, n):
                dve.wait_ge(s["yT_ready"], e + 1)
                dve.wait_ge(s["small_copied"], e + 1)
                wait(dve, s["y2_ready"], e - 1)
                for h in range(2):
                    last = V.tensor_scalar(yT[:, n % 2, h, :], ps[:, 1, h * P:(h + 1) * P], b2_c[:, n, h:h + 1], None,
                                           ALU.add)
                last.then_inc(s["yT_copied"], 1)

            def scale_y(e, n):
                dve.wait_ge(s["y2_ready"], e + 1)
                dve.wait_ge(s["small_copied"], e + 1)
                if not (isinstance(e, int) and e < 2):
                    dve.wait_ge(s["scattered"], 16 * (e - 1))
                V.tensor_scalar(y_sb[:, n % 2], ps[:, 6 + n % 2, 0:D], gate_c[:, n], None, ALU.mult
                                ).then_inc(s["y2_scaled"], 1)

            def step(e, n, static):
                if not (static and e + 1 >= E):
                    small(e + 1, (n + 1) % NBUF)
                    turn_tokens(e + 1, (n + 1) % NBUF)
                if not (static and e < 2):
                    scale_y(e - 2, (n - 2) % NBUF)
                if not (static and e < 1):
                    keep_yT(e - 1, (n - 1) % NBUF)

            small(0, 0)
            turn_tokens(0, 0)
            for n in range(NBUF):
                step(n, n, True)
            with dve.Fori(1, E // NBUF - 1) as i:
                for n in range(NBUF):
                    step(NBUF * i + n, n, False)
            for n in range(NBUF):
                step(E - NBUF + n, n, True)
            scale_y(E - 2, NBUF - 2)
            keep_yT(E - 1, NBUF - 1)
            scale_y(E - 1, NBUF - 1)

            def fin_stats(c):
                wait(dve, s["fin_done"], c - 1)
                dve.wait_ge(acc_loaded[c % FBUF], 16 * (c // FBUF) + 16)
                for v in range(FT):
                    V.bn_stats(fstats[:, c % 2, v], fin_in[:, c % FBUF, v]).then_inc(s["fin_bn"], 1)
                for v in range(FT):
                    dve.wait_ge(s["fin_bn"], FT * c + v + 1)
                    V.bn_aggr(fmv[:, c % 2, v], fstats[:, c % 2, v]).then_inc(s["fin_aggr"], 1)
                dve.wait_ge(s["fin_aggr"], FT * c + FT)
                V.tensor_scalar(fvar[:, c % 2], fmv[:, c % 2, :, 1], EPS, None, ALU.add).then_inc(s["fin_var"], 1)

            def fin_norm(c):
                dve.wait_ge(s["fin_std"], c + 1)
                V.reciprocal(frstd[:, c % 2], fstd[:, c % 2]).then_inc(s["fin_rstd"], 1)
                dve.wait_ge(s["fin_rstd"], c + 1)
                wait(dve, s["fin_stored"], 16 * (c - FBUF + 1))
                for v in range(FT):
                    last = V.tensor_scalar(fin_out[:, c % FBUF, v], fin_in[:, c % FBUF, v], fmv[:, c % 2, v, 0:1],
                                           frstd[:, c % 2, v:v + 1], ALU.subtract, ALU.mult)
                last.then_inc(s["fin_done"], 1)

            fin_stats(0)
            for c in range(CHUNKS):
                if c + 1 < CHUNKS:
                    fin_stats(c + 1)
                fin_norm(c)

        @block.tensor
        def _(pe):
            mm, tp = nc.tensor.matmul, nc.tensor.transpose
            pe.wait_ge(zeroed, 2)
            pe.wait_ge(consts, 2)
            pe.wait_ge(loaded_w, 16 * 10)
            for n in range(4):
                for it in range(DT):
                    for ot in range(DT):
                        last = tp(ps[:, n, it * D + ot * P:it * D + (ot + 1) * P],
                                  w_nat[:, n, ot, it * P:(it + 1) * P], ident[:, :])
                last.then_inc(turned, 1)
            for it in range(DT):
                last = tp(ps[:, 4, it * E:(it + 1) * E], wr_nat[:, it * P:(it + 1) * P], ident[0:E, 0:E])
            last.then_inc(turned, 1)
            pe.wait_ge(s["loaded_b1"], 16)
            for j in range(2):
                for r in range(2):
                    tp(ps[:, 5, (2 * j + r) * 96:(2 * j + r + 1) * 96], b1_nat[:, r, j::2], ident[0:96, 0:96])
            pe.wait_ge(s["loaded_b2"], 16)
            for h in range(2):
                last = tp(ps[:, 5, 4 * 96 + h * E:4 * 96 + (h + 1) * E], b2_nat[:, h * P:(h + 1) * P], ident[0:E, 0:E])
            last.then_inc(turned, 1)
            for r in range(4):
                last = tp(ps[0:H, 6, r * P:(r + 1) * P], tab_nat[:, r, :], ident[:, :])
            last.then_inc(turned, 1)
            pe.wait_ge(turned_copied, 7)
            pe.wait_ge(s["bias_step"], 1)

            for b in range(B):
                with pe.Fori(0, 2) as i:
                    for u in range(2):
                        n = 2 * i + u + 4 * b
                        pe.wait_ge(x_loaded[u], 16 * (i + 2 * b) + 16)
                        for it in range(DT):
                            for a in range(4):
                                last = tp(ps[:, it, a * P:(a + 1) * P], x_sb[:, u, a, it * P:(it + 1) * P], ident[:, :])
                            last.then_inc(s["xT_ready"], 1)
                        pe.wait_ge(s["xT_copied"], 2 * n + 2)
                        for j in range(4):
                            pe.wait_ge(s["q32_done"], QFREE + 4 * (n - 1) + j + 1)
                            for it in range(DT):
                                last = mm(ps[:, 2 + j, :], lhsT=WT[:, j // 2, it, (j % 2) * P:(j % 2 + 1) * P],
                                          rhs=xT[:, u, it, :], start=it == 0, stop=it == DT - 1)
                            last.then_inc(s["qk_ready"], 1)
                        for vb in range(2):
                            pe.wait_ge(s["v_copied"], VFREE + 4 * (n - 1) + 2 * vb + 2)
                            for tt in (2 * vb, 2 * vb + 1):
                                for it in range(DT):
                                    last = mm(ps[:, 6 + vb, (tt % 2) * D:(tt % 2 + 1) * D],
                                              lhsT=xT[:, u, it, tt * P:(tt + 1) * P], rhs=WT[:, 2, it, :],
                                              start=it == 0, stop=it == DT - 1)
                            last.then_inc(s["v_ready"], 1)

            def scores(g, p, qb, kt, half):
                step = GROUP_STEPS * g + SCORE_STEPS[qb] + kt
                q0 = max(0, kt - 4 * qb) * P
                c0 = max(0, 4 * qb - kt) * P
                band = min(QB - q0, BAND - c0)
                wait(pe, s["exp_done"], 2 * step + half - 1)
                for hh in range(2):
                    h = 2 * half + hh
                    last = mm(ps[:, h, q0:QB], lhsT=Ks[p][0:ROWS + MROWS, h, kt * P:(kt + 1) * P],
                              rhs=Qs[p][0:ROWS + MROWS, h, qb * QB + q0:(qb + 1) * QB], start=True, stop=band <= 0)
                    if band > 0:
                        for half_keys in range(2):
                            k0 = 64 * (1 - half_keys)
                            last = mm(ps[k0:k0 + 64, h, q0:q0 + band], lhsT=flip[:, :],
                                      rhs=bk_sb[:, p, h, half_keys, c0:c0 + band], start=False, stop=True)
                last.then_inc(s["s_ready"], 1)

            def ring_bank(g, key):
                place, before = places_of(g)[key]
                if isinstance(before, int):
                    wait(pe, s["max_done"], 4 * GROUP_STEPS * (g + 1) - before + 1)
                elif before[0] == "rows":
                    pe.wait_ge(s["m_copied"], NQB * g + before[1] + NQB)
                elif before[0] == "out":
                    pe.wait_ge(s["att_done"], NQB * g + before[1])
                else:
                    b_qb, b_kt, b_h = before
                    pe.wait_ge(s["max_done"], 4 * (GROUP_STEPS * (g + 1) + SCORE_STEPS[b_qb] + b_kt) + b_h + 1)
                return ps[:, RING[place], :]

            def max_scores(g, p, qb, kt, heads):
                i_, c = max_chunk(qb, kt)
                i = 4 * qb + i_
                lo, hi = max(0, i - 4 * c - 3), i - 4 * c + 1
                for h in heads:
                    mm(ring_bank(g - 1, (qb, kt, h))[:, 0:(hi - lo) * P], lhsT=Qs[p][0:ROWS, h, i * P:(i + 1) * P],
                       rhs=Ks[p][0:ROWS, h, lo * P:hi * P], start=True, stop=True).then_inc(s["max_ready"], 1)

            def values(g, p, qb, kt):
                step = GROUP_STEPS * g + SCORE_STEPS[qb] + kt
                q0 = max(0, kt - 4 * qb) * P
                if kt == 0:
                    wait(pe, s["o_copied"], NQB * g + qb)
                pe.wait_ge(s["exp_done"], 2 * step + 2)
                for h in range(HG):
                    last = mm(ps[32 * h:32 * h + 32, 6, q0:QB], lhsT=Vs[:, p, kt, h, :],
                              rhs=probs[:, kt % 2, h // 2, h % 2, q0:QB], start=kt == 0, stop=kt == 4 * qb + 3)
                last.then_inc(s["pv_done"], 1)

            def turn_max(g, qb, bank):
                hold(pe, s["msplit"], 4 * (NQB * g + qb) + 4, s["pe_passed"])
                tp(bank.bitcast(BF16)[0:48, 0:P], m_parts[:, :, :].rearrange("p s n -> p (s n)"),
                   identb[:, :]).then_inc(s["m_turned"], 1)

            def turn_output(g, qb, bank):
                pe.wait_ge(s["o_copied"], NQB * g + qb + 1)
                for i_ in range(4):
                    last = tp(bank[:, i_ * P:(i_ + 1) * P], o_sb[:, i_ * P:(i_ + 1) * P], ident[:, :])
                last.then_inc(s["o_turned"], 1)

            def unit_pe(gB, pB, gA, pA, qb, prevB, prevA):
                g = -1 if gB is None else gB
                if gA is not None:
                    pe.wait_ge(qk_loaded[pA][qb], 16 * (gA - pA) + 32)
                if gB is not None:
                    pe.wait_ge(mrow_loaded[qb], 16 * gB + 16)
                    if qb == 0:
                        pe.wait_ge(group_loaded[pB], 40 * (gB - pB) + 80)
                for kt in range(4 * (qb + 1)):
                    if gB is not None:
                        scores(gB, pB, qb, kt, 0)
                    if gA is not None:
                        max_scores(gA, pA, qb, kt, (0,))
                    if gB is not None:
                        scores(gB, pB, qb, kt, 1)
                    if gA is not None:
                        max_scores(gA, pA, qb, kt, (1,))
                    if kt == 0 and prevB is not None:
                        gP, qP = prevB
                        values(gP, pB if qb else 1 - pB, qP, 4 * qP + 3)
                    if gB is not None and kt > 0:
                        values(gB, pB, qb, kt - 1)
                    if gA is not None:
                        max_scores(gA, pA, qb, kt, (2, 3))
                    if kt == 0 and prevA is not None:
                        turn_max(*prevA, ring_bank(g, ("rows", qb)))
                    if kt == 1 and prevB is not None:
                        turn_output(*prevB, ring_bank(g, ("out", qb)))

            def schedule(g):
                gB, pB = g
                gA = 0 if gB is None else gB + 1
                pA = 0 if gB is None else 1 - pB
                if isinstance(gB, int) and gB == GROUPS - 1:
                    gA = None
                for qb in range(NQB):
                    if gB is None:
                        prevB, prevA = None, (gA, qb - 1) if qb else None
                    else:
                        prevA = (gB, NQB - 1) if qb == 0 else (gB + 1, qb - 1) if gA is not None else None
                        prevB = (gB, qb - 1) if qb else None if isinstance(gB, int) and gB == 0 else (gB - 1, NQB - 1)
                    unit_pe(gB, pB, gA, pA, qb, prevB, prevA)

            pe.wait_ge(s["v_copied"], VFREE + 32)
            schedule((None, None))
            schedule((0, 0))
            with pe.Fori(0, 3) as i:
                schedule((1 + 2 * i, 1))
                schedule((2 + 2 * i, 0))
            schedule((7, 1))
            values(7, 1, 3, 15)
            pe.wait_ge(s["att_done"], NQB * GROUPS - 1)
            turn_output(7, 3, ps[:, RING[len(LAST) % 3], :])

            def attended(i):
                for u in range(2):
                    pe.wait_ge(at_loaded[u], 16 * i + 16)
                    for it in range(DT):
                        for v in range(2):
                            last = tp(ps[:, u, it * PAIR + v * P:it * PAIR + (v + 1) * P],
                                      at_in[:, u, v, it * P:(it + 1) * P], ident[:, :])
                    last.then_inc(s["at_turned"], 1)

            def project_out(i):
                for u in range(2):
                    pe.wait_ge(s["at_copied"], 2 * i + u + 1)
                    wait(pe, s["res_done"], 2 * (i - 1) + u + 1)
                    for v in range(2):
                        for it in range(DT):
                            last = mm(ps[:, 2 + u, v * D:(v + 1) * D], lhsT=atT[:, u, it, v * P:(v + 1) * P],
                                      rhs=WOT[:, it, :], start=it == 0, stop=it == DT - 1)
                    last.then_inc(s["y_ready"], 1)

            def turn_x1(i):
                for u in range(2):
                    pe.wait_ge(s["x1_done"], 2 * i + u + 1)
                    for it in range(DT):
                        for v in range(2):
                            last = tp(ps[:, 4 + u, it * PAIR + v * P:it * PAIR + (v + 1) * P],
                                      x1[:, u, v, it * P:(it + 1) * P], ident[:, :])
                    last.then_inc(s["x1_turned"], 1)

            def route(i):
                pe.wait_ge(s["x1_copied"], 2 * i + 2)
                if not (isinstance(i, int) and i == 0):
                    pe.wait_ge(s["lg_copied"], 2 * i + 1)
                for it in range(DT):
                    for u in range(2):
                        last = mm(ps[64 * u:64 * u + E, 6 + u, 0:PAIR], lhsT=WrT[:, it, :], rhs=x1T[:, u, it, :],
                                  start=it == 0, stop=it == DT - 1)
                        if it == DT - 1:
                            last.then_inc(s["lg_ready"], 1)

            pe.wait_ge(s["att_done"], 32)
            attended(0)
            project_out(0)
            attended(1)
            with pe.Fori(1, PAIRS - 1) as i:
                project_out(i)
                turn_x1(i - 1)
                attended(i + 1)
                route(i - 1)
            project_out(PAIRS - 1)
            turn_x1(PAIRS - 2)
            route(PAIRS - 2)
            turn_x1(PAIRS - 1)
            route(PAIRS - 1)

            pe.wait_ge(s["top_conv"], 2)
            pe.wait_ge(s["lg_copied"], 2 * PAIRS + 1)
            for n, src in enumerate((top_v[0:E, :], top_f[0:E, :], rev[:, 0, :], rev[:, 1, :])):
                last = tp(ps[:, 0, n * E:(n + 1) * E], src, ident[0:E, 0:E])
            last.then_inc(s["top_turned"], 1)
            pe.wait_ge(s["top_sel"], 1)

            def turn_tokens(e, n):
                pe.wait_ge(gathered[n], 4 * (e - n) + 16)
                if not (isinstance(e, int) and e == 0):
                    pe.wait_ge(s["xg_copied"], e)
                for it in range(DT):
                    last = tp(ps[:, 0, it * P:(it + 1) * P], xg[:, n, it * P:(it + 1) * P], ident[:, :])
                last.then_inc(s["xg_turned"], 1)

            def hidden(e, n):
                pe.wait_ge(w_loaded[n], WLOADS * 4 * (e - n) + WLOADS * 16)
                pe.wait_ge(s["xg_copied"], e + 1)
                for sl in range(S):
                    for j in range(2):
                        m = 2 * sl + j
                        for it in range(DT):
                            last = mm(ps[:, 2 + 2 * (n % 2) + m // 4, (m % 4) * P:(m % 4 + 1) * P],
                                      lhsT=w1_sb[:, n, sl, it, :].rearrange("p (c j) -> p c j", j=2)[:, :, j],
                                      rhs=xgT[:, n % 2, it, :], start=it == 0, stop=it == DT - 1)
                    if sl % 2 == 1:
                        last.then_inc(s["h_ready"], 1)

            def outputs(e, n):
                wait(pe, s["yT_copied"], e)
                for h in range(2):
                    for j in range(2):
                        for side in range(2):
                            sl = 2 * h + side
                            pe.wait_ge(s["gelu_done"], 8 * e + 2 * sl + j + 1)
                            last = mm(ps[64 * side:64 * side + 64, 1, h * P:(h + 1) * P],
                                      lhsT=w2_sb[:, n, sl, j * KO:(j + 1) * KO], rhs=hid[:, n % 2, 2 * sl + j, :],
                                      start=j == 0, stop=j == 1)
                last.then_inc(s["yT_ready"], 1)

            def turn_outputs(e, n):
                wait(pe, s["y2_scaled"], e - 1)
                pe.wait_ge(s["yT_copied"], e + 1)
                for h in range(2):
                    last = tp(ps[:, 6 + n % 2, h * P:(h + 1) * P], yT[:, n % 2, h, :], ident[:, :])
                last.then_inc(s["y2_ready"], 1)

            def step(e, n, static):
                hidden(e, n)
                if not (static and e + 1 >= E):
                    turn_tokens(e + 1, (n + 1) % NBUF)
                if not (static and e < 2):
                    turn_outputs(e - 2, (n - 2) % NBUF)
                if not (static and e < 1):
                    outputs(e - 1, (n - 1) % NBUF)

            turn_tokens(0, 0)
            for n in range(NBUF):
                step(n, n, True)
            with pe.Fori(1, E // NBUF - 1) as i:
                for n in range(NBUF):
                    step(NBUF * i + n, n, False)
            for n in range(NBUF):
                step(E - NBUF + n, n, True)
            turn_outputs(E - 2, NBUF - 2)
            outputs(E - 1, NBUF - 1)
            turn_outputs(E - 1, NBUF - 1)


_INS = ["L0_attn_x", "L0_attn_WQ", "L0_attn_bQ", "L0_attn_WK", "L0_attn_bK", "L0_attn_WV", "L0_attn_bV",
        "L0_attn_WO", "L0_attn_bO", "L0_attn_rel_pos_table", "L0_ffn_Wr", "L0_ffn_W1", "L0_ffn_b1",
        "L0_ffn_W2", "L0_ffn_b2"]


def kernel(**inputs):
    import numpy as np
    import concourse.bacc as bacc
    from concourse.bass_utils import run_bass_kernel_spmd

    nc = bacc.Bacc("TRN2", target_bir_lowering=False, num_devices=1)
    arrays, args = {}, []
    for name in _INS:
        a = np.ascontiguousarray(inputs[name])
        arrays[name] = a
        args.append(nc.dram_tensor(name, a.shape, mybir.dt.from_np(a.dtype), kind="ExternalInput").ap())
    result = nc.dram_tensor("result", (B, T, D), F32, kind="ExternalOutput").ap()
    moe_layer(nc, *args, result)
    r = run_bass_kernel_spmd(nc, [arrays], core_ids=[0])
    return r.results[0]["result"]
```
